# Optimizing a Trainium2 kernel written in Bass

```python
import numpy as np
import jax
import jax.numpy as jnp

def _softmax(x, axis=-1):
    return jax.nn.softmax(x, axis=axis)

def _gelu(x):
    return jax.nn.gelu(x, approximate=True)

def _silu(x):
    return jax.nn.silu(x)

def _sigmoid(x):
    return jax.nn.sigmoid(x)

def _layernorm(x, axis=-1, eps=1e-05):
    m = jnp.mean(x, axis=axis, keepdims=True)
    v = jnp.var(x, axis=axis, keepdims=True)
    return (x - m) / jnp.sqrt(v + eps)

def _scatter_add(tgt, idx, src, axis=0):
    return tgt.at[idx].add(src)

def _segment_sum(src, seg, n):
    return jax.ops.segment_sum(src, seg, n)
kernel_name = 'mk_decoder_preln_d2_seqx_r4_ea58e7'

def setup_inputs(seed: int=0):
    np.random.seed(seed)
    _w = jnp.asarray

    def _rec_inputs():
        import jax
        import jax.numpy as jnp
        _rk = jax.random.key(seed)
        x = 7.22e-05 + 1 * jax.random.normal(jax.random.fold_in(_rk, 1), (1, 2048, 256), jnp.float32)
        _lenS = 2048 - jax.random.randint(jax.random.fold_in(_rk, 7), (1,), 0, max(1, 2048 // 4) + 1, jnp.int32)
        _lenS2 = 1601 - jax.random.randint(jax.random.fold_in(_rk, 8), (1,), 0, max(1, 1601 // 4) + 1, jnp.int32)
        _ctx_768P = jax.random.normal(jax.random.fold_in(_rk, 11), (1, 16, 192), jnp.float32)
        _ctx_768c = jax.random.dirichlet(jax.random.fold_in(_rk, 511), 0.3 * jnp.ones((16,), jnp.float32), (1, 1601))
        _ctx_768t = jnp.einsum('bsk,bkd->bsd', _ctx_768c, _ctx_768P)
        _ctx_768t = _ctx_768t * jax.lax.rsqrt(jnp.mean(jnp.square(_ctx_768t)) + 1e-12) * 0.953939
        ctx_768 = -0.000191848 + 0.999787 * (_ctx_768t + 0.3 * jax.random.normal(jax.random.fold_in(_rk, 611), (1, 1601, 192), jnp.float32))
        return (x, ctx_768)
    x, ctx_768 = _rec_inputs()

    def _L0_attn_setup():
        import math
        import jax, jax.numpy as jnp
        import numpy as np
        D_MODEL = 256
        N_HEAD = 16
        HEAD_DIM = D_MODEL // N_HEAD
        T = 1.0
        EPS = 1e-05

        def _layernorm(t, gamma, beta):
            m = t.mean(axis=-1, keepdims=True)
            var = ((t - m) ** 2).mean(axis=-1, keepdims=True)
            return (t - m) * jax.lax.rsqrt(var + EPS) * gamma + beta
        key = jax.random.key(seed)
        k1, k2, k3 = jax.random.split(key, 3)
        B, S = (4, 512)
        scale = 1.0 / math.sqrt(D_MODEL)
        return {'x': jax.random.normal(k1, (B, S, D_MODEL), dtype=jnp.float32), 'w_qkv': jax.random.normal(k2, (D_MODEL, 3 * D_MODEL), dtype=jnp.float32) * scale, 'w_proj': jax.random.normal(k3, (D_MODEL, D_MODEL), dtype=jnp.float32) * scale, 'q_gamma': jnp.ones((HEAD_DIM,), dtype=jnp.float32), 'q_beta': jnp.zeros((HEAD_DIM,), dtype=jnp.float32), 'k_gamma': jnp.ones((HEAD_DIM,), dtype=jnp.float32), 'k_beta': jnp.zeros((HEAD_DIM,), dtype=jnp.float32)}
    _L0_attn_all = _L0_attn_setup()
    _L0_attn_in = {k: v for k, v in _L0_attn_all.items() if k in ('w_qkv', 'w_proj', 'q_gamma', 'q_beta', 'k_gamma', 'k_beta')}
    del _L0_attn_all

    def _L0_xattn_setup():
        import jax, jax.numpy as jnp
        import numpy as np
        N_HEADS = 16
        key = jax.random.key(seed)
        ks = jax.random.split(key, 8)
        b, l, m = (8, 256, 256)
        d_embed, d_cross = (256, 192)
        s_q = 1.0 / np.sqrt(d_embed)
        s_kv = 1.0 / np.sqrt(d_cross)
        return {'x': jax.random.normal(ks[0], (b, l, d_embed), jnp.float32), 'y': jax.random.normal(ks[1], (b, m, d_cross), jnp.float32), 'Wq': jax.random.normal(ks[2], (d_embed, d_embed), jnp.float32) * s_q, 'bq': jax.random.normal(ks[3], (d_embed,), jnp.float32) * 0.01, 'Wkv': jax.random.normal(ks[4], (2 * d_embed, d_cross), jnp.float32) * s_kv, 'bkv': jax.random.normal(ks[5], (2 * d_embed,), jnp.float32) * 0.01, 'Wo': jax.random.normal(ks[6], (d_embed, d_embed), jnp.float32) * s_q, 'bo': jax.random.normal(ks[7], (d_embed,), jnp.float32) * 0.01}
    _L0_xattn_all = _L0_xattn_setup()
    _L0_xattn_in = {k: v for k, v in _L0_xattn_all.items() if k in ('Wq', 'bq', 'Wkv', 'bkv', 'Wo', 'bo')}
    del _L0_xattn_all

    def _L0_ffn_setup():
        import jax, jax.numpy as jnp
        import numpy as np
        D_MODEL = 256
        N_EXPERTS = 8
        TOP_K = 2
        B, S = (4, 512)
        key = jax.random.key(seed)
        k_x, k_g, k_w = jax.random.split(key, 3)
        x = jax.random.normal(k_x, (B, S, D_MODEL), dtype=jnp.float32)
        gate_w = jax.random.normal(k_g, (N_EXPERTS, D_MODEL), dtype=jnp.float32) * (1.0 / np.sqrt(D_MODEL))
        bound = float(np.sqrt(6.0 / (D_MODEL + D_MODEL)))
        weight = jax.random.uniform(k_w, (N_EXPERTS, D_MODEL, D_MODEL), dtype=jnp.float32, minval=-bound, maxval=bound)
        return {'x': x, 'gate_w': gate_w, 'weight': weight}
    _L0_ffn_all = _L0_ffn_setup()
    _L0_ffn_in = {k: v for k, v in _L0_ffn_all.items() if k in ('gate_w', 'weight')}
    del _L0_ffn_all

    def _L1_attn_setup():
        import jax, jax.numpy as jnp
        import numpy as np
        FOCUS = 3
        EPS = 1e-06

        def _norm_last(t):
            return t / jnp.sum(t, axis=-1, keepdims=True)
        key = jax.random.key(seed)
        ks = jax.random.split(key, 6)
        B, N, C = (4, 1024, 256)
        s = 0.02
        return {'x': jax.random.normal(ks[0], (B, N, C), jnp.float32), 'w_qkv': jax.random.normal(ks[1], (3 * C, C), jnp.float32) * s, 'w_proj': jax.random.normal(ks[2], (C, C), jnp.float32) * s, 'b_proj': jax.random.normal(ks[3], (C,), jnp.float32) * s, 'w_dwc': jax.random.normal(ks[4], (C, 3), jnp.float32) * s, 'b_dwc': jax.random.normal(ks[5], (C,), jnp.float32) * s}
    _L1_attn_all = _L1_attn_setup()
    _L1_attn_in = {k: v for k, v in _L1_attn_all.items() if k in ('w_qkv', 'w_proj', 'b_proj', 'w_dwc', 'b_dwc')}
    del _L1_attn_all

    def _L1_xattn_setup():
        import jax, jax.numpy as jnp
        import numpy as np
        IMG_DIM, TXT_DIM, HID = (256, 192, 256)
        B, LQ, LK = (8, 512, 512)
        key = jax.random.key(seed)
        ks = jax.random.split(key, 8)
        s_img = 1.0 / np.sqrt(IMG_DIM)
        s_txt = 1.0 / np.sqrt(TXT_DIM)
        return {'image_features': jax.random.normal(ks[0], (B, LQ, IMG_DIM), jnp.float32), 'text_features': jax.random.normal(ks[1], (B, LK, TXT_DIM), jnp.float32), 'Wq': jax.random.uniform(ks[2], (IMG_DIM, HID), jnp.float32, -s_img, s_img), 'bq': jax.random.uniform(ks[3], (HID,), jnp.float32, -s_img, s_img), 'Wk': jax.random.uniform(ks[4], (TXT_DIM, HID), jnp.float32, -s_txt, s_txt), 'bk': jax.random.uniform(ks[5], (HID,), jnp.float32, -s_txt, s_txt), 'Wv': jax.random.uniform(ks[6], (TXT_DIM, HID), jnp.float32, -s_txt, s_txt), 'bv': jax.random.uniform(ks[7], (HID,), jnp.float32, -s_txt, s_txt)}
    _L1_xattn_all = _L1_xattn_setup()
    _L1_xattn_in = {k: v for k, v in _L1_xattn_all.items() if k in ('Wq', 'bq', 'Wk', 'bk', 'Wv', 'bv')}
    del _L1_xattn_all

    def _L1_ffn_setup():
        import jax, jax.numpy as jnp
        import numpy as np
        FP8_MAX = 448.0

        def quant_fp8(x):
            amax = jnp.max(jnp.abs(x)).astype(jnp.float32)
            scale = jnp.minimum(FP8_MAX / jnp.maximum(amax, 1e-12), FP8_MAX)
            x_fp8 = jnp.clip(x * scale, -FP8_MAX, FP8_MAX).astype(jnp.float8_e4m3fn)
            return (x_fp8, 1.0 / scale)
        key = jax.random.key(seed)
        k1, k2, k3 = jax.random.split(key, 3)
        B, S, IN, OUT = (4, 2048, 256, 256)
        input = jax.random.normal(k1, (B, S, IN), dtype=jnp.float32)
        bound = 1.0 / np.sqrt(IN)
        weight = jax.random.uniform(k2, (OUT, IN), dtype=jnp.float32, minval=-bound, maxval=bound)
        bias = jax.random.uniform(k3, (OUT,), dtype=jnp.float32, minval=-bound, maxval=bound)
        return {'input': input, 'weight': weight, 'bias': bias}
    _L1_ffn_all = _L1_ffn_setup()
    _L1_ffn_in = {k: v for k, v in _L1_ffn_all.items() if k in ('weight', 'bias')}
    del _L1_ffn_all
    return {'x': x, 'ctx_768': ctx_768, 'L0_attn_w_qkv': _L0_attn_in['w_qkv'], 'L0_attn_w_proj': _L0_attn_in['w_proj'], 'L0_attn_q_gamma': _L0_attn_in['q_gamma'], 'L0_attn_q_beta': _L0_attn_in['q_beta'], 'L0_attn_k_gamma': _L0_attn_in['k_gamma'], 'L0_attn_k_beta': _L0_attn_in['k_beta'], 'L0_xattn_Wq': _L0_xattn_in['Wq'], 'L0_xattn_bq': _L0_xattn_in['bq'], 'L0_xattn_Wkv': _L0_xattn_in['Wkv'], 'L0_xattn_bkv': _L0_xattn_in['bkv'], 'L0_xattn_Wo': _L0_xattn_in['Wo'], 'L0_xattn_bo': _L0_xattn_in['bo'], 'L0_ffn_gate_w': _L0_ffn_in['gate_w'], 'L0_ffn_weight': _L0_ffn_in['weight'], 'L1_attn_w_qkv': _L1_attn_in['w_qkv'], 'L1_attn_w_proj': _L1_attn_in['w_proj'], 'L1_attn_b_proj': _L1_attn_in['b_proj'], 'L1_attn_w_dwc': _L1_attn_in['w_dwc'], 'L1_attn_b_dwc': _L1_attn_in['b_dwc'], 'L1_xattn_Wq': _L1_xattn_in['Wq'], 'L1_xattn_bq': _L1_xattn_in['bq'], 'L1_xattn_Wk': _L1_xattn_in['Wk'], 'L1_xattn_bk': _L1_xattn_in['bk'], 'L1_xattn_Wv': _L1_xattn_in['Wv'], 'L1_xattn_bv': _L1_xattn_in['bv'], 'L1_ffn_weight': _L1_ffn_in['weight'], 'L1_ffn_bias': _L1_ffn_in['bias']}

def reference(x, ctx_768, L0_attn_w_qkv, L0_attn_w_proj, L0_attn_q_gamma, L0_attn_q_beta, L0_attn_k_gamma, L0_attn_k_beta, L0_xattn_Wq, L0_xattn_bq, L0_xattn_Wkv, L0_xattn_bkv, L0_xattn_Wo, L0_xattn_bo, L0_ffn_gate_w, L0_ffn_weight, L1_attn_w_qkv, L1_attn_w_proj, L1_attn_b_proj, L1_attn_w_dwc, L1_attn_b_dwc, L1_xattn_Wq, L1_xattn_bq, L1_xattn_Wk, L1_xattn_bk, L1_xattn_Wv, L1_xattn_bv, L1_ffn_weight, L1_ffn_bias):
    import jax
    import jax.numpy as jnp

    def _L0_attn_ref(x, w_qkv, w_proj, q_gamma, q_beta, k_gamma, k_beta):
        import math
        import jax, jax.numpy as jnp
        import numpy as np
        D_MODEL = 256
        N_HEAD = 16
        HEAD_DIM = D_MODEL // N_HEAD
        T = 1.0
        EPS = 1e-05

        def _layernorm(t, gamma, beta):
            m = t.mean(axis=-1, keepdims=True)
            var = ((t - m) ** 2).mean(axis=-1, keepdims=True)
            return (t - m) * jax.lax.rsqrt(var + EPS) * gamma + beta
        B, S, C = x.shape
        H, Dh = (N_HEAD, HEAD_DIM)
        qkv = (x @ w_qkv).reshape(B, S, 3, H, Dh)
        qkv = jnp.transpose(qkv, (2, 0, 3, 1, 4))
        q, k, v = (qkv[0], qkv[1], qkv[2])
        q = _layernorm(q, q_gamma, q_beta)
        k = _layernorm(k, k_gamma, k_beta)
        logits = jnp.einsum('bhsd,bhtd->bhst', q, k) / (math.sqrt(Dh) * T)
        att = jax.nn.softmax(logits, axis=-1)
        out = jnp.einsum('bhst,bhtd->bhsd', att, v)
        out = jnp.transpose(out, (0, 2, 1, 3)).reshape(B, S, C)
        return out @ w_proj

    def _L0_xattn_ref(x, y, Wq, bq, Wkv, bkv, Wo, bo):
        import jax, jax.numpy as jnp
        import numpy as np
        N_HEADS = 16
        b, l, d = x.shape
        m = y.shape[1]
        h = N_HEADS
        dh = d // h
        q = (jnp.einsum('bld,ed->ble', x, Wq) + bq).reshape(b, l, h, dh)
        kv = (jnp.einsum('bmc,ec->bme', y, Wkv) + bkv).reshape(b, m, h, 2 * dh)
        k, v = (kv[..., :dh], kv[..., dh:])
        scale = 1.0 / jnp.sqrt(jnp.asarray(dh, x.dtype))
        att = jax.nn.softmax(jnp.einsum('blhd,bmhd->blmh', q, k) * scale, axis=2)
        out = jnp.einsum('blmh,bmhd->blhd', att, v).reshape(b, l, d)
        return jnp.einsum('bld,ed->ble', out, Wo) + bo

    def _L0_ffn_ref(x, gate_w, weight):
        import jax, jax.numpy as jnp
        import numpy as np
        D_MODEL = 256
        N_EXPERTS = 8
        TOP_K = 2
        B, S = (4, 512)
        logits = jnp.einsum('bsd,ed->bse', x, gate_w)
        topk_vals, topk_idx = jax.lax.top_k(logits, TOP_K)
        topk_weights = jax.nn.softmax(topk_vals, axis=-1)
        one_hot = jax.nn.one_hot(topk_idx, N_EXPERTS, dtype=x.dtype)
        weights_full = jnp.einsum('bsk,bske->bse', topk_weights, one_hot)
        expert_out = jnp.einsum('bsd,edh->bseh', x, weight)
        out = jnp.einsum('bse,bseh->bsh', weights_full, expert_out)
        return out

    def _L1_attn_ref(x, w_qkv, w_proj, b_proj, w_dwc, b_dwc):
        import jax, jax.numpy as jnp
        import numpy as np
        FOCUS = 3
        EPS = 1e-06

        def _norm_last(t):
            return t / jnp.sum(t, axis=-1, keepdims=True)
        B, N, C = x.shape
        H = 16
        d = C // H
        qkv = jnp.einsum('bnc,oc->bno', x, w_qkv).reshape(B, N, 3, H, d)
        qkv = jnp.transpose(qkv, (2, 0, 3, 1, 4))
        q, k, v = (qkv[0], qkv[1], qkv[2])
        q = _norm_last(jax.nn.relu(q) + EPS)
        k = _norm_last(jax.nn.relu(k) + EPS)
        q = _norm_last(q ** FOCUS)
        k = _norm_last(k ** FOCUS)
        kv = jnp.einsum('bhnd,bhne->bhde', k, v)
        z = 1.0 / (jnp.einsum('bhnd,bhd->bhn', q, k.sum(axis=2)) + EPS)
        out = jnp.einsum('bhnd,bhde,bhn->bhne', q, kv, z)
        out = jnp.transpose(out, (0, 2, 1, 3)).reshape(B, N, C)
        xp = jnp.pad(out, ((0, 0), (1, 1), (0, 0)))
        conv = xp[:, 0:N, :] * w_dwc[:, 0] + xp[:, 1:N + 1, :] * w_dwc[:, 1] + xp[:, 2:N + 2, :] * w_dwc[:, 2] + b_dwc
        out = out + conv
        return jnp.einsum('bnc,oc->bno', out, w_proj) + b_proj

    def _L1_xattn_ref(image_features, text_features, Wq, bq, Wk, bk, Wv, bv):
        import jax, jax.numpy as jnp
        import numpy as np
        IMG_DIM, TXT_DIM, HID = (256, 192, 256)
        B, LQ, LK = (8, 512, 512)
        query = jnp.einsum('bqi,ih->bqh', image_features, Wq) + bq
        key = jnp.einsum('bkt,th->bkh', text_features, Wk) + bk
        value = jnp.einsum('bkt,th->bkh', text_features, Wv) + bv
        scale = 1.0 / jnp.sqrt(jnp.asarray(HID, query.dtype))
        scores = jnp.einsum('bqh,bkh->bqk', query, key) * scale
        weights = jax.nn.softmax(scores, axis=-1)
        attended = jnp.einsum('bqk,bkh->bqh', weights, value)
        return attended

    def _L1_ffn_ref(input, weight, bias):
        import jax, jax.numpy as jnp
        import numpy as np
        FP8_MAX = 448.0

        def quant_fp8(x):
            amax = jnp.max(jnp.abs(x)).astype(jnp.float32)
            scale = jnp.minimum(FP8_MAX / jnp.maximum(amax, 1e-12), FP8_MAX)
            x_fp8 = jnp.clip(x * scale, -FP8_MAX, FP8_MAX).astype(jnp.float8_e4m3fn)
            return (x_fp8, 1.0 / scale)
        prev_shape = input.shape
        x2d = input.reshape(-1, weight.shape[1])
        w_fp8, w_scale = quant_fp8(weight)
        x_fp8, x_scale = quant_fp8(x2d)
        acc = jnp.matmul(x_fp8.astype(jnp.float32), w_fp8.astype(jnp.float32).T)
        out2d = (acc * (x_scale * w_scale) + bias).astype(jnp.bfloat16)
        out = out2d.reshape(*prev_shape[:-1], weight.shape[0]).astype(input.dtype)
        return out
    x = x + _L0_attn_ref(_layernorm(x, axis=-1), L0_attn_w_qkv, L0_attn_w_proj, L0_attn_q_gamma, L0_attn_q_beta, L0_attn_k_gamma, L0_attn_k_beta)
    x = x + _L0_xattn_ref(_layernorm(x, axis=-1), ctx_768, L0_xattn_Wq, L0_xattn_bq, L0_xattn_Wkv, L0_xattn_bkv, L0_xattn_Wo, L0_xattn_bo)
    x = x + _L0_ffn_ref(_layernorm(x, axis=-1), L0_ffn_gate_w, L0_ffn_weight)
    x = x + _L1_attn_ref(_layernorm(x, axis=-1), L1_attn_w_qkv, L1_attn_w_proj, L1_attn_b_proj, L1_attn_w_dwc, L1_attn_b_dwc)
    x = x + _L1_xattn_ref(_layernorm(x, axis=-1), ctx_768, L1_xattn_Wq, L1_xattn_bq, L1_xattn_Wk, L1_xattn_bk, L1_xattn_Wv, L1_xattn_bv)
    x = x + _L1_ffn_ref(_layernorm(x, axis=-1), L1_ffn_weight, L1_ffn_bias)
    return x

_drawn_inputs = setup_inputs


def setup_inputs(seed=0):
    import zlib

    import numpy as np

    out = dict(_drawn_inputs(seed))
    spreads = {'L0_attn_q_gamma': (1.0, 0.2),
     'L0_attn_q_beta': (0.0, 0.1),
     'L0_attn_k_gamma': (1.0, 0.2),
     'L0_attn_k_beta': (0.0, 2.0)}
    factors = {'L0_xattn_bq': 3.826,
     'L1_attn_b_proj': 3.795,
     'L1_attn_w_dwc': 45.256,
     'L1_attn_b_dwc': 7.798,
     'L1_xattn_bq': 34.612,
     'L1_xattn_bk': 64.0}
    for name, (base, spread) in spreads.items():
        noise = np.random.default_rng([zlib.crc32(name.encode()), seed]).standard_normal(out[name].shape)
        drawn = base * np.exp(spread * noise) if base else spread * noise
        out[name] = jnp.asarray(drawn.astype(out[name].dtype))
    for name, factor in factors.items():
        out[name] = (out[name] * factor).astype(out[name].dtype)
    return out
```

```python
from contextlib import ExitStack

import concourse.bass as bass
from concourse import mybir

F32 = mybir.dt.float32
BF16 = mybir.dt.bfloat16
I32 = mybir.dt.int32
U32 = mybir.dt.uint32
ACT = mybir.ActivationFunctionType
ALU = mybir.AluOpType
AX = mybir.AxisListType

P = 128
D = 256
H = 16
HD = D // H
S = 2048
T = S // P
C = 192
CH = C // 2
M = 1601
TM = -(-M // P)
MP = TM * P
NE = 8
HG = 4
QC = 4
GW = HG * HD
NPART = 6
MAXROW = 96
EPS_LN = 1e-5
EPS_FOCUS = 1e-6
FP8_MAX = 448.0


class Counted:

    def __init__(self, eng, sem, base=0, fixed=None):
        self.eng, self.sem, self.base, self.n, self.fixed = eng, sem, base, 0, fixed

    def __call__(self, ins):
        self.n += 1
        ins.then_inc(self.sem, 1)
        return ins

    def wait(self):
        self.eng.wait_ge(self.sem, self.base + self.n)
        if self.fixed is not None:
            self.eng.sem_inc(self.fixed, 1)


def at(t, width=1):
    return bass.ds(t, width)


def fresh(prog, name):
    prog["n"] = prog.get("n", 0) + 1
    return prog["ctx"].enter_context(prog["nc"].semaphore(f"{name}_{prog['n']}"))


class Slots:

    def __init__(self, prog, name, ahead=2):
        self.sem, self.ahead = fresh(prog, name), ahead

    def open(self, eng):
        eng.sem_inc(self.sem, self.ahead)

    def wait(self, eng, value):
        eng.wait_ge(self.sem, value + self.ahead)



def ln_finish(prog, st, mean, rstd, tmp):
    nc = prog["nc"]
    s_v, s_q = fresh(prog, "lnf_v"), fresh(prog, "lnf_sqrt")
    with nc.Block() as block:
        @block.vector
        def _(v):
            c = Counted(v, s_v)
            c(v.tensor_tensor(mean[:, :], st[:, :, 1], st[:, :, 4], ALU.add))
            c(v.tensor_tensor(tmp[:, 0, :], st[:, :, 1], st[:, :, 4], ALU.subtract))
            c(v.tensor_tensor(tmp[:, 1, :], st[:, :, 2], st[:, :, 5], ALU.add))
            c.wait()
            c(v.tensor_scalar(mean[:, :], mean[:, :], 0.5, None, ALU.mult))
            c(v.tensor_tensor(tmp[:, 0, :], tmp[:, 0, :], tmp[:, 0, :], ALU.mult))
            c(v.tensor_scalar(tmp[:, 1, :], tmp[:, 1, :], 1.0 / D, EPS_LN, ALU.mult, ALU.add))
            c.wait()
            c(v.scalar_tensor_tensor(tmp[:, 1, :], tmp[:, 0, :], 0.25, tmp[:, 1, :], ALU.mult, ALU.add))
            v.wait_ge(s_q, 1)
            c(v.reciprocal(rstd[:, :], tmp[:, 0, :]))
            c.wait()

        @block.scalar
        def _(a):
            a.wait_ge(s_v, 7)
            a.activation(tmp[:, 0, :], tmp[:, 1, :], ACT.Sqrt).then_inc(s_q, 1)
            a.wait_ge(s_q, 1)



def linear(prog, tiles, fetch, w, n_cols, epilogue, per, ident=None, rows=P, direct=None):
    nc = prog["nc"]
    s_fetch, s_turned, s_copied = fresh(prog, "fetch"), fresh(prog, "turned"), Slots(prog, "copied")
    s_prod, s_chain = Slots(prog, "prod"), Slots(prog, "epilogue", per + 1)
    banks = -(-n_cols // 512)
    pairs = (tiles - 1) // 2
    with ExitStack() as cx:
        xn = [cx.enter_context(nc.sbuf_tensor(f"xn{prog['n']}_{p}", [P, D], F32)) for p in range(2)]
        xt = [cx.enter_context(nc.sbuf_tensor(f"xt{prog['n']}_{p}", [P, 2, P], F32)) for p in range(2)]
        turn = [cx.enter_context(nc.psum_tensor(f"turn{prog['n']}_{p}", [P, 2, 256], F32)) for p in range(2)]
        prod = [cx.enter_context(nc.psum_tensor(f"prod{prog['n']}_{p}", [P, banks, 512], F32)) for p in range(2)]

        def every(body, eng):
            if pairs:
                with eng.Fori(0, pairs) as i:
                    for p in range(2):
                        body(2 * i + p, p, False)
            for n in range(2 * pairs, tiles):
                body(n, n % 2, n == tiles - 1)

        block = cx.enter_context(nc.Block())

        @block.tensor
        def _(pe):
            def turn_tile(n, p):
                pe.wait_ge(s_fetch, n + 1)
                s_copied.wait(pe, n - 1)
                for k in range(2):
                    m = pe.transpose(turn[p][:, 0, k * P:(k + 1) * P], xn[p][:, k * P:(k + 1) * P], ident[:, :])
                m.then_inc(s_turned, 1)

            def multiply(n, p, last):
                if direct is None and not last:
                    turn_tile(n + 1, 1 - p)
                s_copied.wait(pe, n + 1)
                s_chain.wait(pe, (n - 1) * per)
                for b in range(banks):
                    lo, hi = b * 512, min(n_cols, b * 512 + 512)
                    for k in range(2):
                        m = pe.matmul(prod[p][:, b, 0:hi - lo], xt[p][0:rows, k, :], w[0:rows, k, lo:hi],
                                      start=(k == 0), stop=(k == 1))
                m.then_inc(s_prod.sem, 1)

            s_prod.open(pe)
            if direct is None:
                turn_tile(0, 0)
            every(multiply, pe)

        @block.scalar
        def _(a):
            def copy(n, p, last):
                s_prod.wait(a, n - 1)
                if direct is None:
                    a.wait_ge(s_turned, n + 1)
                    a.copy(xt[p][:, :, :], turn[p][:, 0, :].rearrange("p (k n) -> p k n", k=2)).then_inc(s_copied.sem, 1)
                else:
                    a.copy(xt[p][0:rows, :, :], direct(n)).then_inc(s_copied.sem, 1)
            s_copied.open(a)
            every(copy, a)

        @block.vector
        def _(v):
            s_chain.open(v)
            if direct is None:
                for n in range(2):
                    fetch(v, xn[n], n).then_inc(s_fetch, 1)

            def finish(n, p, last):
                s_prod.wait(v, n + 1)
                c = Counted(v, s_chain.sem, n * per + s_chain.ahead)
                epilogue(v, prod[p], n, p, c)
                assert c.n == per, c.n
                c.wait()
                if direct is None and not (last or (type(n) is int and n + 2 >= tiles)):
                    v.wait_ge(s_turned, n + 1)
                    fetch(v, xn[p], n + 2).then_inc(s_fetch, 1)
            if pairs:
                with v.Fori(0, pairs) as i:
                    for p in range(2):
                        finish(2 * i + p, p, False)
            for n in range(2 * pairs, tiles):
                finish(n, n % 2, n == tiles - 1)


def ln_rows(x, mean, rstd):
    return lambda v, out, n: v.tensor_scalar(out[:, :], x[:, n, :], mean[:, at(n)], rstd[:, at(n)],
                                             ALU.subtract, ALU.mult)


def plain_rows(src):
    return lambda v, out, n: v.tensor_copy(out[:, :], src[:, n, :])


def residual(x, st, bias=None):
    def run(v, prod, n, p, c):
        c(v.tensor_tensor(x[:, n, :], prod[:, 0, 0:D], x[:, n, :], ALU.add))
        c.wait()
        if bias is not None:
            c(v.tensor_tensor(x[:, n, :], x[:, n, :], bias[:, :], ALU.add))
            c.wait()
        c(v.bn_stats(st[:, n, :], x[:, n, :]))
    return run



def load(prog, pairs):
    nc = prog["nc"]
    s = fresh(prog, "load")
    with nc.Block() as block:
        @block.sync
        def _(e):
            for dst, src in pairs:
                e.dma_start(dst, src).then_inc(s, 16)
            e.wait_ge(s, 16 * len(pairs))


def rows2(w):
    return w.rearrange("(k p) n -> p k n", k=2)



def split3(eng, c, src, tmp, hi, mid, lo):
    for d in hi:
        c(eng.tensor_copy(d, src))
    c.wait()
    c(eng.tensor_tensor(tmp, src, hi[0], ALU.subtract))
    c.wait()
    for d in mid:
        c(eng.tensor_copy(d, tmp))
    c.wait()
    c(eng.tensor_tensor(lo[0], tmp, mid[0], ALU.subtract))


def parts(stack, which):
    order = "hhmmlh" if which == "q" else "hmhmhl"
    out = {"h": [], "m": [], "l": []}
    for slot, part in enumerate(order):
        out[part].append(stack[..., slot * HD:(slot + 1) * HD])
    return out["h"], out["m"], out["l"]


def build_kt(prog, kn, tiles, kt, identb):
    nc = prog["nc"]
    s_set, s_split = fresh(prog, "ks_set"), fresh(prog, "ks_split")
    s_turn, s_out, s_out2 = (Slots(prog, n) for n in ("ks_turn", "ks_dve", "ks_act"))
    per = 7
    with ExitStack() as cx:
        nat = cx.enter_context(nc.sbuf_tensor(f"knat{prog['n']}", [P, 2, H, P], BF16))
        tmp = cx.enter_context(nc.sbuf_tensor(f"ktmp{prog['n']}", [P, H, HD], F32))
        ps = cx.enter_context(nc.psum_tensor(f"kps{prog['n']}", [P, 4, 8, P], BF16))
        block = cx.enter_context(nc.Block())

        def every(body, eng):
            with eng.Fori(0, tiles // 2) as i:
                for p in range(2):
                    body(2 * i + p, p)
            if tiles % 2:
                body(tiles - 1, 0)

        @block.gpsimd
        def _(g):
            g.memset(nat[:, :, :, :], 0.0).then_inc(s_set, 1)
            g.wait_ge(s_set, 1)
            g.memset(nat[:, :, :, MAXROW:MAXROW + 3], 1.0).then_inc(s_set, 1)
            g.wait_ge(s_set, 2)

            def body(n, p):
                s_turn.wait(g, n - 1)
                g.sem_inc(s_set, 1)
                c = Counted(g, s_split, n * per, s_set)
                src = kn[:, n, :].rearrange("p (h d) -> p h d", d=HD)
                hi, mid, lo = parts(nat[:, p, :, :], "k")
                split3(g, c, src, tmp[:, :, :], hi, mid, lo)
                assert c.n == per, c.n
                c.wait()
            every(body, g)

        @block.tensor
        def _(pe):
            def body(n, p):
                pe.wait_ge(s_split, n * per + per)
                s_out.wait(pe, n - 1)
                s_out2.wait(pe, n - 1)
                for h in range(H):
                    m = pe.transpose(ps[:, 2 * p + h // 8, h % 8, :], nat[:, p, h, :], identb[:, :])
                m.then_inc(s_turn.sem, 1)
            s_turn.open(pe)
            every(body, pe)

        @block.vector
        def _(v):
            def body(n, p):
                s_turn.wait(v, n + 1)
                v.tensor_copy(kt[:, 0:8, at(n * P, P)], ps[:, 2 * p, :, :]).then_inc(s_out.sem, 1)
            s_out.open(v)
            every(body, v)

        @block.scalar
        def _(a):
            def body(n, p):
                s_turn.wait(a, n + 1)
                a.copy(kt[:, 8:16, at(n * P, P)], ps[:, 2 * p + 1, :, :]).then_inc(s_out2.sem, 1)
            s_out2.open(a)
            every(body, a)


def attention(prog, qn, v_nat, key_tiles, kt, valid, ident, identb):
    nc = prog["nc"]
    NU = QC * HG
    widths = [min(512, key_tiles * P - b) for b in range(0, key_tiles * P, 512)]
    KB = len(widths)
    UN = NU * KB
    NCH = T // QC * H // HG
    s = {k: fresh(prog, k) for k in ("set", "qsplit", "ta", "taev", "mx", "msplit", "tb", "tbev",
                                     "sc", "rc")}
    s["tb0"] = fresh(prog, "tb0")
    for k in ("mred", "exp", "norm", "av", "avev", "te"):
        s[k] = Slots(prog, k, 2)
    QS, MS = 9, 7
    with ExitStack() as cx:
        def sb(name, shape, dt):
            return cx.enter_context(nc.sbuf_tensor(f"{name}_{prog['n']}", shape, dt))
        qnat = sb("qnat", [P, QC, HG, P], BF16)
        qtmp = sb("qtmp", [P, QC, HG, HD], F32)
        qt = [sb(f"qt{p}", [P, HG, QC, P], BF16) for p in range(2)]
        vst = [sb(f"vst{p}", [P, key_tiles, HG, 32], F32) for p in range(2)]
        pbuf = [sb(f"pb{p}", [P, HG, 512], F32) for p in range(2)]
        mxp = sb("mxp", [P, NU, KB], F32)
        negm = sb("negm", [P, NU], F32)
        mtmp = sb("mtmp", [P, NU], F32)
        avs = sb("avs", [P, QC, P], F32)
        rc = sb("rc", [P, QC, HG], F32)
        ps_s = cx.enter_context(nc.psum_tensor(f"ps_s{prog['n']}", [P, 4, 512], F32))
        ps_m = cx.enter_context(nc.psum_tensor(f"ps_m{prog['n']}", [P, 2, 512], F32))
        ps_av = cx.enter_context(nc.psum_tensor(f"ps_av{prog['n']}", [P, 512], F32))
        ps_t = cx.enter_context(nc.psum_tensor(f"ps_t{prog['n']}", [P, QC, P], F32))
        ps_tb = ps_t[:, :, :].rearrange("p a b -> p (a b)").bitcast(BF16).rearrange("p (a b) -> p a b", b=P)
        block = cx.enter_context(nc.Block())

        def group(n):
            return n // (T // QC)

        def chunk(n):
            return n % (T // QC)

        def pairs(eng, body):
            with eng.Fori(0, NCH // 2 - 1) as j:
                for p in range(2):
                    body(2 * j + p, p, True)
            body(NCH - 2, 0, True)
            body(NCH - 1, 1, False)

        @block.gpsimd
        def _(g):
            g.memset(qnat[:, :, :, :], 0.0).then_inc(s["set"], 1)
            for p in range(2):
                g.memset(vst[p][:, :, :, :], 0.0).then_inc(s["set"], 1)
            g.wait_ge(s["set"], 3)
            for p in range(2):
                for h in range(HG):
                    g.tensor_copy(vst[p][:, :, h, HD], valid[:, 0:key_tiles]).then_inc(s["set"], 1)
            g.wait_ge(s["set"], 3 + 2 * HG)

            def prepare(n, p):
                if not (type(n) is int and n == 0):
                    g.wait_ge(s["tb"], n)
                g.sem_inc(s["set"], 1)
                c = Counted(g, s["qsplit"], n * QS, s["set"])
                src = qn[:, at(chunk(n) * QC, QC), at(group(n) * GW, GW)].rearrange("p t (h d) -> p t h d", d=HD)
                c(g.tensor_copy(qtmp[:, :, :, :], src))
                c.wait()
                hi, mid, lo = parts(qnat[:, :, :, :], "q")
                for d in hi:
                    c(g.tensor_copy(d, qtmp[:, :, :, :]))
                c.wait()
                c(g.tensor_tensor(qtmp[:, :, :, :], qtmp[:, :, :, :], hi[0], ALU.subtract))
                c.wait()
                for d in mid:
                    c(g.tensor_copy(d, qtmp[:, :, :, :]))
                c.wait()
                c(g.tensor_tensor(lo[0], qtmp[:, :, :, :], mid[0], ALU.subtract))
                c(g.tensor_copy(vst[p][:, :, :, 0:HD],
                                v_nat[:, 0:key_tiles, at(group(n) * GW, GW)].rearrange("p t (h d) -> p t h d", d=HD)))
                assert c.n == QS, c.n
                c.wait()

            prepare(0, 0)

            def body(n, p, more):
                if more:
                    if not (type(n) is int and n == 0):
                        s["av"].wait(g, n * key_tiles)
                    prepare(n + 1, 1 - p)
            pairs(g, body)

        @block.tensor
        def _(pe):
            def turn_q(n, p, half):
                if half == 0:
                    pe.wait_ge(s["qsplit"], n * QS + QS)
                    s["norm"].wait(pe, n - 1)
                    if not (type(n) is int and n == 0):
                        pe.wait_ge(s["tbev"], 2 * n)
                else:
                    pe.wait_ge(s["taev"], 2 * n + 1)
                for u in range(8):
                    a, h = 2 * half + u // HG, u % HG
                    m = pe.transpose(ps_tb[0:MAXROW, u, :], qnat[:, a, h, 0:MAXROW], identb[:, :])
                m.then_inc(s["ta"], 1)

            def turn_m(n, p, half):
                if half == 0:
                    pe.wait_ge(s["msplit"], n * MS + MS)
                    pe.wait_ge(s["taev"], 2 * n + 2)
                    if not (type(n) is int and n == 0):
                        s["norm"].wait(pe, n - 1)
                else:
                    pe.wait_ge(s["tbev"], 2 * n + 1)
                for u in range(8):
                    a, h = 2 * half + u // HG, u % HG
                    m = pe.transpose(ps_tb[MAXROW:P, u, :], qnat[:, a, h, MAXROW:P], identb[:, :])
                m.then_inc(s["tb"] if half else s["tb0"], 1)

            def max_unit(n, p, u):
                a, h, b = u // (HG * KB), u // KB % HG, u % KB
                s["mred"].wait(pe, n * UN + u - 1)
                pe.matmul(ps_m[:, u % 2, 0:widths[b]], qt[p][0:MAXROW, h, a, :],
                          kt[0:MAXROW, group(n) * HG + h, b * 512:b * 512 + widths[b]],
                          start=True, stop=True).then_inc(s["mx"], 1)

            def scores(n, p, t, half):
                e = 2 * (n * key_tiles + t) + half
                s["exp"].wait(pe, e - 1)
                for h in (2 * half, 2 * half + 1):
                    m = pe.matmul(ps_s[:, h, :], kt[:, group(n) * HG + h, t * P:(t + 1) * P],
                                  qt[p][:, h, :, :], start=True, stop=True)
                m.then_inc(s["sc"], 1)

            def values(n, p, t):
                s["exp"].wait(pe, 2 * (n * key_tiles + t) + 2)
                if t == 0:
                    s["avev"].wait(pe, n)
                for h in range(HG):
                    m = pe.matmul(ps_av[32 * h:32 * h + 32, :], vst[p][:, t, h, :], pbuf[t % 2][:, h, :],
                                  start=(t == 0), stop=(t == key_tiles - 1))
                m.then_inc(s["av"].sem, 1)

            def max_pass(n, p, lo, hi):
                if lo == 0:
                    pe.wait_ge(s["taev"], 2 * n + 2)
                for u in range(lo, hi):
                    max_unit(n, p, u)

            s["av"].open(pe)
            s["te"].open(pe)
            turn_q(0, 0, 0)
            turn_q(0, 0, 1)
            max_pass(0, 0, 0, UN)
            turn_m(0, 0, 0)
            turn_m(0, 0, 1)

            def body(n, p, more):
                if more:
                    turn_q(n + 1, 1 - p, 0)
                pe.wait_ge(s["tbev"], 2 * n + 2)
                scores(n, p, 0, 0)
                scores(n, p, 0, 1)
                if more:
                    turn_q(n + 1, 1 - p, 1)
                done = 0
                for t in range(key_tiles):
                    if t + 1 < key_tiles:
                        scores(n, p, t + 1, 0)
                    mid = UN * (2 * t + 1) // (2 * key_tiles)
                    end = UN * (t + 1) // key_tiles
                    if more:
                        max_pass(n + 1, 1 - p, done, mid)
                    if t + 1 < key_tiles:
                        scores(n, p, t + 1, 1)
                    values(n, p, t)
                    if more:
                        max_pass(n + 1, 1 - p, mid, end)
                    done = end
                if more:
                    turn_m(n + 1, 1 - p, 0)
                    turn_m(n + 1, 1 - p, 1)
                    pe.wait_ge(s["tbev"], 2 * n + 4)
                s["norm"].wait(pe, n)
                s["avev"].wait(pe, n + 1)
                for a in range(QC):
                    m = pe.transpose(ps_t[:, a, :], avs[:, a, :], ident[:, :])
                m.then_inc(s["te"].sem, 1)
            pairs(pe, body)

        @block.scalar
        def _(a):
            def ev_q(n, p, half):
                a.wait_ge(s["ta"], 2 * n + half + 1)
                if half == 0 and not (type(n) is int and n < 2):
                    a.wait_ge(s["sc"], 2 * key_tiles * (n - 1))
                a.copy(qt[p][0:MAXROW, :, 2 * half:2 * half + 2, :],
                       ps_tb[0:MAXROW, :, :].rearrange("p (a h) b -> p h a b", h=HG)).then_inc(s["taev"], 1)

            def body(n, p, more):
                for t in range(key_tiles):
                    for half in range(2):
                        e = 2 * (n * key_tiles + t) + half
                        a.wait_ge(s["sc"], e + 1)
                        s["av"].wait(a, n * key_tiles + t - 1)
                        a.activation(pbuf[t % 2][:, 2 * half:2 * half + 2, :], ps_s[:, 2 * half:2 * half + 2, :],
                                     ACT.Exp).then_inc(s["exp"].sem, 1)
                        if t == 0 and more:
                            ev_q(n + 1, 1 - p, half)
                s["av"].wait(a, (n + 1) * key_tiles)
                s["te"].wait(a, n)
                a.copy(avs[:, :, :], ps_av[:, :].rearrange("p (a b) -> p a b", b=P)).then_inc(s["avev"].sem, 1)

            s["exp"].open(a)
            s["avev"].open(a)
            ev_q(0, 0, 0)
            ev_q(0, 0, 1)
            pairs(a, body)

        @block.vector
        def _(v):
            def reduce_units(n, lo, hi):
                for u in range(lo, hi):
                    v.wait_ge(s["mx"], n * UN + u + 1)
                    v.tensor_reduce(mxp[:, u // KB, u % KB:u % KB + 1], ps_m[:, u % 2, 0:widths[u % KB]],
                                    AX.X, ALU.max).then_inc(s["mred"].sem, 1)

            def maxima(n, p):
                s["mred"].wait(v, n * UN + UN)
                c = Counted(v, s["msplit"], n * MS)
                place = [qnat[:, :, :, MAXROW + i] for i in range(3)]
                neg = negm[:, :].rearrange("p (a h) -> p a h", h=HG)
                tmp = mtmp[:, :].rearrange("p (a h) -> p a h", h=HG)
                c(v.tensor_reduce(negm[:, :], mxp[:, :, :], AX.X, ALU.max, negate=True))
                c.wait()
                v.wait_ge(s["qsplit"], n * QS + QS)
                c(v.tensor_copy(place[0], neg))
                c.wait()
                c(v.tensor_tensor(tmp, neg, place[0], ALU.subtract))
                c.wait()
                c(v.tensor_copy(place[1], tmp))
                c.wait()
                c(v.tensor_tensor(neg, tmp, place[1], ALU.subtract))
                c.wait()
                c(v.tensor_copy(place[2], neg))
                c.wait()
                c(v.tensor_copy(mtmp[:, 0:1], negm[:, 0:1]))
                assert c.n == MS, c.n
                c.wait()
                for half in range(2):
                    v.wait_ge(s["tb0"] if half == 0 else s["tb"], n + 1)
                    v.tensor_copy(qt[p][MAXROW:P, :, 2 * half:2 * half + 2, :],
                                  ps_tb[MAXROW:P, :, :].rearrange("p (a h) b -> p h a b", h=HG)).then_inc(s["tbev"], 1)

            def body(n, p, more):
                if more:
                    reduce_units(n + 1, 0, UN)
                    maxima(n + 1, 1 - p)
                s["te"].wait(v, n + 1)
                res = ps_t[:, :, :].rearrange("p a (h d) -> p a h d", d=32)
                v.reciprocal(rc[:, :, :], res[:, :, :, HD]).then_inc(s["rc"], 1)
                v.wait_ge(s["rc"], n + 1)
                v.tensor_tensor(qn[:, at(chunk(n) * QC, QC), at(group(n) * GW, GW)].rearrange("p t (h d) -> p t h d", d=HD),
                                res[:, :, :, 0:HD], rc[:, :, :].unsqueeze(3).to_broadcast([P, QC, HG, HD]),
                                ALU.mult).then_inc(s["norm"].sem, 1)
                s["norm"].wait(v, n + 1)
            s["mred"].open(v)
            s["norm"].open(v)
            reduce_units(0, 0, UN)
            maxima(0, 0)
            pairs(v, body)



def self_qkv(prog, x, mean, rstd, w, gain, shift, qn, kn, v_nat, ident):
    nc = prog["nc"]
    with ExitStack() as cx:
        sums = cx.enter_context(nc.sbuf_tensor("hsum", [P, 2 * H], F32))
        squares = cx.enter_context(nc.sbuf_tensor("hsq", [P, 2 * H, HD], F32))
        var = cx.enter_context(nc.sbuf_tensor("hvar", [P, T, 2 * H], F32))
        sd = cx.enter_context(nc.sbuf_tensor("hsd", [P, T, 2 * H], F32))

        def epilogue(v, prod, n, p, c):
            qk = prod[:, 0, :].rearrange("p (h d) -> p h d", d=HD)
            c(v.tensor_copy(v_nat[:, n, :], prod[:, 1, 0:D]))
            c(v.tensor_reduce(sums[:, :], qk, AX.X, ALU.add))
            c.wait()
            c(v.tensor_scalar(sums[:, :], sums[:, :], 1.0 / HD, None, ALU.mult))
            c.wait()
            for i, dst in enumerate((qn, kn)):
                c(v.tensor_tensor(dst[:, n, :].rearrange("p (h d) -> p h d", d=HD), qk[:, i * H:i * H + H, :],
                                  sums[:, i * H:i * H + H].unsqueeze(2).to_broadcast([P, H, HD]), ALU.subtract))
            c.wait()
            for i, dst in enumerate((qn, kn)):
                cen = dst[:, n, :].rearrange("p (h d) -> p h d", d=HD)
                c(v.tensor_tensor(squares[:, i * H:i * H + H, :], cen, cen, ALU.mult))
            c.wait()
            c(v.tensor_reduce(sums[:, :], squares[:, :, :], AX.X, ALU.add))
            c.wait()
            c(v.tensor_scalar(var[:, n, :], sums[:, :], 1.0 / HD, EPS_LN, ALU.mult, ALU.add))

        linear(prog, T, ln_rows(x, mean, rstd), w, 3 * D, epilogue, 9, ident)

        s_sd, s_r, s_q, s_k = (fresh(prog, k) for k in ("head_sd", "head_rstd", "head_q", "head_k"))
        with nc.Block() as block:
            @block.scalar
            def _(a):
                a.activation(sd[:, :, :], var[:, :, :], ACT.Sqrt).then_inc(s_sd, 1)

            def apply(eng, c, t, i):
                th = t[:, :, :].rearrange("p t (h d) -> p t h d", d=HD)
                c(eng.tensor_tensor(th, th, var[:, :, i * H:i * H + H].unsqueeze(3).to_broadcast([P, T, H, HD]), ALU.mult))
                c.wait()
                c(eng.tensor_tensor(t[:, :, :], t[:, :, :], gain[:, i, :].unsqueeze(1).to_broadcast([P, T, D]), ALU.mult))
                c.wait()
                c(eng.tensor_tensor(t[:, :, :], t[:, :, :], shift[:, i, :].unsqueeze(1).to_broadcast([P, T, D]), ALU.add))
                c.wait()

            @block.vector
            def _(v):
                c = Counted(v, s_q)
                c(v.tensor_scalar(gain[:, 0, :], gain[:, 0, :], 0.25, None, ALU.mult))
                c(v.tensor_scalar(shift[:, 0, :], shift[:, 0, :], 0.25, None, ALU.mult))
                v.wait_ge(s_sd, 1)
                v.reciprocal(var[:, :, :], sd[:, :, :]).then_inc(s_r, 1)
                v.wait_ge(s_r, 1)
                c.wait()
                apply(v, c, qn, 0)

            @block.gpsimd
            def _(g):
                g.wait_ge(s_r, 1)
                apply(g, Counted(g, s_k), kn, 1)


def cross_q(bias):
    def fill(qn):
        def epilogue(v, prod, n, p, c):
            c(v.tensor_tensor(qn[:, n, :], prod[:, 0, 0:D], bias[:, :], ALU.add))
            c.wait()
            c(v.tensor_scalar(qn[:, n, :], qn[:, n, :], 0.25, None, ALU.mult))
        return epilogue
    return fill


def experts(prog, x, st, mean, rstd, gate, w, iota, ident):
    nc = prog["nc"]
    s_fetch, s_turned = fresh(prog, "mfetch"), fresh(prog, "mturned")
    s_copied, s_gate, s_w = Slots(prog, "mcopied"), Slots(prog, "mgate"), Slots(prog, "mprod", 5)
    s_d, s_e = fresh(prog, "mdiff"), fresh(prog, "mexp")
    s_gc = fresh(prog, "mgchain")
    s_used, s_gused = Slots(prog, "mused", 4), Slots(prog, "mgused", 2)
    s_tick = fresh(prog, "mtick")
    per = 14
    with ExitStack() as cx:
        def sb(name, shape, dt=F32):
            return cx.enter_context(nc.sbuf_tensor(name, shape, dt))
        xn = [sb(f"mxn{p}", [P, D]) for p in range(2)]
        xt = [sb(f"mxt{p}", [P, 2, P]) for p in range(2)]
        lg, m8, i8, pair = sb("mlg", [P, NE]), sb("mm8", [P, 8]), sb("mi8", [P, 8], U32), sb("mpair", [P, 2])
        dif, ex, den, w1, w2 = (sb(k, [P, 1]) for k in ("mdif", "mex", "mden", "mw1", "mw2"))
        wa, wb, we = sb("mwa", [P, NE]), sb("mwb", [P, NE]), sb("mwe", [P, NE])
        turn = [cx.enter_context(nc.psum_tensor(f"mturn{p}", [P, 512], F32)) for p in range(2)]
        pg = [cx.enter_context(nc.psum_tensor(f"mpg{p}", [P, 512], F32)) for p in range(2)]
        prod = cx.enter_context(nc.psum_tensor("mprodp", [P, 4, 512], F32))
        block = cx.enter_context(nc.Block())

        def every(body, eng):
            with eng.Fori(0, T // 2 - 1) as i:
                for p in range(2):
                    body(2 * i + p, p, False)
            body(T - 2, 0, False)
            body(T - 1, 1, True)

        @block.tensor
        def _(pe):
            def turn_tile(n, p):
                pe.wait_ge(s_fetch, n + 1)
                s_copied.wait(pe, n - 1)
                for k in range(2):
                    m = pe.transpose(turn[p][:, k * P:(k + 1) * P], xn[p][:, k * P:(k + 1) * P], ident[:, :])
                m.then_inc(s_turned, 1)

            def multiply(n, p, last):
                if not last:
                    turn_tile(n + 1, 1 - p)
                s_copied.wait(pe, n + 1)
                s_gused.wait(pe, n - 1)
                for k in range(2):
                    m = pe.matmul(pg[p][:, 0:NE], xt[p][:, k, :], gate[:, k, :], start=(k == 0), stop=(k == 1))
                m.then_inc(s_gate.sem, 1)
                for b in range(4):
                    s_used.wait(pe, 4 * n + b - 3)
                    for k in range(2):
                        m = pe.matmul(prod[:, b, :], xt[p][:, k, :], w[:, k, b * 512:b * 512 + 512],
                                      start=(k == 0), stop=(k == 1))
                    m.then_inc(s_w.sem, 1)
            s_gate.open(pe)
            s_w.open(pe)
            turn_tile(0, 0)
            every(multiply, pe)

        @block.scalar
        def _(a):
            def copy(n, p, last):
                s_w.wait(a, 4 * (n - 1))
                a.wait_ge(s_turned, n + 1)
                a.copy(xt[p][:, :, :], turn[p][:, 0:D].rearrange("p (k n) -> p k n", k=2)).then_inc(s_copied.sem, 1)
                a.wait_ge(s_d, n + 1)
                a.activation(ex[:, :], dif[:, :], ACT.Exp).then_inc(s_e, 1)
            s_copied.open(a)
            every(copy, a)

        @block.vector
        def _(v):
            fetch = ln_rows(x, mean, rstd)
            s_used.open(v)
            s_gused.open(v)
            for n in range(2):
                fetch(v, xn[n], n).then_inc(s_fetch, 1)

            def body(n, p, last):
                c = Counted(v, s_gc, n * per)
                s_gate.wait(v, n + 1)
                v.tensor_copy(lg[:, :], pg[p][:, 0:NE]).then_inc(s_gused.sem, 1)
                s_gused.wait(v, n + 1)
                v.sem_inc(s_tick, 1)
                c(v.max(m8[:, :], lg[:, :]))
                c.wait()
                v.sem_inc(s_tick, 1)
                c(v.max_index(i8[:, :], m8[:, :], lg[:, :]))
                v.tensor_tensor(dif[:, :], m8[:, 1:2], m8[:, 0:1], ALU.subtract).then_inc(s_d, 1)
                c.wait()
                c(v.tensor_copy(pair[:, :], i8[:, 0:2]))
                v.wait_ge(s_e, n + 1)
                c(v.tensor_scalar(den[:, :], ex[:, :], 1.0, None, ALU.add))
                c.wait()
                c(v.reciprocal(w1[:, :], den[:, :]))
                c.wait()
                c(v.tensor_tensor(w2[:, :], ex[:, :], w1[:, :], ALU.mult))
                c(v.tensor_scalar(wa[:, :], iota[:, :], pair[:, 0:1], w1[:, :], ALU.is_equal, ALU.mult))
                c.wait()
                c(v.tensor_scalar(wb[:, :], iota[:, :], pair[:, 1:2], w2[:, :], ALU.is_equal, ALU.mult))
                c.wait()
                c(v.tensor_tensor(we[:, :], wa[:, :], wb[:, :], ALU.add))
                c.wait()
                for e in range(NE):
                    if e % 2 == 0:
                        s_w.wait(v, 4 * n + e // 2 + 1)
                    o = v.scalar_tensor_tensor(x[:, n, :], prod[:, e // 2, (e % 2) * D:(e % 2) * D + D], we[:, e:e + 1],
                                               x[:, n, :], ALU.mult, ALU.add)
                    if e % 2:
                        o.then_inc(s_used.sem, 1)
                        s_used.wait(v, 4 * n + e // 2 + 1)
                    else:
                        c(o)
                        c.wait()
                c(v.bn_stats(st[:, n, :], x[:, n, :]))
                assert c.n == per, c.n
                if not (type(n) is int and n + 2 >= T):
                    v.wait_ge(s_turned, n + 1)
                    fetch(v, xn[p], n + 2).then_inc(s_fetch, 1)
            every(body, v)



def focused_qkv(prog, x, mean, rstd, w, qf, kf, vf, ident):
    nc = prog["nc"]
    with ExitStack() as cx:
        sums = cx.enter_context(nc.sbuf_tensor("fsum", [P, 2 * H], F32))
        rs = cx.enter_context(nc.sbuf_tensor("frs", [P, 2 * H], F32))
        a = cx.enter_context(nc.sbuf_tensor("fa", [P, 2 * H, HD], F32))
        b = cx.enter_context(nc.sbuf_tensor("fb", [P, 2 * H, HD], F32))
        spread = lambda t, i, n: t[:, i:i + n].unsqueeze(2).to_broadcast([P, n, HD])

        def epilogue(v, prod, n, p, c):
            qk = prod[:, 0, :].rearrange("p (h d) -> p h d", d=HD)
            c(v.tensor_copy(vf[:, n, :], prod[:, 1, 0:D]))
            c(v.tensor_scalar(a[:, :, :], qk, 0.0, EPS_FOCUS, ALU.max, ALU.add))
            c.wait()
            c(v.tensor_reduce(sums[:, :], a[:, :, :], AX.X, ALU.add))
            c.wait()
            c(v.reciprocal(rs[:, :], sums[:, :]))
            c.wait()
            c(v.tensor_tensor(a[:, :, :], a[:, :, :], spread(rs, 0, 2 * H), ALU.mult))
            c.wait()
            c(v.tensor_tensor(b[:, :, :], a[:, :, :], a[:, :, :], ALU.mult))
            c.wait()
            c(v.tensor_tensor(b[:, :, :], b[:, :, :], a[:, :, :], ALU.mult))
            c.wait()
            c(v.tensor_reduce(sums[:, :], b[:, :, :], AX.X, ALU.add))
            c.wait()
            c(v.reciprocal(rs[:, :], sums[:, :]))
            c.wait()
            for i, dst in enumerate((qf, kf)):
                c(v.tensor_tensor(dst[:, n, :].rearrange("p (h d) -> p h d", d=HD), b[:, i * H:i * H + H, :],
                                  spread(rs, i * H, H), ALU.mult))
        linear(prog, T, ln_rows(x, mean, rstd), w, 3 * D, epilogue, 11, ident)


def linear_attention(prog, qf, kf, vf, yt, tap, tap_bias, mask, ones, ident):
    nc = prog["nc"]
    s = {k: fresh(prog, k) for k in ("kv", "v", "bd", "tr", "ev", "num", "g")}
    with ExitStack() as cx:
        ksum = cx.enter_context(nc.sbuf_tensor("ksum", [P, D], F32))
        prodq = cx.enter_context(nc.sbuf_tensor("prodq", [P, T, H, HD], F32))
        z = cx.enter_context(nc.sbuf_tensor("lz", [P, T, H], F32))
        bd = cx.enter_context(nc.sbuf_tensor("lbd", [P, 2, P], F32))
        qt = cx.enter_context(nc.sbuf_tensor("lqt", [P, 2, 512], F32))
        ot = cx.enter_context(nc.sbuf_tensor("lot", [P, 2, S + 2], F32))
        ps_k = cx.enter_context(nc.psum_tensor("lpsk", [P, 512], F32))
        ps_kv = [cx.enter_context(nc.psum_tensor(f"lpskv{j}", [P, 512], F32)) for j in range(2)]
        ps_t = cx.enter_context(nc.psum_tensor("lpst", [P, 2, 512], F32))
        ps_n = cx.enter_context(nc.psum_tensor("lpsn", [P, 2, 512], F32))
        block = cx.enter_context(nc.Block())

        @block.tensor
        def _(pe):
            for t in range(T):
                pe.matmul(ps_k[:, 0:D], ones[:, :], kf[:, t, :], start=(t == 0), stop=(t == T - 1))
                for j in range(2):
                    m = pe.matmul(ps_kv[j][:, 0:P], kf[:, t, j * P:j * P + P], vf[:, t, j * P:j * P + P],
                                  start=(t == 0), stop=(t == T - 1))
            m.then_inc(s["kv"], 1)
            pe.wait_ge(s["v"], 6)
            for c in range(4):
                if c:
                    pe.wait_ge(s["ev"], c)
                for j in range(2):
                    for t in range(4):
                        m = pe.transpose(ps_t[:, j, t * P:t * P + P], qf[:, 4 * c + t, j * P:j * P + P], ident[:, :])
                m.then_inc(s["tr"], 1)
                pe.wait_ge(s["ev"], c + 1)
                if c:
                    pe.wait_ge(s["g"], 1 + c)
                for j in range(2):
                    m = pe.matmul(ps_n[:, j, :], bd[:, j, :], qt[:, j, :], start=True, stop=True)
                m.then_inc(s["num"], 1)

        @block.scalar
        def _(a):
            for c in range(4):
                a.wait_ge(s["tr"], c + 1)
                if c:
                    a.wait_ge(s["num"], c)
                a.copy(qt[:, :, :], ps_t[:, :, :]).then_inc(s["ev"], 1)

        @block.vector
        def _(v):
            c = Counted(v, s["v"])
            v.memset(ot[:, :, 0:S + 2:S + 1], 0.0).then_inc(s["g"], 1)
            v.wait_ge(s["kv"], 1)
            c(v.tensor_copy(ksum[:, :], ps_k[:, 0:D]))
            for j in range(2):
                v.tensor_tensor(bd[:, j, :], ps_kv[j][:, 0:P], mask[:, :], ALU.mult).then_inc(s["bd"], 1)
            v.wait_ge(s["bd"], 2)
            c.wait()
            q4 = qf[:, :, :].rearrange("p t (h d) -> p t h d", d=HD)
            c(v.tensor_tensor(prodq[:, :, :, :].rearrange("p t h d -> p t (h d)"), qf[:, :, :],
                              ksum[:, :].unsqueeze(1).to_broadcast([P, T, D]), ALU.mult))
            c.wait()
            c(v.tensor_reduce(z[:, :, :], prodq[:, :, :, :], AX.X, ALU.add))
            c.wait()
            c(v.tensor_scalar(z[:, :, :], z[:, :, :], EPS_FOCUS, None, ALU.add))
            c.wait()
            c(v.reciprocal(prodq[:, :, :, 0], z[:, :, :]))
            c.wait()
            c(v.tensor_tensor(q4, q4, prodq[:, :, :, 0].unsqueeze(3).to_broadcast([P, T, H, HD]), ALU.mult))
            for k in range(4):
                v.wait_ge(s["num"], k + 1)
                v.tensor_copy(ot[:, :, 1 + 512 * k:1 + 512 * k + 512], ps_n[:, :, :]).then_inc(s["g"], 1)
            v.wait_ge(s["g"], 5)
            for j in range(2):
                c(v.tensor_scalar(yt[:, j, :], ot[:, j, 1:S + 1], tap[:, j, 1:2], tap_bias[:, j:j + 1], ALU.mult, ALU.add))
            for sh, i in ((0, 0), (2, 2), (1, 3)):
                c.wait()
                for j in range(2):
                    if i == 3:
                        c(v.tensor_tensor(yt[:, j, :], yt[:, j, :], ot[:, j, 1:S + 1], ALU.add))
                    else:
                        c(v.scalar_tensor_tensor(yt[:, j, :], ot[:, j, sh:sh + S], tap[:, j, i:i + 1], yt[:, j, :],
                                                 ALU.mult, ALU.add))
            c.wait()


def cross_keys(prog, ctx_t, wk, bk, keyt):
    nc = prog["nc"]
    s_m, s_c = fresh(prog, "ckm"), fresh(prog, "ckc")
    with ExitStack() as cx:
        ps = cx.enter_context(nc.psum_tensor("ckps", [P, 2, 4, 512], F32))
        block = cx.enter_context(nc.Block())

        @block.tensor
        def _(pe):
            for j in range(2):
                for b in range(4):
                    w = min(512, M - 512 * b)
                    for k in range(2):
                        m = pe.matmul(ps[:, j, b, 0:w], wk[0:CH, k, j * P:j * P + P], ctx_t[:, k, 512 * b:512 * b + w],
                                      start=(k == 0), stop=(k == 1))
                m.then_inc(s_m, 1)

        @block.vector
        def _(v):
            for j in range(2):
                v.wait_ge(s_m, j + 1)
                v.tensor_scalar(keyt[:, j, 0:M], ps[:, j, :, :].rearrange("p b n -> p (b n)")[:, 0:M], bk[:, j:j + 1], None,
                                ALU.add).then_inc(s_c, 1)
            v.wait_ge(s_c, 2)


def cross_one_head(prog, x, st, mean, rstd, wq, bq, keyt, vals, ident):
    nc = prog["nc"]
    s = {k: fresh(prog, k) for k in ("xf", "xtr", "xcp", "qm", "qc", "sc", "mx", "r", "ev")}
    for k in ("ex", "pt", "av", "o"):
        s[k] = Slots(prog, "x" + k, 4 if k == "ev" else 2)
    LAST = M - (TM - 1) * P
    UT = -(-TM // 4)
    with ExitStack() as cx:
        def sb(name, shape, dt=F32):
            return cx.enter_context(nc.sbuf_tensor(name, shape, dt))
        xn, xt, qt = sb("oxn", [P, D]), sb("oxt", [P, 2, P]), [sb(f"oqt{p}", [P, 2, P]) for p in range(2)]
        pn, pt = [sb(f"opn{p}", [P, MP]) for p in range(2)], sb("opt", [P, TM, P])
        nm, sm, rr = [sb(f"onm{p}", [P, 1]) for p in range(2)], [sb(f"osm{p}", [P, 1]) for p in range(2)], sb("orr", [P, 1])
        ps_s = cx.enter_context(nc.psum_tensor("ops_s", [P, 2048], F32))
        ps_x = cx.enter_context(nc.psum_tensor("ops_x", [P, 2, P], F32))
        ps_q = ps_x
        ps_p = cx.enter_context(nc.psum_tensor("ops_p", [P, 2, 4, P], F32))
        ps_o = cx.enter_context(nc.psum_tensor("ops_o", [P, 512], F32))
        block = cx.enter_context(nc.Block())

        def every(body, eng):
            with eng.Fori(0, T // 2 - 1) as i:
                for p in range(2):
                    body(2 * i + p, p, True)
            body(T - 2, 0, True)
            body(T - 1, 1, False)

        @block.tensor
        def _(pe):
            def query(n, p):
                pe.wait_ge(s["xf"], n + 1)
                if not (type(n) is int and n == 0):
                    pe.wait_ge(s["qc"], n)
                for k in range(2):
                    m = pe.transpose(ps_x[:, k, :], xn[:, k * P:k * P + P], ident[:, :])
                m.then_inc(s["xtr"], 1)
                pe.wait_ge(s["xcp"], n + 1)
                for j in range(2):
                    for k in range(2):
                        m = pe.matmul(ps_q[:, j, :], wq[:, k, j * P:j * P + P], xt[:, k, :], start=(k == 0), stop=(k == 1))
                m.then_inc(s["qm"], 1)

            def score(n, p):
                pe.wait_ge(s["qc"], n + 1)
                s["ex"].wait(pe, n)
                for b in range(4):
                    w = min(512, M - 512 * b)
                    for j in range(2):
                        m = pe.matmul(ps_s[:, 512 * b:512 * b + w], qt[p][:, j, :], keyt[:, j, 512 * b:512 * b + w],
                                      start=(j == 0), stop=(j == 1))
                m.then_inc(s["sc"], 1)
            s["av"].open(pe)
            query(0, 0)
            score(0, 0)

            def body(n, p, more):
                if more:
                    query(n + 1, 1 - p)
                s["ex"].wait(pe, n + 1)
                for u in range(UT):
                    s["pt"].wait(pe, n * UT + u - 1)
                    for t in range(4 * u, min(TM, 4 * u + 4)):
                        r = P if t < TM - 1 else LAST
                        m = pe.transpose(ps_p[0:r, u % 2, t % 4, :], pn[p][:, t * P:t * P + r], ident[:, :])
                    m.then_inc(s["ev"], 1)
                if more:
                    score(n + 1, 1 - p)
                s["pt"].wait(pe, n * UT + UT)
                s["o"].wait(pe, n)
                for t in range(TM):
                    r = P if t < TM - 1 else LAST
                    m = pe.matmul(ps_o[:, 0:D], pt[0:r, t, :], vals[0:r, t, :], start=(t == 0), stop=(t == TM - 1))
                m.then_inc(s["av"].sem, 1)
            every(body, pe)

        @block.scalar
        def _(a):
            def query(n, p):
                a.wait_ge(s["xtr"], n + 1)
                a.copy(xt[:, :, :], ps_x[:, :, :]).then_inc(s["xcp"], 1)
            s["ex"].open(a)
            s["pt"].open(a)
            query(0, 0)

            def body(n, p, more):
                a.wait_ge(s["mx"], n + 1)
                a.activation(pn[p][:, 0:M], ps_s[:, 0:M], ACT.Exp, bias=nm[p][:, :], accum_out=sm[p][:, :]).then_inc(s["ex"].sem, 1)
                if more:
                    query(n + 1, 1 - p)
                for u in range(UT):
                    a.wait_ge(s["ev"], n * UT + u + 1)
                    s["av"].wait(a, n)
                    lo, hi = 4 * u, min(TM, 4 * u + 4)
                    r = P if hi < TM else LAST
                    a.copy(pt[0:r, lo:hi, :], ps_p[0:r, u % 2, 0:hi - lo, :]).then_inc(s["pt"].sem, 1)
            every(body, a)

        @block.vector
        def _(v):
            fetch = ln_rows(x, mean, rstd)

            def query(n, p):
                v.wait_ge(s["qm"], n + 1)
                for j in range(2):
                    o = v.tensor_scalar(qt[p][:, j, :], ps_q[:, j, :], bq[:, j:j + 1], 1.0 / 16.0, ALU.add, ALU.mult)
                o.then_inc(s["qc"], 1)
            s["o"].open(v)
            fetch(v, xn, 0).then_inc(s["xf"], 1)
            query(0, 0)

            def body(n, p, more):
                v.wait_ge(s["sc"], n + 1)
                v.tensor_reduce(nm[p][:, :], ps_s[:, 0:M], AX.X, ALU.max, negate=True).then_inc(s["mx"], 1)
                if more:
                    v.wait_ge(s["xtr"], n + 1)
                    fetch(v, xn, n + 1).then_inc(s["xf"], 1)
                    query(n + 1, 1 - p)
                s["ex"].wait(v, n + 1)
                v.reciprocal(rr[:, :], sm[p][:, :]).then_inc(s["r"], 1)
                v.wait_ge(s["r"], 2 * n + 1)
                s["av"].wait(v, n + 1)
                v.scalar_tensor_tensor(x[:, n, :], ps_o[:, 0:D], rr[:, :], x[:, n, :], ALU.mult, ALU.add).then_inc(s["o"].sem, 1)
                s["o"].wait(v, n + 1)
                v.bn_stats(st[:, n, :], x[:, n, :]).then_inc(s["r"], 1)
                v.wait_ge(s["r"], 2 * n + 2)
            every(body, v)


def quantise(prog, items, ident):
    nc = prog["nc"]
    s_v, s_g = fresh(prog, "qv"), fresh(prog, "qg")
    with ExitStack() as cx:
        am = cx.enter_context(nc.sbuf_tensor("qam", [P, len(items)], F32))
        al = cx.enter_context(nc.sbuf_tensor("qal", [P, len(items)], F32))
        block = cx.enter_context(nc.Block())

        @block.vector
        def _(v):
            c = Counted(v, s_v)
            for i, (src, work, magic, scale, inv) in enumerate(items):
                c(v.tensor_reduce(am[:, i:i + 1], src, AX.X, ALU.max, apply_absolute_value=True))
            v.wait_ge(s_g, 1)
            for i, (src, work, magic, scale, inv) in enumerate(items):
                c(v.tensor_scalar(scale, al[:, i:i + 1], 1e-12, None, ALU.max))
                c.wait()
                c(v.reciprocal(inv, scale))
                c.wait()
                c(v.tensor_scalar(scale, inv, FP8_MAX, FP8_MAX, ALU.mult, ALU.min))
                c.wait()
                c(v.reciprocal(inv, scale))
                c(v.tensor_scalar(src, src, scale, FP8_MAX, ALU.mult, ALU.min))
                c.wait()
                c(v.tensor_scalar(src, src, -FP8_MAX, None, ALU.max))
                c.wait()
                c(v.tensor_scalar(magic.bitcast(I32), src.bitcast(I32), 0x7F800000, None, ALU.bitwise_and))
                c.wait()
                c(v.tensor_scalar(magic, magic, 2.0 ** -6, 1.5 * 2.0 ** 20, ALU.max, ALU.mult))
                c.wait()
                c(v.tensor_tensor(src, src, magic, ALU.add))
                c.wait()
                c(v.tensor_tensor(src, src, magic, ALU.subtract))
                c.wait()

        @block.gpsimd
        def _(g):
            g.wait_ge(s_v, len(items))
            g.partition_all_reduce(al[:, :], am[:, :], P, bass.bass_isa.ReduceOp.max).then_inc(s_g, 1)



def decoder(nc, a, out, upto=99):
    with ExitStack() as ctx:
        prog = {"nc": nc, "ctx": ctx}

        def sb(cx, name, shape, dt=F32):
            return cx.enter_context(nc.sbuf_tensor(name, shape, dt))
        x = sb(ctx, "x_res", [P, T, D])
        st, tmp = sb(ctx, "stats", [P, T, 6]), sb(ctx, "ln_tmp", [P, 2, T])
        mean, rstd = sb(ctx, "ln_mean", [P, T]), sb(ctx, "ln_rstd", [P, T])
        ident, identb = sb(ctx, "ident", [P, P]), sb(ctx, "identb", [P, P], BF16)
        ones = sb(ctx, "ones", [P, P])
        s0 = fresh(prog, "start")
        x_rows = a["x"].rearrange("(t p) d -> p t d", p=P)
        load(prog, [(x[:, :, :], x_rows), (ident[:, :], a["ident"]), (ones[:, :], a["ones"])])
        with nc.Block() as block:
            @block.vector
            def _(v):
                v.tensor_copy(identb[:, :], ident[:, :]).then_inc(s0, 1)
                for t in range(T):
                    v.bn_stats(st[:, t, :], x[:, t, :]).then_inc(s0, 1)
                v.wait_ge(s0, T + 1)

        def layer_norm():
            ln_finish(prog, st, mean, rstd, tmp)

        def done():
            load(prog, [(out.rearrange("(t p) d -> p t d", p=P), x[:, :, :])])

        with ExitStack() as l0:
            qn, v_nat = sb(l0, "q_rows", [P, T, D]), sb(l0, "v_rows", [P, T, D])
            with ExitStack() as cs:
                kt = sb(cs, "k_stack", [P, H, S], BF16)
                with ExitStack() as cx:
                    kn = sb(cx, "k_rows", [P, T, D])
                    w = sb(cx, "w_qkv", [P, 2, 3 * D])
                    gain, shift = sb(cx, "gain", [P, 2, D]), sb(cx, "shift", [P, 2, D])
                    load(prog, [(w[:, :, :], rows2(a["w0_qkv"])), (gain[:, :, :], a["gain"]), (shift[:, :, :], a["shift"])])
                    layer_norm()
                    self_qkv(prog, x, mean, rstd, w, gain, shift, qn, kn, v_nat, ident)
                    build_kt(prog, kn, T, kt, identb)
                attention(prog, qn, v_nat, T, kt, ones, ident, identb)
            with ExitStack() as cx:
                w = sb(cx, "w_proj", [P, 2, D])
                load(prog, [(w[:, :, :], rows2(a["w0_proj"]))])
                linear(prog, T, plain_rows(qn), w, D, residual(x, st), 2, ident)
            if upto <= 1:
                return done()
            layer_norm()
            with ExitStack() as cs:
                kt = sb(cs, "k_stack2", [P, H, MP], BF16)
                valid = sb(cs, "valid", [P, TM])
                with ExitStack() as cx:
                    kn = sb(cx, "k_rows2", [P, TM, D])
                    wq, bq = sb(cx, "w_xq", [P, 2, D]), sb(cx, "b_xq", [P, D])
                    wkv, bkv = sb(cx, "w_xkv", [CH, 2, 2 * D]), sb(cx, "b_xkv", [P, 2 * D])
                    ctx_t = sb(cx, "ctx_t", [CH, 2, MP])
                    load(prog, [(wq[:, :, :], rows2(a["w0_xq"])), (bq[:, :], a["b0_xq"]), (wkv[:, :, :], rows2(a["w0_xkv"])),
                                (bkv[:, :], a["b0_xkv"]), (ctx_t[:, :, :], rows2(a["ctx_t"])), (valid[:, :], a["valid"])])
                    linear(prog, T, ln_rows(x, mean, rstd), wq, D, cross_q(bq)(qn), 2, ident)

                    def keys_values(v, prod, n, p, c):
                        c(v.tensor_tensor(kn[:, n, :], prod[:, 0, 0:D], bkv[:, 0:D], ALU.add))
                        c(v.tensor_tensor(v_nat[:, n, :], prod[:, 0, D:2 * D], bkv[:, D:2 * D], ALU.add))
                        c.wait()
                        c(v.tensor_scalar(v_nat[:, n, :], v_nat[:, n, :], valid[:, at(n)], None, ALU.mult))
                    linear(prog, TM, None, wkv, 2 * D, keys_values, 3, rows=CH, direct=lambda n: ctx_t[:, :, at(n * P, P)])
                    build_kt(prog, kn, TM, kt, identb)
                attention(prog, qn, v_nat, TM, kt, valid, ident, identb)
            with ExitStack() as cx:
                w, b = sb(cx, "w_xo", [P, 2, D]), sb(cx, "b_xo", [P, D])
                load(prog, [(w[:, :, :], rows2(a["w0_xo"])), (b[:, :], a["b0_xo"])])
                linear(prog, T, plain_rows(qn), w, D, residual(x, st, b), 3, ident)
        if upto <= 2:
            return done()
        layer_norm()
        with ExitStack() as cx:
            gate, w, iota = sb(cx, "w_gate", [P, 2, NE]), sb(cx, "w_experts", [P, 2, NE * D]), sb(cx, "iota8", [P, NE])
            load(prog, [(gate[:, :, :], rows2(a["w0_gate"])), (w[:, :, :], rows2(a["w0_experts"])), (iota[:, :], a["iota"])])
            experts(prog, x, st, mean, rstd, gate, w, iota, ident)
        if upto <= 3:
            return done()
        layer_norm()
        with ExitStack() as cx:
            yt = sb(cx, "conv_out", [P, 2, S])
            with ExitStack() as cy:
                qf, kf, vf = (sb(cy, k, [P, T, D]) for k in ("q_focus", "k_focus", "v_focus"))
                w, mask = sb(cy, "w1_qkv", [P, 2, 3 * D]), sb(cy, "head_mask", [P, P])
                tap, tap_bias = sb(cy, "taps", [P, 2, 3]), sb(cy, "tap_bias", [P, 2])
                load(prog, [(w[:, :, :], rows2(a["w1_qkv"])), (mask[:, :], a["mask"]), (tap[:, :, :], rows2(a["taps"])),
                            (tap_bias[:, :], a["tap_bias"])])
                focused_qkv(prog, x, mean, rstd, w, qf, kf, vf, ident)
                linear_attention(prog, qf, kf, vf, yt, tap, tap_bias, mask, ones, ident)
            w, b = sb(cx, "w1_proj", [P, 2, D]), sb(cx, "b1_proj", [P, D])
            load(prog, [(w[:, :, :], rows2(a["w1_proj"])), (b[:, :], a["b1_proj"])])
            linear(prog, T, None, w, D, residual(x, st, b), 3, direct=lambda n: yt[:, :, at(n * P, P)])
        if upto <= 4:
            return done()
        layer_norm()
        with ExitStack() as cx:
            keyt, vals = sb(cx, "key_t", [P, 2, MP]), sb(cx, "values1", [P, TM, D])
            wq, bq = sb(cx, "w1_xq", [P, 2, D]), sb(cx, "b1_xq", [P, 2])
            with ExitStack() as cy:
                ctx_t = sb(cy, "ctx_t1", [CH, 2, MP])
                wk, wv = sb(cy, "w1_xk", [CH, 2, D]), sb(cy, "w1_xv", [CH, 2, D])
                bk, bv = sb(cy, "b1_xk", [P, 2]), sb(cy, "b1_xv", [P, D])
                load(prog, [(ctx_t[:, :, :], rows2(a["ctx_t"])), (wk[:, :, :], rows2(a["w1_xk"])), (wv[:, :, :], rows2(a["w1_xv"])),
                            (bk[:, :], a["b1_xk"]), (bv[:, :], a["b1_xv"]), (wq[:, :, :], rows2(a["w1_xq"])), (bq[:, :], a["b1_xq"])])
                cross_keys(prog, ctx_t, wk, bk, keyt)

                def value_rows(v, prod, n, p, c):
                    c(v.tensor_tensor(vals[:, n, :], prod[:, 0, 0:D], bv[:, :], ALU.add))
                linear(prog, TM, None, wv, D, value_rows, 1, rows=CH, direct=lambda n: ctx_t[:, :, at(n * P, P)])
            cross_one_head(prog, x, st, mean, rstd, wq, bq, keyt, vals, ident)
        if upto <= 5:
            return done()
        layer_norm()
        with ExitStack() as cx:
            xq, work = sb(cx, "x_q", [P, T, D]), sb(cx, "q_magic", [P, T, D])
            w, wm, b = sb(cx, "w1_ffn", [P, 2, D]), sb(cx, "w_magic", [P, 2, D]), sb(cx, "b1_ffn", [P, D])
            sc = sb(cx, "q_scales", [P, 5])
            load(prog, [(w[:, :, :], rows2(a["w1_ffn"])), (b[:, :], a["b1_ffn"])])
            s_n = fresh(prog, "xn_all")
            with nc.Block() as block:
                @block.vector
                def _(v):
                    c = Counted(v, s_n)
                    c(v.tensor_tensor(xq[:, :, :], x[:, :, :], mean[:, :].unsqueeze(2).to_broadcast([P, T, D]), ALU.subtract))
                    c.wait()
                    c(v.tensor_tensor(xq[:, :, :], xq[:, :, :], rstd[:, :].unsqueeze(2).to_broadcast([P, T, D]), ALU.mult))
                    c.wait()
            flat = lambda t: t[:, :, :].rearrange("p a b -> p (a b)")
            quantise(prog, [(flat(xq), None, flat(work), sc[:, 0:1], sc[:, 1:2]),
                            (flat(w), None, flat(wm), sc[:, 2:3], sc[:, 3:4])], ident)
            s_s = fresh(prog, "scale_xw")
            with nc.Block() as block:
                @block.vector
                def _(v):
                    v.tensor_tensor(sc[:, 4:5], sc[:, 1:2], sc[:, 3:4], ALU.mult).then_inc(s_s, 1)
                    v.wait_ge(s_s, 1)
            half = [sb(cx, f"y_half{p}", [P, D], BF16) for p in range(2)]

            def finish(v, prod, n, p, c):
                c(v.scalar_tensor_tensor(half[p][:, :], prod[:, 0, 0:D], sc[:, 4:5], b[:, :], ALU.mult, ALU.add))
                c.wait()
                c(v.tensor_tensor(x[:, n, :], x[:, n, :], half[p][:, :], ALU.add))
            linear(prog, T, plain_rows(xq), w, D, finish, 2, ident)
        done()


def kernel(**inputs):
    import numpy as _np
    import concourse.bacc as _bacc
    from concourse.bass_utils import run_bass_kernel_spmd as _run

    i = {k: _np.asarray(v) for k, v in inputs.items()}
    wide = lambda v: _np.broadcast_to(v, (P, v.size))
    cols = lambda v: v.reshape(2, P).T
    kv = i["L0_xattn_Wkv"].reshape(H, 2, HD, C).transpose(1, 0, 2, 3).reshape(2 * D, C)
    bkv = i["L0_xattn_bkv"].reshape(H, 2, HD).transpose(1, 0, 2).reshape(2 * D)
    ctx = i["ctx_768"][0]
    ctx = _np.concatenate([ctx, _np.broadcast_to(ctx[-1:], (MP - M, C))])
    arrays = {
        "x": i["x"][0],
        "ctx_t": ctx.T,
        "ident": _np.eye(P, dtype=_np.float32),
        "ones": _np.ones((P, P), _np.float32),
        "valid": (_np.arange(MP).reshape(TM, P).T < M).astype(_np.float32),
        "mask": _np.kron(_np.eye(P // HD), _np.ones((HD, HD))).astype(_np.float32),
        "iota": wide(_np.arange(NE, dtype=_np.float32)),
        "w0_qkv": i["L0_attn_w_qkv"],
        "gain": _np.stack([wide(_np.tile(i[f"L0_attn_{k}_gamma"], H)) for k in "qk"], 1),
        "shift": _np.stack([wide(_np.tile(i[f"L0_attn_{k}_beta"], H)) for k in "qk"], 1),
        "w0_proj": i["L0_attn_w_proj"],
        "w0_xq": i["L0_xattn_Wq"].T, "b0_xq": wide(i["L0_xattn_bq"]),
        "w0_xkv": kv.T, "b0_xkv": wide(bkv),
        "w0_xo": i["L0_xattn_Wo"].T, "b0_xo": wide(i["L0_xattn_bo"]),
        "w0_gate": i["L0_ffn_gate_w"].T,
        "w0_experts": i["L0_ffn_weight"].transpose(1, 0, 2).reshape(D, NE * D),
        "w1_qkv": i["L1_attn_w_qkv"].T,
        "w1_proj": i["L1_attn_w_proj"].T, "b1_proj": wide(i["L1_attn_b_proj"]),
        "taps": i["L1_attn_w_dwc"], "tap_bias": cols(i["L1_attn_b_dwc"]),
        "w1_xq": i["L1_xattn_Wq"], "b1_xq": cols(i["L1_xattn_bq"]),
        "w1_xk": i["L1_xattn_Wk"], "b1_xk": cols(i["L1_xattn_bk"]),
        "w1_xv": i["L1_xattn_Wv"], "b1_xv": wide(i["L1_xattn_bv"]),
        "w1_ffn": i["L1_ffn_weight"].T, "b1_ffn": wide(i["L1_ffn_bias"]),
    }
    arrays = {"in_" + k: _np.ascontiguousarray(v) for k, v in arrays.items()}
    nc = _bacc.Bacc("TRN2", target_bir_lowering=False, num_devices=1)
    args = {k[3:]: nc.dram_tensor(k, v.shape, F32, kind="ExternalInput").ap() for k, v in arrays.items()}
    out = nc.dram_tensor("out", (S, D), F32, kind="ExternalOutput").ap()
    decoder(nc, args, out)
    r = _run(nc, [arrays], core_ids=[0])
    return r.results[0]["out"].reshape(1, S, D)
```

```python
from contextlib import ExitStack

import concourse.bass as bass
from concourse import mybir

F32 = mybir.dt.float32
BF16 = mybir.dt.bfloat16
I32 = mybir.dt.int32
U32 = mybir.dt.uint32
ACT = mybir.ActivationFunctionType
ALU = mybir.AluOpType
AX = mybir.AxisListType

P = 128
D = 256
H = 16
HD = D // H
S = 2048
T = S // P
C = 192
CH = C // 2
M = 1601
TM = -(-M // P)
MP = TM * P
NE = 8
HG = 4
QC = 4
TAIL = 3
GW = HG * HD
NPART = 6
MAXROW = 96
EPS_LN = 1e-5
EPS_FOCUS = 1e-6
FP8_MAX = 448.0


class Counted:

    def __init__(self, eng, sem, base=0, fixed=None):
        self.eng, self.sem, self.base, self.n, self.fixed = eng, sem, base, 0, fixed

    def __call__(self, ins):
        self.n += 1
        ins.then_inc(self.sem, 1)
        return ins

    def wait(self):
        self.eng.wait_ge(self.sem, self.base + self.n)
        if self.fixed is not None:
            self.eng.sem_inc(self.fixed, 1)


def at(t, width=1):
    return bass.ds(t, width)


def fresh(prog, name):
    prog["n"] = prog.get("n", 0) + 1
    sem = prog["nc"].alloc_semaphore(f"{name}_{prog['n']}")
    prog["used"].append(sem)
    return sem


def recycle(prog):
    prog["nc"].clear_and_free_semaphores(prog["used"])
    prog["nc"].all_engine_barrier()
    prog["used"] = []


class Slots:

    def __init__(self, prog, name, ahead=2):
        self.sem, self.ahead = fresh(prog, name), ahead

    def open(self, eng):
        eng.sem_inc(self.sem, self.ahead)

    def wait(self, eng, value):
        eng.wait_ge(self.sem, value + self.ahead)



def ln_finish(prog, st, mean, rstd, tmp):
    nc = prog["nc"]
    s_v, s_q = fresh(prog, "lnf_v"), fresh(prog, "lnf_sqrt")
    with nc.Block() as block:
        @block.vector
        def _(v):
            c = Counted(v, s_v)
            c(v.tensor_tensor(mean[:, :], st[:, :, 1], st[:, :, 4], ALU.add))
            c(v.tensor_tensor(tmp[:, 0, :], st[:, :, 1], st[:, :, 4], ALU.subtract))
            c(v.tensor_tensor(tmp[:, 1, :], st[:, :, 2], st[:, :, 5], ALU.add))
            c.wait()
            c(v.tensor_scalar(mean[:, :], mean[:, :], 0.5, None, ALU.mult))
            c(v.tensor_tensor(tmp[:, 0, :], tmp[:, 0, :], tmp[:, 0, :], ALU.mult))
            c(v.tensor_scalar(tmp[:, 1, :], tmp[:, 1, :], 1.0 / D, EPS_LN, ALU.mult, ALU.add))
            c.wait()
            c(v.scalar_tensor_tensor(tmp[:, 1, :], tmp[:, 0, :], 0.25, tmp[:, 1, :], ALU.mult, ALU.add))
            v.wait_ge(s_q, 1)
            c(v.reciprocal(rstd[:, :], tmp[:, 0, :]))
            c.wait()

        @block.scalar
        def _(a):
            a.wait_ge(s_v, 7)
            a.activation(tmp[:, 0, :], tmp[:, 1, :], ACT.Sqrt).then_inc(s_q, 1)
            a.wait_ge(s_q, 1)



def linear(prog, tiles, fetch, w, n_cols, epilogue, per, ident=None, rows=P, direct=None, side=None):
    nc = prog["nc"]
    s_fetch, s_turned, s_copied = fresh(prog, "fetch"), fresh(prog, "turned"), Slots(prog, "copied")
    s_prod, s_chain, s_side = Slots(prog, "prod"), Slots(prog, "epilogue", per + 1), Slots(prog, "side")
    banks = -(-n_cols // 512)
    pairs = (tiles - 1) // 2
    with ExitStack() as cx:
        xn = [cx.enter_context(nc.sbuf_tensor(f"xn{prog['n']}_{p}", [P, D], F32)) for p in range(2)]
        xt = [cx.enter_context(nc.sbuf_tensor(f"xt{prog['n']}_{p}", [P, 2, P], F32)) for p in range(2)]
        turn = [cx.enter_context(nc.psum_tensor(f"turn{prog['n']}_{p}", [P, 2, 256], F32)) for p in range(2)]
        prod = [cx.enter_context(nc.psum_tensor(f"prod{prog['n']}_{p}", [P, banks, 512], F32)) for p in range(2)]

        def every(body, eng):
            if pairs:
                with eng.Fori(0, pairs) as i:
                    for p in range(2):
                        body(2 * i + p, p, False)
            for n in range(2 * pairs, tiles):
                body(n, n % 2, n == tiles - 1)

        block = cx.enter_context(nc.Block())

        @block.tensor
        def _(pe):
            def turn_tile(n, p):
                pe.wait_ge(s_fetch, n + 1)
                s_copied.wait(pe, n - 1)
                for k in range(2):
                    m = pe.transpose(turn[p][:, 0, k * P:(k + 1) * P], xn[p][:, k * P:(k + 1) * P], ident[:, :])
                m.then_inc(s_turned, 1)

            def multiply(n, p, last):
                if direct is None and not last:
                    turn_tile(n + 1, 1 - p)
                s_copied.wait(pe, n + 1)
                if side is not None:
                    s_side.wait(pe, n - 1)
                s_chain.wait(pe, (n - 1) * per)
                for b in range(banks):
                    lo, hi = b * 512, min(n_cols, b * 512 + 512)
                    for k in range(2):
                        m = pe.matmul(prod[p][:, b, 0:hi - lo], xt[p][0:rows, k, :], w[0:rows, k, lo:hi],
                                      start=(k == 0), stop=(k == 1))
                m.then_inc(s_prod.sem, 1)

            s_prod.open(pe)
            if direct is None:
                turn_tile(0, 0)
            every(multiply, pe)

        @block.scalar
        def _(a):
            def copy(n, p, last):
                s_prod.wait(a, n - 1)
                if direct is None:
                    a.wait_ge(s_turned, n + 1)
                    a.copy(xt[p][:, :, :], turn[p][:, 0, :].rearrange("p (k n) -> p k n", k=2)).then_inc(s_copied.sem, 1)
                else:
                    a.copy(xt[p][0:rows, :, :], direct(n)).then_inc(s_copied.sem, 1)

            def copy_ahead(n, p, last):
                if not last:
                    copy(n + 1, 1 - p, last)
                if side is not None:
                    s_prod.wait(a, n + 1)
                    side(a, prod[p], n).then_inc(s_side.sem, 1)
            s_copied.open(a)
            s_side.open(a)
            copy(0, 0, False)
            every(copy_ahead, a)

        @block.vector
        def _(v):
            s_chain.open(v)
            if direct is None:
                for n in range(2):
                    fetch(v, xn[n], n).then_inc(s_fetch, 1)

            def finish(n, p, last):
                if direct is None and not (type(n) is int and n + 2 >= tiles):
                    v.wait_ge(s_turned, n + 1)
                    fetch(v, xn[p], n + 2).then_inc(s_fetch, 1)
                s_prod.wait(v, n + 1)
                c = Counted(v, s_chain.sem, n * per + s_chain.ahead)
                epilogue(v, prod[p], n, p, c)
                assert c.n == per, c.n
                c.wait()
            if pairs:
                with v.Fori(0, pairs) as i:
                    for p in range(2):
                        finish(2 * i + p, p, False)
            for n in range(2 * pairs, tiles):
                finish(n, n % 2, n == tiles - 1)


def ln_rows(x, mean, rstd):
    return lambda v, out, n: v.tensor_scalar(out[:, :], x[:, n, :], mean[:, at(n)], rstd[:, at(n)],
                                             ALU.subtract, ALU.mult)


def plain_rows(src):
    return lambda v, out, n: v.tensor_copy(out[:, :], src[:, n, :])


def residual(x, st, bias=None):
    def run(v, prod, n, p, c):
        c(v.tensor_tensor(x[:, n, :], prod[:, 0, 0:D], x[:, n, :], ALU.add))
        c.wait()
        if bias is not None:
            c(v.tensor_tensor(x[:, n, :], x[:, n, :], bias[:, :], ALU.add))
            c.wait()
        c(v.bn_stats(st[:, n, :], x[:, n, :]))
    return run



def load(prog, pairs):
    nc = prog["nc"]
    s = fresh(prog, "load")
    with nc.Block() as block:
        @block.sync
        def _(e):
            for dst, src in pairs:
                e.dma_start(dst, src).then_inc(s, 16)
            e.wait_ge(s, 16 * len(pairs))


def rows2(w):
    return w.rearrange("(k p) n -> p k n", k=2)



def parts(stack, which):
    order = "hhmmlh" if which == "q" else "hmhmhl"
    out = {"h": [], "m": [], "l": []}
    for slot, part in enumerate(order):
        out[part].append(stack[..., slot * HD:(slot + 1) * HD])
    return out["h"], out["m"], out["l"]


def build_kt(prog, kn, tiles, kt, identb):
    nc = prog["nc"]
    s_set, s_rest = fresh(prog, "ks_set"), fresh(prog, "ks_rest")
    s_hi, s_lo, s_turn, s_out, s_out2 = (Slots(prog, n) for n in ("ks_hi", "ks_lo", "ks_turn", "ks_dve", "ks_act"))
    with ExitStack() as cx:
        nat = cx.enter_context(nc.sbuf_tensor(f"knat{prog['n']}", [P, 2, H, P], BF16))
        rest = [cx.enter_context(nc.sbuf_tensor(f"krest{prog['n']}_{p}", [P, H, HD], F32)) for p in range(2)]
        ps = cx.enter_context(nc.psum_tensor(f"kps{prog['n']}", [P, 4, 8, P], BF16))
        block = cx.enter_context(nc.Block())

        def every(body, eng):
            with eng.Fori(0, tiles // 2) as i:
                for p in range(2):
                    body(2 * i + p, p)
            if tiles % 2:
                body(tiles - 1, 0)

        def slots(p, first, count):
            return nat[:, p, :, first * HD:(first + 2 * count) * HD].rearrange("p h (s d) -> p h s d", d=2 * HD)[:, :, :, 0:HD]

        @block.gpsimd
        def _(g):
            g.memset(nat[:, :, :, MAXROW:P], 0.0).then_inc(s_set, 1)
            g.wait_ge(s_set, 1)
            g.memset(nat[:, :, :, MAXROW:MAXROW + 3], 1.0).then_inc(s_set, 1)

        @block.scalar
        def _(a):
            s_hi.open(a)
            s_out2.open(a)

            def split(n, p):
                s_turn.wait(a, n - 1)
                src = kn[:, n, :].rearrange("p (h d) -> p h d", d=HD)
                a.copy(slots(p, 0, 3), src.unsqueeze(2).to_broadcast([P, H, 3, HD])).then_inc(s_hi.sem, 1)

            def out(n, p):
                s_turn.wait(a, n + 1)
                a.copy(kt[:, 8:16, at(n * P, P)], ps[:, 2 * p + 1, :, :]).then_inc(s_out2.sem, 1)
            split(0, 0)

            def body(n, p):
                if not (type(n) is int and n == tiles - 1):
                    split(n + 1, 1 - p)
                out(n, p)
            loop_ahead(a, tiles, body)

        @block.vector
        def _(v):
            s_lo.open(v)
            s_out.open(v)

            def split(n, p):
                s_turn.wait(v, n - 1)
                s_hi.wait(v, n + 1)
                src = kn[:, n, :].rearrange("p (h d) -> p h d", d=HD)
                v.tensor_tensor(rest[p][:, :, :], src, nat[:, p, :, 0:HD], ALU.subtract).then_inc(s_rest, 1)
                v.wait_ge(s_rest, 2 * n + 1)
                v.tensor_copy(slots(p, 1, 2), rest[p][:, :, :].unsqueeze(2).to_broadcast([P, H, 2, HD])).then_inc(s_rest, 1)
                v.wait_ge(s_rest, 2 * n + 2)
                v.tensor_tensor(nat[:, p, :, 5 * HD:6 * HD], rest[p][:, :, :], nat[:, p, :, HD:2 * HD], ALU.subtract)\
                 .then_inc(s_lo.sem, 1)

            def out(n, p):
                s_turn.wait(v, n + 1)
                v.tensor_copy(kt[:, 0:8, at(n * P, P)], ps[:, 2 * p, :, :]).then_inc(s_out.sem, 1)
            split(0, 0)

            def body(n, p):
                if not (type(n) is int and n == tiles - 1):
                    split(n + 1, 1 - p)
                out(n, p)
            loop_ahead(v, tiles, body)

        @block.tensor
        def _(pe):
            s_turn.open(pe)
            pe.wait_ge(s_set, 2)

            def body(n, p):
                s_lo.wait(pe, n + 1)
                s_out.wait(pe, n - 1)
                s_out2.wait(pe, n - 1)
                for h in range(H):
                    m = pe.transpose(ps[:, 2 * p + h // 8, h % 8, :], nat[:, p, h, :], identb[:, :])
                m.then_inc(s_turn.sem, 1)
            every(body, pe)


def loop_ahead(eng, tiles, body):
    pairs = (tiles - 1) // 2
    with eng.Fori(0, pairs) as i:
        for p in range(2):
            body(2 * i + p, p)
    for n in range(2 * pairs, tiles):
        body(n, n % 2)


def ring(count, banks):
    use = [k % banks for k in range(count)]
    return [(use[k], next(b for b in range(1, count) if use[(k - b) % count] == use[k])) for k in range(count)]


def attention(prog, qn, v_nat, key_tiles, kt, valid, ident, identb):
    nc = prog["nc"]
    NU = QC * HG
    widths = [min(512, key_tiles * P - b) for b in range(0, key_tiles * P, 512)]
    KB = len(widths)
    UN = NU * KB
    NCH = T // QC * H // HG
    s = {k: fresh(prog, k) for k in ("set", "qsplit", "ta", "taev", "mx", "msplit", "tb", "tbev",
                                     "sc", "rc", "vst", "qcopy")}
    s["tb0"] = fresh(prog, "tb0")
    for k in ("mred", "exp", "norm", "av", "avev", "te"):
        s[k] = Slots(prog, k, 3)
    QS, MS = 8, 5
    with ExitStack() as cx:
        def sb(name, shape, dt):
            return cx.enter_context(nc.sbuf_tensor(f"{name}_{prog['n']}", shape, dt))
        qnat = [sb(f"qnat{p}", [P, QC, HG, P], BF16) for p in range(2)]
        qtmp = sb("qtmp", [P, QC, HG, HD], F32)
        qm = [sb(f"qm{p}", [MAXROW, HG, QC, P], BF16) for p in range(2)]
        qt = [sb(f"qt{p}", [P, HG, QC, P], BF16) for p in range(2)]
        vst = [sb(f"vst{p}", [P, key_tiles, HG, 32], F32) for p in range(2)]
        pbuf = [sb(f"pb{p}", [P, HG, 512], F32) for p in range(2)]
        mxp = [sb(f"mxp{p}", [P, NU, KB], F32) for p in range(2)]
        negm = sb("negm", [P, NU], F32)
        mtmp = sb("mtmp", [P, NU], F32)
        avs = sb("avs", [P, QC, P], F32)
        rc = sb("rc", [P, QC, HG], F32)
        ps_s = cx.enter_context(nc.psum_tensor(f"ps_s{prog['n']}", [P, 3, 512], F32))
        ps_m = cx.enter_context(nc.psum_tensor(f"ps_m{prog['n']}", [P, 3, 512], F32))
        ps_av = cx.enter_context(nc.psum_tensor(f"ps_av{prog['n']}", [P, 512], F32))
        ps_t = cx.enter_context(nc.psum_tensor(f"ps_t{prog['n']}", [P, QC, P], F32))
        ps_tb = ps_t[:, :, :].rearrange("p a b -> p (a b)").bitcast(BF16).rearrange("p (a b) -> p a b", b=P)
        block = cx.enter_context(nc.Block())

        def group(n):
            return n // (T // QC)

        def chunk(n):
            return n % (T // QC)

        def pairs(eng, body):
            body(0, 0, True, True)
            body(1, 1, False, True)
            with eng.Fori(1, NCH // 2 - 1) as j:
                for p in range(2):
                    body(2 * j + p, p, False, True)
            body(NCH - 2, 0, False, True)
            body(NCH - 1, 1, False, False)

        bounds = [UN * t // key_tiles for t in range(key_tiles + 1)]
        lead = UN - bounds[key_tiles - TAIL]
        ring_m, ring_s = ring(UN, 3), ring(key_tiles * HG, 3)
        TURN = (key_tiles // 2 - 3, key_tiles // 2 - 1)

        @block.gpsimd
        def _(g):
            for p in range(2):
                g.memset(qnat[p][:, :, :, :], 0.0).then_inc(s["set"], 1)
                g.memset(vst[p][:, :, :, :], 0.0).then_inc(s["set"], 1)
            g.wait_ge(s["set"], 4)
            for p in range(2):
                for h in range(HG):
                    g.tensor_copy(vst[p][:, :, h, HD], valid[:, 0:key_tiles]).then_inc(s["set"], 1)
            g.wait_ge(s["set"], 4 + 2 * HG)

            def queries(n, p):
                if not (type(n) is int and n < 2):
                    g.wait_ge(s["tb"], n - 1)
                g.sem_inc(s["set"], 1)
                c = Counted(g, s["qsplit"], n * QS, s["set"])
                src = qn[:, at(chunk(n) * QC, QC), at(group(n) * GW, GW)].rearrange("p t (h d) -> p t h d", d=HD)
                c(g.tensor_copy(qtmp[:, :, :, :], src))
                c.wait()
                hi, mid, lo = parts(qnat[p][:, :, :, :], "q")
                for d in hi:
                    c(g.tensor_copy(d, qtmp[:, :, :, :]))
                c.wait()
                c(g.tensor_tensor(qtmp[:, :, :, :], qtmp[:, :, :, :], hi[0], ALU.subtract))
                c.wait()
                for d in mid:
                    c(g.tensor_copy(d, qtmp[:, :, :, :]))
                c.wait()
                c(g.tensor_tensor(lo[0], qtmp[:, :, :, :], mid[0], ALU.subtract))
                assert c.n == QS, c.n
                c.wait()

            def values(n, p):
                g.tensor_copy(vst[p][:, :, :, 0:HD],
                              v_nat[:, 0:key_tiles, at(group(n) * GW, GW)].rearrange("p t (h d) -> p t h d", d=HD))\
                 .then_inc(s["vst"], 1)

            queries(0, 0)
            values(0, 0)
            queries(1, 1)

            def body(n, p, first, more):
                if more:
                    if not first:
                        s["av"].wait(g, n * key_tiles)
                        g.sem_inc(s["set"], 1)
                    values(n + 1, 1 - p)
                    if not (type(n) is int and n + 2 >= NCH):
                        queries(n + 2, p)
            pairs(g, body)

        @block.tensor
        def _(pe):
            def turn_q(n, p, half):
                if half == 0:
                    pe.wait_ge(s["qsplit"], n * QS + QS)
                    s["norm"].wait(pe, n - 2)
                    if type(n) is int and n == 1:
                        pe.wait_ge(s["tbev"], 2)
                else:
                    pe.wait_ge(s["taev"], 2 * n + 1)
                for u in range(8):
                    a, h = 2 * half + u // HG, u % HG
                    m = pe.transpose(ps_tb[0:MAXROW, u, :], qnat[p][:, a, h, 0:MAXROW], identb[:, :])
                m.then_inc(s["ta"], 1)

            def turn_m(n, p, half):
                if half == 0:
                    pe.wait_ge(s["msplit"], n * MS + MS)
                    if type(n) is int and n in (0, NCH - 1):
                        pe.wait_ge(s["taev"], 2 * n + 2)
                        s["norm"].wait(pe, n - 1)
                    else:
                        pe.wait_ge(s["taev"], 2 * n + 4)
                else:
                    pe.wait_ge(s["tbev"], 2 * n + 1)
                for u in range(8):
                    a, h = 2 * half + u // HG, u % HG
                    m = pe.transpose(ps_tb[MAXROW:P, u, :], qnat[p][:, a, h, MAXROW:P], identb[:, :])
                m.then_inc(s["tb"] if half else s["tb0"], 1)

            def max_unit(n, p, u):
                a, h, b = u // (HG * KB), u // KB % HG, u % KB
                bank, back = ring_m[(u - lead) % UN]
                s["mred"].wait(pe, n * UN + u - back + 1)
                pe.matmul(ps_m[:, bank, 0:widths[b]], qm[p][:, h, a, :],
                          kt[0:MAXROW, group(n) * HG + h, b * 512:b * 512 + widths[b]],
                          start=True, stop=True).then_inc(s["mx"], 1)

            def score(n, p, t, h):
                bank, back = ring_s[t * HG + h]
                s["exp"].wait(pe, (n * key_tiles + t) * HG + h - back + 1)
                m = pe.matmul(ps_s[:, bank, :], kt[:, group(n) * HG + h, t * P:(t + 1) * P], qt[p][:, h, :, :],
                              start=True, stop=True)
                m.then_inc(s["sc"], 1)

            def values(n, p, t):
                s["exp"].wait(pe, (n * key_tiles + t) * HG + HG)
                if t == 0:
                    pe.wait_ge(s["vst"], n + 1)
                    s["avev"].wait(pe, n)
                for h in range(HG):
                    m = pe.matmul(ps_av[32 * h:32 * h + 32, :], vst[p][:, t, h, :], pbuf[t % 2][:, h, :],
                                  start=(t == 0), stop=(t == key_tiles - 1))
                m.then_inc(s["av"].sem, 1)

            def results(n):
                s["avev"].wait(pe, n + 1)
                for a in range(QC):
                    m = pe.transpose(ps_t[:, a, :], avs[:, a, :], ident[:, :])
                m.then_inc(s["te"].sem, 1)

            def max_units(n, p, lo, hi):
                for k in range(lo, hi):
                    u = lead + k
                    if u < UN:
                        max_unit(n + 1, 1 - p, u)
                    elif not (type(n) is int and n + 2 >= NCH):
                        if u == UN:
                            pe.wait_ge(s["taev"], 2 * n + 6)
                        max_unit(n + 2, p, u - UN)

            s["av"].open(pe)
            s["te"].open(pe)
            turn_q(0, 0, 0)
            turn_q(0, 0, 1)
            pe.wait_ge(s["taev"], 2)
            for u in range(UN):
                max_unit(0, 0, u)
            turn_m(0, 0, 0)
            turn_m(0, 0, 1)
            turn_q(1, 1, 0)
            turn_q(1, 1, 1)
            pe.wait_ge(s["taev"], 4)
            for u in range(lead):
                max_unit(1, 1, u)

            def body(n, p, first, more):
                more2 = not (type(n) is int and n + 2 >= NCH)
                pe.wait_ge(s["tbev"], 2 * n + 2)
                pe.wait_ge(s["qcopy"], n + 1)
                for h in range(HG):
                    score(n, p, 0, h)
                for t in range(key_tiles):
                    if t == 2 and not first:
                        results(n - 1)
                    if t in TURN and more2:
                        turn_q(n + 2, p, TURN.index(t))
                    if t == key_tiles - 2 and more:
                        turn_m(n + 1, 1 - p, 0)
                    if t == key_tiles - 1 and more:
                        turn_m(n + 1, 1 - p, 1)
                    units = bounds[t + 1] - bounds[t]
                    for h in range(HG):
                        if more:
                            max_units(n, p, bounds[t] + units * h // HG, bounds[t] + units * (h + 1) // HG)
                        if t + 1 < key_tiles:
                            score(n, p, t + 1, h)
                    values(n, p, t)
                if not more:
                    s["norm"].wait(pe, n)
                    results(n)
            pairs(pe, body)

        @block.scalar
        def _(a):
            def ev_q(n, p, half):
                a.wait_ge(s["ta"], 2 * n + half + 1)
                a.copy(qm[p][:, :, 2 * half:2 * half + 2, :],
                       ps_tb[0:MAXROW, :, :].rearrange("p (a h) b -> p h a b", h=HG)).then_inc(s["taev"], 1)

            def ev_m(n, p, half):
                a.wait_ge(s["tb0"] if half == 0 else s["tb"], n + 1)
                a.copy(qt[p][MAXROW:P, :, 2 * half:2 * half + 2, :],
                       ps_tb[MAXROW:P, :, :].rearrange("p (a h) b -> p h a b", h=HG)).then_inc(s["tbev"], 1)

            def body(n, p, first, more):
                more2 = not (type(n) is int and n + 2 >= NCH)
                for t in range(key_tiles):
                    for h in range(HG):
                        a.wait_ge(s["sc"], (n * key_tiles + t) * HG + h + 1)
                        if h == 0:
                            s["av"].wait(a, n * key_tiles + t - 1)
                        a.activation(pbuf[t % 2][:, h, :], ps_s[:, ring_s[t * HG + h][0], :], ACT.Exp)\
                         .then_inc(s["exp"].sem, 1)
                        if more2 and h == 1 and t - 1 in TURN:
                            ev_q(n + 2, p, TURN.index(t - 1))
                        if more and h == 1 and t == key_tiles - 1:
                            ev_m(n + 1, 1 - p, 0)
                if more:
                    ev_m(n + 1, 1 - p, 1)
                s["av"].wait(a, (n + 1) * key_tiles)
                s["te"].wait(a, n)
                a.copy(avs[:, :, :], ps_av[:, :].rearrange("p (a b) -> p a b", b=P)).then_inc(s["avev"].sem, 1)

            s["exp"].open(a)
            s["avev"].open(a)
            ev_q(0, 0, 0)
            ev_q(0, 0, 1)
            ev_m(0, 0, 0)
            ev_m(0, 0, 1)
            ev_q(1, 1, 0)
            ev_q(1, 1, 1)
            pairs(a, body)

        @block.vector
        def _(v):
            def reduce_unit(n, p, u):
                v.wait_ge(s["mx"], n * UN + u + 1)
                v.tensor_reduce(mxp[p][:, u // KB, u % KB:u % KB + 1], ps_m[:, ring_m[(u - lead) % UN][0], 0:widths[u % KB]],
                                AX.X, ALU.max).then_inc(s["mred"].sem, 1)

            def stream(n, p, lo, hi):
                for k in range(lo, hi):
                    u = lead + k
                    if u < UN:
                        reduce_unit(n + 1, 1 - p, u)
                    elif not (type(n) is int and n + 2 >= NCH):
                        reduce_unit(n + 2, p, u - UN)

            def maxima(n, p, between):
                s["mred"].wait(v, n * UN + UN)
                c = Counted(v, s["msplit"], n * MS)
                place = [qnat[p][:, :, :, MAXROW + i] for i in range(3)]
                neg = negm[:, :].rearrange("p (a h) -> p a h", h=HG)
                tmp = mtmp[:, :].rearrange("p (a h) -> p a h", h=HG)
                c(v.tensor_reduce(negm[:, :], mxp[p][:, :, :], AX.X, ALU.max, negate=True))
                between()
                c.wait()
                v.wait_ge(s["qsplit"], n * QS + QS)
                c(v.tensor_copy(place[0], neg))
                between()
                c.wait()
                c(v.tensor_tensor(tmp, neg, place[0], ALU.subtract))
                between()
                c.wait()
                c(v.tensor_copy(place[1], tmp))
                between()
                c.wait()
                c(v.tensor_tensor(place[2], tmp, place[1], ALU.subtract))
                assert c.n == MS, c.n
                c.wait()
                v.wait_ge(s["taev"], 2 * n + 2)
                if not (type(n) is int and n < 2):
                    v.wait_ge(s["sc"], HG * key_tiles * (n - 1))
                v.tensor_copy(qt[p][0:MAXROW, :, :, :], qm[p][:, :, :, :]).then_inc(s["qcopy"], 1)

            def normalise(n):
                s["te"].wait(v, n + 1)
                res = ps_t[:, :, :].rearrange("p a (h d) -> p a h d", d=32)
                v.reciprocal(rc[:, :, :], res[:, :, :, HD]).then_inc(s["rc"], 1)
                v.wait_ge(s["rc"], n + 1)
                v.tensor_tensor(qn[:, at(chunk(n) * QC, QC), at(group(n) * GW, GW)].rearrange("p t (h d) -> p t h d", d=HD),
                                res[:, :, :, 0:HD], rc[:, :, :].unsqueeze(3).to_broadcast([P, QC, HG, HD]),
                                ALU.mult).then_inc(s["norm"].sem, 1)

            def body(n, p, first, more):
                if not more:
                    normalise(n - 1)
                    normalise(n)
                    s["norm"].wait(v, n + 1)
                    return
                early, end = bounds[2], UN - lead
                stream(n, p, 0, early)
                if not first:
                    normalise(n - 1)
                stream(n, p, early, end)
                at_unit = [end]

                def between():
                    if at_unit[0] < UN:
                        stream(n, p, at_unit[0], at_unit[0] + 1)
                        at_unit[0] += 1
                maxima(n + 1, 1 - p, between)
                stream(n, p, at_unit[0], UN)
            s["mred"].open(v)
            s["norm"].open(v)
            for u in range(UN):
                reduce_unit(0, 0, u)
            maxima(0, 0, lambda: None)
            for u in range(lead):
                reduce_unit(1, 1, u)
            pairs(v, body)



def self_qkv(prog, x, mean, rstd, w, gain, shift, qn, kn, v_nat, ident):
    nc = prog["nc"]
    with ExitStack() as cx:
        sums = cx.enter_context(nc.sbuf_tensor("hsum", [P, 2 * H], F32))
        squares = cx.enter_context(nc.sbuf_tensor("hsq", [P, 2 * H, HD], F32))
        var = cx.enter_context(nc.sbuf_tensor("hvar", [P, T, 2 * H], F32))
        sd = cx.enter_context(nc.sbuf_tensor("hsd", [P, T, 2 * H], F32))

        def epilogue(v, prod, n, p, c):
            qk = prod[:, 0, :].rearrange("p (h d) -> p h d", d=HD)
            c(v.tensor_reduce(sums[:, :], qk, AX.X, ALU.add))
            c.wait()
            c(v.tensor_scalar(sums[:, :], sums[:, :], 1.0 / HD, None, ALU.mult))
            c.wait()
            for i, dst in enumerate((qn, kn)):
                c(v.tensor_tensor(dst[:, n, :].rearrange("p (h d) -> p h d", d=HD), qk[:, i * H:i * H + H, :],
                                  sums[:, i * H:i * H + H].unsqueeze(2).to_broadcast([P, H, HD]), ALU.subtract))
            c.wait()
            for i, dst in enumerate((qn, kn)):
                cen = dst[:, n, :].rearrange("p (h d) -> p h d", d=HD)
                c(v.tensor_tensor(squares[:, i * H:i * H + H, :], cen, cen, ALU.mult))
            c.wait()
            c(v.tensor_reduce(sums[:, :], squares[:, :, :], AX.X, ALU.add))
            c.wait()
            c(v.tensor_scalar(var[:, n, :], sums[:, :], 1.0 / HD, EPS_LN, ALU.mult, ALU.add))

        linear(prog, T, ln_rows(x, mean, rstd), w, 3 * D, epilogue, 8, ident,
               side=lambda a, prod, n: a.copy(v_nat[:, n, :], prod[:, 1, 0:D]))

        s_sd, s_r, s_q = (fresh(prog, k) for k in ("head_sd", "head_rstd", "head_chain"))
        with nc.Block() as block:
            @block.scalar
            def _(a):
                a.activation(sd[:, :, :], var[:, :, :], ACT.Sqrt).then_inc(s_sd, 1)

            def apply(eng, c, t, i):
                th = t[:, :, :].rearrange("p t (h d) -> p t h d", d=HD)
                c(eng.tensor_tensor(th, th, var[:, :, i * H:i * H + H].unsqueeze(3).to_broadcast([P, T, H, HD]), ALU.mult))
                c.wait()
                c(eng.tensor_tensor(t[:, :, :], t[:, :, :], gain[:, i, :].unsqueeze(1).to_broadcast([P, T, D]), ALU.mult))
                c.wait()
                c(eng.tensor_tensor(t[:, :, :], t[:, :, :], shift[:, i, :].unsqueeze(1).to_broadcast([P, T, D]), ALU.add))
                c.wait()

            @block.vector
            def _(v):
                c = Counted(v, s_q)
                c(v.tensor_scalar(gain[:, 0, :], gain[:, 0, :], 0.25, None, ALU.mult))
                c(v.tensor_scalar(shift[:, 0, :], shift[:, 0, :], 0.25, None, ALU.mult))
                v.wait_ge(s_sd, 1)
                v.reciprocal(var[:, :, :], sd[:, :, :]).then_inc(s_r, 1)
                v.wait_ge(s_r, 1)
                c.wait()
                apply(v, c, kn, 1)
                apply(v, c, qn, 0)


def cross_q(bias):
    def fill(qn):
        def epilogue(v, prod, n, p, c):
            c(v.tensor_tensor(qn[:, n, :], prod[:, 0, 0:D], bias[:, :], ALU.add))
            c.wait()
            c(v.tensor_scalar(qn[:, n, :], qn[:, n, :], 0.25, None, ALU.mult))
        return epilogue
    return fill


def experts(prog, x, st, mean, rstd, gate, w, iota, ident):
    nc = prog["nc"]
    s_fetch, s_turned = fresh(prog, "mfetch"), fresh(prog, "mturned")
    s_copied, s_gate, s_w = Slots(prog, "mcopied"), Slots(prog, "mgate"), Slots(prog, "mprod", 5)
    s_d, s_e = fresh(prog, "mdiff"), fresh(prog, "mexp")
    s_gc = fresh(prog, "mgchain")
    s_used, s_gused = Slots(prog, "mused", 4), Slots(prog, "mgused", 2)
    s_tick = fresh(prog, "mtick")
    per = 14
    with ExitStack() as cx:
        def sb(name, shape, dt=F32):
            return cx.enter_context(nc.sbuf_tensor(name, shape, dt))
        xn = [sb(f"mxn{p}", [P, D]) for p in range(2)]
        xt = [sb(f"mxt{p}", [P, 2, P]) for p in range(2)]
        lg, m8, i8, pair = sb("mlg", [P, NE]), sb("mm8", [P, 8]), sb("mi8", [P, 8], U32), sb("mpair", [P, 2])
        dif, ex, den, w1, w2 = (sb(k, [P, 1]) for k in ("mdif", "mex", "mden", "mw1", "mw2"))
        wa, wb, we = sb("mwa", [P, NE]), sb("mwb", [P, NE]), sb("mwe", [P, NE])
        turn = [cx.enter_context(nc.psum_tensor(f"mturn{p}", [P, 512], F32)) for p in range(2)]
        pg = [cx.enter_context(nc.psum_tensor(f"mpg{p}", [P, 512], F32)) for p in range(2)]
        prod = cx.enter_context(nc.psum_tensor("mprodp", [P, 4, 512], F32))
        block = cx.enter_context(nc.Block())

        def every(body, eng):
            with eng.Fori(0, T // 2 - 1) as i:
                for p in range(2):
                    body(2 * i + p, p, False)
            body(T - 2, 0, False)
            body(T - 1, 1, True)

        @block.tensor
        def _(pe):
            def turn_tile(n, p):
                pe.wait_ge(s_fetch, n + 1)
                s_copied.wait(pe, n - 1)
                for k in range(2):
                    m = pe.transpose(turn[p][:, k * P:(k + 1) * P], xn[p][:, k * P:(k + 1) * P], ident[:, :])
                m.then_inc(s_turned, 1)

            def multiply(n, p, last):
                if not last:
                    turn_tile(n + 1, 1 - p)
                s_copied.wait(pe, n + 1)
                s_gused.wait(pe, n - 1)
                for k in range(2):
                    m = pe.matmul(pg[p][:, 0:NE], xt[p][:, k, :], gate[:, k, :], start=(k == 0), stop=(k == 1))
                m.then_inc(s_gate.sem, 1)
                for b in range(4):
                    s_used.wait(pe, 4 * n + b - 3)
                    for k in range(2):
                        m = pe.matmul(prod[:, b, :], xt[p][:, k, :], w[:, k, b * 512:b * 512 + 512],
                                      start=(k == 0), stop=(k == 1))
                    m.then_inc(s_w.sem, 1)
            s_gate.open(pe)
            s_w.open(pe)
            turn_tile(0, 0)
            every(multiply, pe)

        @block.scalar
        def _(a):
            def copy(n, p, last):
                s_w.wait(a, 4 * (n - 1))
                a.wait_ge(s_turned, n + 1)
                a.copy(xt[p][:, :, :], turn[p][:, 0:D].rearrange("p (k n) -> p k n", k=2)).then_inc(s_copied.sem, 1)
                a.wait_ge(s_d, n + 1)
                a.activation(ex[:, :], dif[:, :], ACT.Exp).then_inc(s_e, 1)
            s_copied.open(a)
            every(copy, a)

        @block.vector
        def _(v):
            fetch = ln_rows(x, mean, rstd)
            s_used.open(v)
            s_gused.open(v)
            for n in range(2):
                fetch(v, xn[n], n).then_inc(s_fetch, 1)

            def body(n, p, last):
                c = Counted(v, s_gc, n * per)
                s_gate.wait(v, n + 1)
                v.tensor_copy(lg[:, :], pg[p][:, 0:NE]).then_inc(s_gused.sem, 1)
                s_gused.wait(v, n + 1)
                v.sem_inc(s_tick, 1)
                c(v.max(m8[:, :], lg[:, :]))
                c.wait()
                v.sem_inc(s_tick, 1)
                c(v.max_index(i8[:, :], m8[:, :], lg[:, :]))
                v.tensor_tensor(dif[:, :], m8[:, 1:2], m8[:, 0:1], ALU.subtract).then_inc(s_d, 1)
                c.wait()
                c(v.tensor_copy(pair[:, :], i8[:, 0:2]))
                v.wait_ge(s_e, n + 1)
                c(v.tensor_scalar(den[:, :], ex[:, :], 1.0, None, ALU.add))
                c.wait()
                c(v.reciprocal(w1[:, :], den[:, :]))
                c.wait()
                c(v.tensor_tensor(w2[:, :], ex[:, :], w1[:, :], ALU.mult))
                c(v.tensor_scalar(wa[:, :], iota[:, :], pair[:, 0:1], w1[:, :], ALU.is_equal, ALU.mult))
                c.wait()
                c(v.tensor_scalar(wb[:, :], iota[:, :], pair[:, 1:2], w2[:, :], ALU.is_equal, ALU.mult))
                c.wait()
                c(v.tensor_tensor(we[:, :], wa[:, :], wb[:, :], ALU.add))
                c.wait()
                for e in range(NE):
                    if e % 2 == 0:
                        s_w.wait(v, 4 * n + e // 2 + 1)
                    o = v.scalar_tensor_tensor(x[:, n, :], prod[:, e // 2, (e % 2) * D:(e % 2) * D + D], we[:, e:e + 1],
                                               x[:, n, :], ALU.mult, ALU.add)
                    if e % 2:
                        o.then_inc(s_used.sem, 1)
                        s_used.wait(v, 4 * n + e // 2 + 1)
                    else:
                        c(o)
                        c.wait()
                c(v.bn_stats(st[:, n, :], x[:, n, :]))
                assert c.n == per, c.n
                if not (type(n) is int and n + 2 >= T):
                    v.wait_ge(s_turned, n + 1)
                    fetch(v, xn[p], n + 2).then_inc(s_fetch, 1)
            every(body, v)



def focused_qkv(prog, x, mean, rstd, w, qf, kf, vf, ident):
    nc = prog["nc"]
    with ExitStack() as cx:
        sums = cx.enter_context(nc.sbuf_tensor("fsum", [P, 2 * H], F32))
        rs = cx.enter_context(nc.sbuf_tensor("frs", [P, 2 * H], F32))
        a = cx.enter_context(nc.sbuf_tensor("fa", [P, 2 * H, HD], F32))
        b = cx.enter_context(nc.sbuf_tensor("fb", [P, 2 * H, HD], F32))
        spread = lambda t, i, n: t[:, i:i + n].unsqueeze(2).to_broadcast([P, n, HD])

        def epilogue(v, prod, n, p, c):
            qk = prod[:, 0, :].rearrange("p (h d) -> p h d", d=HD)
            c(v.tensor_scalar(a[:, :, :], qk, 0.0, EPS_FOCUS, ALU.max, ALU.add))
            c.wait()
            c(v.tensor_reduce(sums[:, :], a[:, :, :], AX.X, ALU.add))
            c.wait()
            c(v.reciprocal(rs[:, :], sums[:, :]))
            c.wait()
            c(v.tensor_tensor(a[:, :, :], a[:, :, :], spread(rs, 0, 2 * H), ALU.mult))
            c.wait()
            c(v.tensor_tensor(b[:, :, :], a[:, :, :], a[:, :, :], ALU.mult))
            c.wait()
            c(v.tensor_tensor(b[:, :, :], b[:, :, :], a[:, :, :], ALU.mult))
            c.wait()
            c(v.tensor_reduce(sums[:, :], b[:, :, :], AX.X, ALU.add))
            c.wait()
            c(v.reciprocal(rs[:, :], sums[:, :]))
            c.wait()
            for i, dst in enumerate((qf, kf)):
                c(v.tensor_tensor(dst[:, n, :].rearrange("p (h d) -> p h d", d=HD), b[:, i * H:i * H + H, :],
                                  spread(rs, i * H, H), ALU.mult))
        linear(prog, T, ln_rows(x, mean, rstd), w, 3 * D, epilogue, 10, ident,
               side=lambda a, prod, n: a.copy(vf[:, n, :], prod[:, 1, 0:D]))


def linear_attention(prog, qf, kf, vf, yt, tap, tap_bias, mask, ones, ident):
    nc = prog["nc"]
    s = {k: fresh(prog, k) for k in ("kv", "v", "bd", "tr", "ev", "num", "g")}
    with ExitStack() as cx:
        ksum = cx.enter_context(nc.sbuf_tensor("ksum", [P, D], F32))
        prodq = cx.enter_context(nc.sbuf_tensor("prodq", [P, T, H, HD], F32))
        z = cx.enter_context(nc.sbuf_tensor("lz", [P, T, H], F32))
        bd = cx.enter_context(nc.sbuf_tensor("lbd", [P, 2, P], F32))
        qt = cx.enter_context(nc.sbuf_tensor("lqt", [P, 2, 512], F32))
        ot = cx.enter_context(nc.sbuf_tensor("lot", [P, 2, S + 2], F32))
        ps_k = cx.enter_context(nc.psum_tensor("lpsk", [P, 512], F32))
        ps_kv = [cx.enter_context(nc.psum_tensor(f"lpskv{j}", [P, 512], F32)) for j in range(2)]
        ps_t = cx.enter_context(nc.psum_tensor("lpst", [P, 2, 512], F32))
        ps_n = cx.enter_context(nc.psum_tensor("lpsn", [P, 2, 512], F32))
        block = cx.enter_context(nc.Block())

        @block.tensor
        def _(pe):
            for t in range(T):
                pe.matmul(ps_k[:, 0:D], ones[:, :], kf[:, t, :], start=(t == 0), stop=(t == T - 1))
                for j in range(2):
                    m = pe.matmul(ps_kv[j][:, 0:P], kf[:, t, j * P:j * P + P], vf[:, t, j * P:j * P + P],
                                  start=(t == 0), stop=(t == T - 1))
            m.then_inc(s["kv"], 1)
            pe.wait_ge(s["v"], 6)
            for c in range(4):
                if c:
                    pe.wait_ge(s["ev"], c)
                for j in range(2):
                    for t in range(4):
                        m = pe.transpose(ps_t[:, j, t * P:t * P + P], qf[:, 4 * c + t, j * P:j * P + P], ident[:, :])
                m.then_inc(s["tr"], 1)
                pe.wait_ge(s["ev"], c + 1)
                if c:
                    pe.wait_ge(s["g"], 1 + c)
                for j in range(2):
                    m = pe.matmul(ps_n[:, j, :], bd[:, j, :], qt[:, j, :], start=True, stop=True)
                m.then_inc(s["num"], 1)

        @block.scalar
        def _(a):
            for c in range(4):
                a.wait_ge(s["tr"], c + 1)
                if c:
                    a.wait_ge(s["num"], c)
                a.copy(qt[:, :, :], ps_t[:, :, :]).then_inc(s["ev"], 1)

        @block.vector
        def _(v):
            c = Counted(v, s["v"])
            v.memset(ot[:, :, 0:S + 2:S + 1], 0.0).then_inc(s["g"], 1)
            v.wait_ge(s["kv"], 1)
            c(v.tensor_copy(ksum[:, :], ps_k[:, 0:D]))
            for j in range(2):
                v.tensor_tensor(bd[:, j, :], ps_kv[j][:, 0:P], mask[:, :], ALU.mult).then_inc(s["bd"], 1)
            v.wait_ge(s["bd"], 2)
            c.wait()
            q4 = qf[:, :, :].rearrange("p t (h d) -> p t h d", d=HD)
            c(v.tensor_tensor(prodq[:, :, :, :].rearrange("p t h d -> p t (h d)"), qf[:, :, :],
                              ksum[:, :].unsqueeze(1).to_broadcast([P, T, D]), ALU.mult))
            c.wait()
            c(v.tensor_reduce(z[:, :, :], prodq[:, :, :, :], AX.X, ALU.add))
            c.wait()
            c(v.tensor_scalar(z[:, :, :], z[:, :, :], EPS_FOCUS, None, ALU.add))
            c.wait()
            c(v.reciprocal(prodq[:, :, :, 0], z[:, :, :]))
            c.wait()
            c(v.tensor_tensor(q4, q4, prodq[:, :, :, 0].unsqueeze(3).to_broadcast([P, T, H, HD]), ALU.mult))
            for k in range(4):
                v.wait_ge(s["num"], k + 1)
                v.tensor_copy(ot[:, :, 1 + 512 * k:1 + 512 * k + 512], ps_n[:, :, :]).then_inc(s["g"], 1)
            v.wait_ge(s["g"], 5)
            for j in range(2):
                c(v.tensor_scalar(yt[:, j, :], ot[:, j, 1:S + 1], tap[:, j, 1:2], tap_bias[:, j:j + 1], ALU.mult, ALU.add))
            for sh, i in ((0, 0), (2, 2), (1, 3)):
                c.wait()
                for j in range(2):
                    if i == 3:
                        c(v.tensor_tensor(yt[:, j, :], yt[:, j, :], ot[:, j, 1:S + 1], ALU.add))
                    else:
                        c(v.scalar_tensor_tensor(yt[:, j, :], ot[:, j, sh:sh + S], tap[:, j, i:i + 1], yt[:, j, :],
                                                 ALU.mult, ALU.add))
            c.wait()


def cross_keys(prog, ctx_t, wk, bk, keyt):
    nc = prog["nc"]
    s_m, s_c = fresh(prog, "ckm"), fresh(prog, "ckc")
    with ExitStack() as cx:
        ps = cx.enter_context(nc.psum_tensor("ckps", [P, 2, 4, 512], F32))
        block = cx.enter_context(nc.Block())

        @block.tensor
        def _(pe):
            for j in range(2):
                for b in range(4):
                    w = min(512, M - 512 * b)
                    for k in range(2):
                        m = pe.matmul(ps[:, j, b, 0:w], wk[0:CH, k, j * P:j * P + P], ctx_t[:, k, 512 * b:512 * b + w],
                                      start=(k == 0), stop=(k == 1))
                m.then_inc(s_m, 1)

        @block.vector
        def _(v):
            for j in range(2):
                v.wait_ge(s_m, j + 1)
                v.tensor_scalar(keyt[:, j, 0:M], ps[:, j, :, :].rearrange("p b n -> p (b n)")[:, 0:M], bk[:, j:j + 1], None,
                                ALU.add).then_inc(s_c, 1)
            v.wait_ge(s_c, 2)


def cross_one_head(prog, x, st, mean, rstd, wq, bq, keyt, vals, ident):
    nc = prog["nc"]
    s = {k: fresh(prog, k) for k in ("xf", "xtr", "xcp", "qm", "qc", "sc", "mx", "r", "ev")}
    for k in ("ex", "pt", "av", "o"):
        s[k] = Slots(prog, "x" + k, 4 if k == "ev" else 2)
    LAST = M - (TM - 1) * P
    UT = -(-TM // 4)
    with ExitStack() as cx:
        def sb(name, shape, dt=F32):
            return cx.enter_context(nc.sbuf_tensor(name, shape, dt))
        xn, xt, qt = sb("oxn", [P, D]), sb("oxt", [P, 2, P]), [sb(f"oqt{p}", [P, 2, P]) for p in range(2)]
        pn, pt = [sb(f"opn{p}", [P, MP]) for p in range(2)], sb("opt", [P, TM, P])
        nm, sm, rr = [sb(f"onm{p}", [P, 1]) for p in range(2)], [sb(f"osm{p}", [P, 1]) for p in range(2)], sb("orr", [P, 1])
        ps_s = cx.enter_context(nc.psum_tensor("ops_s", [P, 2048], F32))
        ps_x = cx.enter_context(nc.psum_tensor("ops_x", [P, 2, P], F32))
        ps_q = ps_x
        ps_p = cx.enter_context(nc.psum_tensor("ops_p", [P, 2, 4, P], F32))
        ps_o = cx.enter_context(nc.psum_tensor("ops_o", [P, 512], F32))
        block = cx.enter_context(nc.Block())

        def every(body, eng):
            with eng.Fori(0, T // 2 - 1) as i:
                for p in range(2):
                    body(2 * i + p, p, True)
            body(T - 2, 0, True)
            body(T - 1, 1, False)

        @block.tensor
        def _(pe):
            def query(n, p):
                pe.wait_ge(s["xf"], n + 1)
                if not (type(n) is int and n == 0):
                    pe.wait_ge(s["qc"], n)
                for k in range(2):
                    m = pe.transpose(ps_x[:, k, :], xn[:, k * P:k * P + P], ident[:, :])
                m.then_inc(s["xtr"], 1)
                pe.wait_ge(s["xcp"], n + 1)
                for j in range(2):
                    for k in range(2):
                        m = pe.matmul(ps_q[:, j, :], wq[:, k, j * P:j * P + P], xt[:, k, :], start=(k == 0), stop=(k == 1))
                m.then_inc(s["qm"], 1)

            def score(n, p):
                pe.wait_ge(s["qc"], n + 1)
                s["ex"].wait(pe, n)
                for b in range(4):
                    w = min(512, M - 512 * b)
                    for j in range(2):
                        m = pe.matmul(ps_s[:, 512 * b:512 * b + w], qt[p][:, j, :], keyt[:, j, 512 * b:512 * b + w],
                                      start=(j == 0), stop=(j == 1))
                m.then_inc(s["sc"], 1)
            s["av"].open(pe)
            query(0, 0)
            score(0, 0)

            def body(n, p, more):
                if more:
                    query(n + 1, 1 - p)
                s["ex"].wait(pe, n + 1)
                for u in range(UT):
                    s["pt"].wait(pe, n * UT + u - 1)
                    for t in range(4 * u, min(TM, 4 * u + 4)):
                        r = P if t < TM - 1 else LAST
                        m = pe.transpose(ps_p[0:r, u % 2, t % 4, :], pn[p][:, t * P:t * P + r], ident[:, :])
                    m.then_inc(s["ev"], 1)
                if more:
                    score(n + 1, 1 - p)
                s["pt"].wait(pe, n * UT + UT)
                s["o"].wait(pe, n)
                for t in range(TM):
                    r = P if t < TM - 1 else LAST
                    m = pe.matmul(ps_o[:, 0:D], pt[0:r, t, :], vals[0:r, t, :], start=(t == 0), stop=(t == TM - 1))
                m.then_inc(s["av"].sem, 1)
            every(body, pe)

        @block.scalar
        def _(a):
            def query(n, p):
                a.wait_ge(s["xtr"], n + 1)
                a.copy(xt[:, :, :], ps_x[:, :, :]).then_inc(s["xcp"], 1)
            s["ex"].open(a)
            s["pt"].open(a)
            query(0, 0)

            def body(n, p, more):
                a.wait_ge(s["mx"], n + 1)
                a.activation(pn[p][:, 0:M], ps_s[:, 0:M], ACT.Exp, bias=nm[p][:, :], accum_out=sm[p][:, :]).then_inc(s["ex"].sem, 1)
                if more:
                    query(n + 1, 1 - p)
                for u in range(UT):
                    a.wait_ge(s["ev"], n * UT + u + 1)
                    s["av"].wait(a, n)
                    lo, hi = 4 * u, min(TM, 4 * u + 4)
                    r = P if hi < TM else LAST
                    a.copy(pt[0:r, lo:hi, :], ps_p[0:r, u % 2, 0:hi - lo, :]).then_inc(s["pt"].sem, 1)
            every(body, a)

        @block.vector
        def _(v):
            fetch = ln_rows(x, mean, rstd)

            def query(n, p):
                v.wait_ge(s["qm"], n + 1)
                for j in range(2):
                    o = v.tensor_scalar(qt[p][:, j, :], ps_q[:, j, :], bq[:, j:j + 1], 1.0 / 16.0, ALU.add, ALU.mult)
                o.then_inc(s["qc"], 1)
            s["o"].open(v)
            fetch(v, xn, 0).then_inc(s["xf"], 1)
            query(0, 0)

            def body(n, p, more):
                v.wait_ge(s["sc"], n + 1)
                v.tensor_reduce(nm[p][:, :], ps_s[:, 0:M], AX.X, ALU.max, negate=True).then_inc(s["mx"], 1)
                if more:
                    v.wait_ge(s["xtr"], n + 1)
                    fetch(v, xn, n + 1).then_inc(s["xf"], 1)
                    query(n + 1, 1 - p)
                s["ex"].wait(v, n + 1)
                v.reciprocal(rr[:, :], sm[p][:, :]).then_inc(s["r"], 1)
                v.wait_ge(s["r"], 2 * n + 1)
                s["av"].wait(v, n + 1)
                v.scalar_tensor_tensor(x[:, n, :], ps_o[:, 0:D], rr[:, :], x[:, n, :], ALU.mult, ALU.add).then_inc(s["o"].sem, 1)
                s["o"].wait(v, n + 1)
                v.bn_stats(st[:, n, :], x[:, n, :]).then_inc(s["r"], 1)
                v.wait_ge(s["r"], 2 * n + 2)
            every(body, v)


def quantise(prog, items, ident):
    nc = prog["nc"]
    s_v, s_g = fresh(prog, "qv"), fresh(prog, "qg")
    with ExitStack() as cx:
        am = cx.enter_context(nc.sbuf_tensor("qam", [P, len(items)], F32))
        al = cx.enter_context(nc.sbuf_tensor("qal", [P, len(items)], F32))
        block = cx.enter_context(nc.Block())

        @block.vector
        def _(v):
            c = Counted(v, s_v)
            for i, (src, work, magic, scale, inv) in enumerate(items):
                c(v.tensor_reduce(am[:, i:i + 1], src, AX.X, ALU.max, apply_absolute_value=True))
            v.wait_ge(s_g, 1)
            for i, (src, work, magic, scale, inv) in enumerate(items):
                c(v.tensor_scalar(scale, al[:, i:i + 1], 1e-12, None, ALU.max))
                c.wait()
                c(v.reciprocal(inv, scale))
                c.wait()
                c(v.tensor_scalar(scale, inv, FP8_MAX, FP8_MAX, ALU.mult, ALU.min))
                c.wait()
                c(v.reciprocal(inv, scale))
                c(v.tensor_scalar(src, src, scale, FP8_MAX, ALU.mult, ALU.min))
                c.wait()
                c(v.tensor_scalar(src, src, -FP8_MAX, None, ALU.max))
                c.wait()
                c(v.tensor_scalar(magic.bitcast(I32), src.bitcast(I32), 0x7F800000, None, ALU.bitwise_and))
                c.wait()
                c(v.tensor_scalar(magic, magic, 2.0 ** -6, 1.5 * 2.0 ** 20, ALU.max, ALU.mult))
                c.wait()
                c(v.tensor_tensor(src, src, magic, ALU.add))
                c.wait()
                c(v.tensor_tensor(src, src, magic, ALU.subtract))
                c.wait()

        @block.gpsimd
        def _(g):
            g.wait_ge(s_v, len(items))
            g.partition_all_reduce(al[:, :], am[:, :], P, bass.bass_isa.ReduceOp.max).then_inc(s_g, 1)



def decoder(nc, a, out, upto=99):
    with ExitStack() as ctx:
        prog = {"nc": nc, "used": []}

        def sb(cx, name, shape, dt=F32):
            return cx.enter_context(nc.sbuf_tensor(name, shape, dt))
        x = sb(ctx, "x_res", [P, T, D])
        st, tmp = sb(ctx, "stats", [P, T, 6]), sb(ctx, "ln_tmp", [P, 2, T])
        mean, rstd = sb(ctx, "ln_mean", [P, T]), sb(ctx, "ln_rstd", [P, T])
        ident, identb = sb(ctx, "ident", [P, P]), sb(ctx, "identb", [P, P], BF16)
        ones = sb(ctx, "ones", [P, P])
        s0 = fresh(prog, "start")
        x_rows = a["x"].rearrange("(t p) d -> p t d", p=P)
        load(prog, [(x[:, :, :], x_rows), (ident[:, :], a["ident"]), (ones[:, :], a["ones"])])
        with nc.Block() as block:
            @block.vector
            def _(v):
                v.tensor_copy(identb[:, :], ident[:, :]).then_inc(s0, 1)
                for t in range(T):
                    v.bn_stats(st[:, t, :], x[:, t, :]).then_inc(s0, 1)
                v.wait_ge(s0, T + 1)

        def layer_norm():
            ln_finish(prog, st, mean, rstd, tmp)

        def done():
            load(prog, [(out.rearrange("(t p) d -> p t d", p=P), x[:, :, :])])

        with ExitStack() as l0:
            qn, v_nat = sb(l0, "q_rows", [P, T, D]), sb(l0, "v_rows", [P, T, D])
            with ExitStack() as cs:
                kt = sb(cs, "k_stack", [P, H, S], BF16)
                with ExitStack() as cx:
                    kn = sb(cx, "k_rows", [P, T, D])
                    w = sb(cx, "w_qkv", [P, 2, 3 * D])
                    gain, shift = sb(cx, "gain", [P, 2, D]), sb(cx, "shift", [P, 2, D])
                    load(prog, [(w[:, :, :], rows2(a["w0_qkv"])), (gain[:, :, :], a["gain"]), (shift[:, :, :], a["shift"])])
                    layer_norm()
                    self_qkv(prog, x, mean, rstd, w, gain, shift, qn, kn, v_nat, ident)
                    build_kt(prog, kn, T, kt, identb)
                attention(prog, qn, v_nat, T, kt, ones, ident, identb)
            with ExitStack() as cx:
                w = sb(cx, "w_proj", [P, 2, D])
                load(prog, [(w[:, :, :], rows2(a["w0_proj"]))])
                linear(prog, T, plain_rows(qn), w, D, residual(x, st), 2, ident)
            if upto <= 1:
                return done()
            recycle(prog)
            layer_norm()
            with ExitStack() as cs:
                kt = sb(cs, "k_stack2", [P, H, MP], BF16)
                valid = sb(cs, "valid", [P, TM])
                with ExitStack() as cx:
                    kn = sb(cx, "k_rows2", [P, TM, D])
                    wq, bq = sb(cx, "w_xq", [P, 2, D]), sb(cx, "b_xq", [P, D])
                    wkv, bkv = sb(cx, "w_xkv", [CH, 2, 2 * D]), sb(cx, "b_xkv", [P, 2 * D])
                    ctx_t = sb(cx, "ctx_t", [CH, 2, MP])
                    load(prog, [(wq[:, :, :], rows2(a["w0_xq"])), (bq[:, :], a["b0_xq"]), (wkv[:, :, :], rows2(a["w0_xkv"])),
                                (bkv[:, :], a["b0_xkv"]), (ctx_t[:, :, :], rows2(a["ctx_t"])), (valid[:, :], a["valid"])])
                    linear(prog, T, ln_rows(x, mean, rstd), wq, D, cross_q(bq)(qn), 2, ident)

                    def keys_values(v, prod, n, p, c):
                        c(v.tensor_tensor(kn[:, n, :], prod[:, 0, 0:D], bkv[:, 0:D], ALU.add))
                        c(v.tensor_tensor(v_nat[:, n, :], prod[:, 0, D:2 * D], bkv[:, D:2 * D], ALU.add))
                        c.wait()
                        c(v.tensor_scalar(v_nat[:, n, :], v_nat[:, n, :], valid[:, at(n)], None, ALU.mult))
                    linear(prog, TM, None, wkv, 2 * D, keys_values, 3, rows=CH, direct=lambda n: ctx_t[:, :, at(n * P, P)])
                    build_kt(prog, kn, TM, kt, identb)
                attention(prog, qn, v_nat, TM, kt, valid, ident, identb)
            with ExitStack() as cx:
                w, b = sb(cx, "w_xo", [P, 2, D]), sb(cx, "b_xo", [P, D])
                load(prog, [(w[:, :, :], rows2(a["w0_xo"])), (b[:, :], a["b0_xo"])])
                linear(prog, T, plain_rows(qn), w, D, residual(x, st, b), 3, ident)
        if upto <= 2:
            return done()
        layer_norm()
        with ExitStack() as cx:
            gate, w, iota = sb(cx, "w_gate", [P, 2, NE]), sb(cx, "w_experts", [P, 2, NE * D]), sb(cx, "iota8", [P, NE])
            load(prog, [(gate[:, :, :], rows2(a["w0_gate"])), (w[:, :, :], rows2(a["w0_experts"])), (iota[:, :], a["iota"])])
            experts(prog, x, st, mean, rstd, gate, w, iota, ident)
        if upto <= 3:
            return done()
        recycle(prog)
        layer_norm()
        with ExitStack() as cx:
            yt = sb(cx, "conv_out", [P, 2, S])
            with ExitStack() as cy:
                qf, kf, vf = (sb(cy, k, [P, T, D]) for k in ("q_focus", "k_focus", "v_focus"))
                w, mask = sb(cy, "w1_qkv", [P, 2, 3 * D]), sb(cy, "head_mask", [P, P])
                tap, tap_bias = sb(cy, "taps", [P, 2, 3]), sb(cy, "tap_bias", [P, 2])
                load(prog, [(w[:, :, :], rows2(a["w1_qkv"])), (mask[:, :], a["mask"]), (tap[:, :, :], rows2(a["taps"])),
                            (tap_bias[:, :], a["tap_bias"])])
                focused_qkv(prog, x, mean, rstd, w, qf, kf, vf, ident)
                linear_attention(prog, qf, kf, vf, yt, tap, tap_bias, mask, ones, ident)
            w, b = sb(cx, "w1_proj", [P, 2, D]), sb(cx, "b1_proj", [P, D])
            load(prog, [(w[:, :, :], rows2(a["w1_proj"])), (b[:, :], a["b1_proj"])])
            linear(prog, T, None, w, D, residual(x, st, b), 3, direct=lambda n: yt[:, :, at(n * P, P)])
        if upto <= 4:
            return done()
        layer_norm()
        with ExitStack() as cx:
            keyt, vals = sb(cx, "key_t", [P, 2, MP]), sb(cx, "values1", [P, TM, D])
            wq, bq = sb(cx, "w1_xq", [P, 2, D]), sb(cx, "b1_xq", [P, 2])
            with ExitStack() as cy:
                ctx_t = sb(cy, "ctx_t1", [CH, 2, MP])
                wk, wv = sb(cy, "w1_xk", [CH, 2, D]), sb(cy, "w1_xv", [CH, 2, D])
                bk, bv = sb(cy, "b1_xk", [P, 2]), sb(cy, "b1_xv", [P, D])
                load(prog, [(ctx_t[:, :, :], rows2(a["ctx_t"])), (wk[:, :, :], rows2(a["w1_xk"])), (wv[:, :, :], rows2(a["w1_xv"])),
                            (bk[:, :], a["b1_xk"]), (bv[:, :], a["b1_xv"]), (wq[:, :, :], rows2(a["w1_xq"])), (bq[:, :], a["b1_xq"])])
                cross_keys(prog, ctx_t, wk, bk, keyt)

                def value_rows(v, prod, n, p, c):
                    c(v.tensor_tensor(vals[:, n, :], prod[:, 0, 0:D], bv[:, :], ALU.add))
                linear(prog, TM, None, wv, D, value_rows, 1, rows=CH, direct=lambda n: ctx_t[:, :, at(n * P, P)])
            cross_one_head(prog, x, st, mean, rstd, wq, bq, keyt, vals, ident)
        if upto <= 5:
            return done()
        layer_norm()
        with ExitStack() as cx:
            xq, work = sb(cx, "x_q", [P, T, D]), sb(cx, "q_magic", [P, T, D])
            w, wm, b = sb(cx, "w1_ffn", [P, 2, D]), sb(cx, "w_magic", [P, 2, D]), sb(cx, "b1_ffn", [P, D])
            sc = sb(cx, "q_scales", [P, 5])
            load(prog, [(w[:, :, :], rows2(a["w1_ffn"])), (b[:, :], a["b1_ffn"])])
            s_n = fresh(prog, "xn_all")
            with nc.Block() as block:
                @block.vector
                def _(v):
                    c = Counted(v, s_n)
                    c(v.tensor_tensor(xq[:, :, :], x[:, :, :], mean[:, :].unsqueeze(2).to_broadcast([P, T, D]), ALU.subtract))
                    c.wait()
                    c(v.tensor_tensor(xq[:, :, :], xq[:, :, :], rstd[:, :].unsqueeze(2).to_broadcast([P, T, D]), ALU.mult))
                    c.wait()
            flat = lambda t: t[:, :, :].rearrange("p a b -> p (a b)")
            quantise(prog, [(flat(xq), None, flat(work), sc[:, 0:1], sc[:, 1:2]),
                            (flat(w), None, flat(wm), sc[:, 2:3], sc[:, 3:4])], ident)
            s_s = fresh(prog, "scale_xw")
            with nc.Block() as block:
                @block.vector
                def _(v):
                    v.tensor_tensor(sc[:, 4:5], sc[:, 1:2], sc[:, 3:4], ALU.mult).then_inc(s_s, 1)
                    v.wait_ge(s_s, 1)
            half = [sb(cx, f"y_half{p}", [P, D], BF16) for p in range(2)]

            def finish(v, prod, n, p, c):
                c(v.scalar_tensor_tensor(half[p][:, :], prod[:, 0, 0:D], sc[:, 4:5], b[:, :], ALU.mult, ALU.add))
                c.wait()
                c(v.tensor_tensor(x[:, n, :], x[:, n, :], half[p][:, :], ALU.add))
            linear(prog, T, plain_rows(xq), w, D, finish, 2, ident)
        done()


def kernel(**inputs):
    import numpy as _np
    import concourse.bacc as _bacc
    from concourse.bass_utils import run_bass_kernel_spmd as _run

    i = {k: _np.asarray(v) for k, v in inputs.items()}
    wide = lambda v: _np.broadcast_to(v, (P, v.size))
    cols = lambda v: v.reshape(2, P).T
    kv = i["L0_xattn_Wkv"].reshape(H, 2, HD, C).transpose(1, 0, 2, 3).reshape(2 * D, C)
    bkv = i["L0_xattn_bkv"].reshape(H, 2, HD).transpose(1, 0, 2).reshape(2 * D)
    ctx = i["ctx_768"][0]
    ctx = _np.concatenate([ctx, _np.broadcast_to(ctx[-1:], (MP - M, C))])
    arrays = {
        "x": i["x"][0],
        "ctx_t": ctx.T,
        "ident": _np.eye(P, dtype=_np.float32),
        "ones": _np.ones((P, P), _np.float32),
        "valid": (_np.arange(MP).reshape(TM, P).T < M).astype(_np.float32),
        "mask": _np.kron(_np.eye(P // HD), _np.ones((HD, HD))).astype(_np.float32),
        "iota": wide(_np.arange(NE, dtype=_np.float32)),
        "w0_qkv": i["L0_attn_w_qkv"],
        "gain": _np.stack([wide(_np.tile(i[f"L0_attn_{k}_gamma"], H)) for k in "qk"], 1),
        "shift": _np.stack([wide(_np.tile(i[f"L0_attn_{k}_beta"], H)) for k in "qk"], 1),
        "w0_proj": i["L0_attn_w_proj"],
        "w0_xq": i["L0_xattn_Wq"].T, "b0_xq": wide(i["L0_xattn_bq"]),
        "w0_xkv": kv.T, "b0_xkv": wide(bkv),
        "w0_xo": i["L0_xattn_Wo"].T, "b0_xo": wide(i["L0_xattn_bo"]),
        "w0_gate": i["L0_ffn_gate_w"].T,
        "w0_experts": i["L0_ffn_weight"].transpose(1, 0, 2).reshape(D, NE * D),
        "w1_qkv": i["L1_attn_w_qkv"].T,
        "w1_proj": i["L1_attn_w_proj"].T, "b1_proj": wide(i["L1_attn_b_proj"]),
        "taps": i["L1_attn_w_dwc"], "tap_bias": cols(i["L1_attn_b_dwc"]),
        "w1_xq": i["L1_xattn_Wq"], "b1_xq": cols(i["L1_xattn_bq"]),
        "w1_xk": i["L1_xattn_Wk"], "b1_xk": cols(i["L1_xattn_bk"]),
        "w1_xv": i["L1_xattn_Wv"], "b1_xv": wide(i["L1_xattn_bv"]),
        "w1_ffn": i["L1_ffn_weight"].T, "b1_ffn": wide(i["L1_ffn_bias"]),
    }
    arrays = {"in_" + k: _np.ascontiguousarray(v) for k, v in arrays.items()}
    nc = _bacc.Bacc("TRN2", target_bir_lowering=False, num_devices=1)
    args = {k[3:]: nc.dram_tensor(k, v.shape, F32, kind="ExternalInput").ap() for k, v in arrays.items()}
    out = nc.dram_tensor("out", (S, D), F32, kind="ExternalOutput").ap()
    decoder(nc, args, out)
    r = _run(nc, [arrays], core_ids=[0])
    return r.results[0]["out"].reshape(1, S, D)
```

```python
from contextlib import ExitStack

import concourse.bass as bass
from concourse import mybir

F32 = mybir.dt.float32
BF16 = mybir.dt.bfloat16
I32 = mybir.dt.int32
U32 = mybir.dt.uint32
ACT = mybir.ActivationFunctionType
ALU = mybir.AluOpType
AX = mybir.AxisListType

P = 128
D = 256
H = 16
HD = D // H
S = 2048
T = S // P
C = 192
CH = C // 2
M = 1601
TM = -(-M // P)
MP = TM * P
NE = 8
HG = 4
QC = 4
TAIL = 4
GW = HG * HD
UNROLL = 4
AHEAD = 3
BANKS_S = 3
BANKS_M = 3
LIGHT_STEP = 2
SHARE_LIGHT = 0.6
MAXROW = 96
EPS_LN = 1e-5
EPS_FOCUS = 1e-6
FP8_MAX = 448.0


class Counted:

    def __init__(self, eng, sem, base=0, fixed=None):
        self.eng, self.sem, self.base, self.n, self.fixed = eng, sem, base, 0, fixed

    def __call__(self, ins):
        self.n += 1
        ins.then_inc(self.sem, 1)
        return ins

    def wait(self):
        self.eng.wait_ge(self.sem, self.base + self.n)
        if self.fixed is not None:
            self.eng.sem_inc(self.fixed, 1)


def at(t, width=1):
    return bass.ds(t, width)


def fresh(prog, name):
    prog["n"] = prog.get("n", 0) + 1
    sem = prog["nc"].alloc_semaphore(f"{name}_{prog['n']}")
    prog["used"].append(sem)
    return sem


def recycle(prog):
    prog["nc"].clear_and_free_semaphores(prog["used"])
    prog["nc"].all_engine_barrier()
    prog["used"] = []


class Slots:

    def __init__(self, prog, name, ahead=2):
        self.sem, self.ahead = fresh(prog, name), ahead

    def open(self, eng):
        eng.sem_inc(self.sem, self.ahead)

    def wait(self, eng, value):
        eng.wait_ge(self.sem, value + self.ahead)



def ln_finish(prog, st, mean, rstd, tmp, extra=None):
    nc = prog["nc"]
    s_v, s_q = fresh(prog, "lnf_v"), fresh(prog, "lnf_sqrt")
    with nc.Block() as block:
        @block.vector
        def _(v):
            c = Counted(v, s_v)
            c(v.tensor_tensor(mean[:, :], st[:, :, 1], st[:, :, 4], ALU.add))
            c(v.tensor_tensor(tmp[:, 0, :], st[:, :, 1], st[:, :, 4], ALU.subtract))
            c(v.tensor_tensor(tmp[:, 1, :], st[:, :, 2], st[:, :, 5], ALU.add))
            c.wait()
            c(v.tensor_scalar(mean[:, :], mean[:, :], 0.5, None, ALU.mult))
            c(v.tensor_tensor(tmp[:, 0, :], tmp[:, 0, :], tmp[:, 0, :], ALU.mult))
            c(v.tensor_scalar(tmp[:, 1, :], tmp[:, 1, :], 1.0 / D, EPS_LN, ALU.mult, ALU.add))
            c.wait()
            c(v.scalar_tensor_tensor(tmp[:, 1, :], tmp[:, 0, :], 0.25, tmp[:, 1, :], ALU.mult, ALU.add))
            v.wait_ge(s_q, 1)
            c(v.reciprocal(rstd[:, :], tmp[:, 0, :]))
            if extra is not None:
                c(extra(v))
            c.wait()

        @block.scalar
        def _(a):
            a.wait_ge(s_v, 7)
            a.activation(tmp[:, 0, :], tmp[:, 1, :], ACT.Sqrt).then_inc(s_q, 1)
            a.wait_ge(s_q, 1)



def linear(prog, tiles, fetch, w, n_cols, epilogue, per, ident=None, rows=P, direct=None, side=None, late=None,
           early=None, beside=None, second=None, side_end=None):
    nc = prog["nc"]
    s_fetch, s_turned, s_copied = fresh(prog, "fetch"), fresh(prog, "turned"), Slots(prog, "copied")
    s_prod, s_chain, s_side = Slots(prog, "prod"), Slots(prog, "epilogue", per + 1), Slots(prog, "side")
    s_tick = fresh(prog, "linear_tick")
    banks = -(-n_cols // 512)
    rounds = (tiles - 1) // UNROLL
    with ExitStack() as cx:
        xn = [cx.enter_context(nc.sbuf_tensor(f"xn{prog['n']}_{p}", [P, D], F32)) for p in range(UNROLL)]
        xt = [cx.enter_context(nc.sbuf_tensor(f"xt{prog['n']}_{p}", [P, 2, P], F32)) for p in range(2)]
        turn = [cx.enter_context(nc.psum_tensor(f"turn{prog['n']}_{p}", [P, 2, 256], F32)) for p in range(2)]
        prod = [cx.enter_context(nc.psum_tensor(f"prod{prog['n']}_{p}", [P, banks, 512], F32)) for p in range(2)]

        def every(body, eng, peel=False):
            if peel:
                for n in range(UNROLL):
                    body(n, n, False)
            with eng.Fori(1 if peel else 0, rounds) as i:
                for r in range(UNROLL):
                    body(UNROLL * i + r, r, False)
            for n in range(UNROLL * rounds, tiles):
                body(n, n % UNROLL, n == tiles - 1)

        block = cx.enter_context(nc.Block())

        @block.tensor
        def _(pe):
            def turn_tile(n, r):
                pe.wait_ge(s_fetch, n + 1)
                s_copied.wait(pe, n - 1)
                for k in range(2):
                    m = pe.transpose(turn[r % 2][:, 0, k * P:(k + 1) * P], xn[r][:, k * P:(k + 1) * P], ident[:, :])
                m.then_inc(s_turned, 1)

            def multiply(n, r, last):
                p = r % 2
                if direct is None and not last:
                    turn_tile(n + 1, (r + 1) % UNROLL)
                s_copied.wait(pe, n + 1)
                if side is not None:
                    s_side.wait(pe, n - 1)
                s_chain.wait(pe, (n - 1) * per)
                for b in range(banks):
                    lo, hi = b * 512, min(n_cols, b * 512 + 512)
                    for k in range(2):
                        m = pe.matmul(prod[p][:, b, 0:hi - lo], xt[p][0:rows, k, :], w[0:rows, k, lo:hi],
                                      start=(k == 0), stop=(k == 1))
                m.then_inc(s_prod.sem, 1)
                if beside is not None and not (type(n) is int and n < beside[1]):
                    beside[0](pe, n - beside[1], (r - beside[1]) % UNROLL)

            s_prod.open(pe)
            if direct is None:
                turn_tile(0, 0)
            every(multiply, pe, peel=beside is not None)
            if beside is not None:
                for n in range(tiles - beside[1], tiles):
                    beside[0](pe, n, n % UNROLL)

        @block.scalar
        def _(a):
            def copy(n, p, last):
                s_prod.wait(a, n - 1)
                if direct is None:
                    a.wait_ge(s_turned, n + 1)
                    a.copy(xt[p][:, :, :], turn[p][:, 0, :].rearrange("p (k n) -> p k n", k=2)).then_inc(s_copied.sem, 1)
                else:
                    a.copy(xt[p][0:rows, :, :], direct(n)).then_inc(s_copied.sem, 1)

            def copy_ahead(n, r, last):
                p = r % 2
                if not last:
                    copy(n + 1, 1 - p, last)
                if side is not None:
                    s_prod.wait(a, n + 1)
                    side(a, prod[p], n, r, s_side.sem)
            s_copied.open(a)
            s_side.open(a)
            copy(0, 0, False)
            every(copy_ahead, a, peel=side_end is not None)
            if side_end is not None:
                side_end(a)

        @block.vector
        def _(v):
            s_chain.open(v)
            if direct is None:
                for n in range(AHEAD):
                    fetch(v, xn[n], n).then_inc(s_fetch, 1)

            def finish(n, r, last):
                p = r % 2
                if direct is None and not (type(n) is int and n + AHEAD >= tiles):
                    v.wait_ge(s_turned, n + 1)
                    fetch(v, xn[(r + AHEAD) % UNROLL], n + AHEAD).then_inc(s_fetch, 1)
                s_prod.wait(v, n + 1)
                c = Counted(v, s_chain.sem, n * per + s_chain.ahead)
                epilogue(v, prod[p], n, r, c)
                assert c.n == per, c.n
                c.wait()
                if second is not None and not (type(n) is int and n == 0):
                    second(v, n - 1, (r - 1) % UNROLL)
            every(finish, v, peel=second is not None)
            if second is not None:
                second(v, tiles - 1, (tiles - 1) % UNROLL)

        if early is not None:
            @block.gpsimd
            def _(g):
                every(lambda n, r, last: early(g, n), g)

        if late is not None:
            @block.gpsimd
            def _(g):
                def go_on(n, r, last):
                    if second is None:
                        s_chain.wait(g, (n + 1) * per)
                        g.sem_inc(s_tick, 1)
                    late(g, n, r)
                every(go_on, g)


def ln_rows(x, mean, rstd):
    return lambda v, out, n: v.tensor_scalar(out[:, :], x[:, n, :], mean[:, at(n)], rstd[:, at(n)],
                                             ALU.subtract, ALU.mult)


def plain_rows(src):
    return lambda v, out, n: v.tensor_copy(out[:, :], src[:, n, :])


def residual(x, st, s_biased=None):
    def run(v, prod, n, r, c):
        if s_biased is not None:
            v.wait_ge(s_biased, n + 1)
        c(v.tensor_tensor(x[:, n, :], prod[:, 0, 0:D], x[:, n, :], ALU.add))
        c.wait()
        c(v.bn_stats(st[:, n, :], x[:, n, :]))
    return run


def biased_residual(prog, x, st, bias):
    s_biased = fresh(prog, "biased")
    return residual(x, st, s_biased), lambda g, n: g.tensor_tensor(x[:, n, :], x[:, n, :], bias[:, :], ALU.add).then_inc(s_biased, 1)



def begin_load(prog, pairs):
    s = prog["nc"].alloc_semaphore(f"ahead_{prog['n']}_{len(pairs)}")
    with prog["nc"].Block() as block:
        @block.sync
        def _(e):
            for dst, src in pairs:
                e.dma_start(dst, src).then_inc(s, 16)
    return s, 16 * len(pairs)


def end_load(prog, load):
    with prog["nc"].Block() as block:
        @block.sync
        def _(e):
            e.wait_ge(load[0], load[1])


def rows2(w):
    return w.rearrange("(k p) n -> p k n", k=2)



def parts(stack, which):
    order = "hhmmlh" if which == "q" else "hmhmhl"
    out = {"h": [], "m": [], "l": []}
    for slot, part in enumerate(order):
        out[part].append(stack[..., slot * HD:(slot + 1) * HD])
    return out["h"], out["m"], out["l"]


def build_kt(prog, kn, tiles, kt, identb):
    nc = prog["nc"]
    s_set, s_rest = fresh(prog, "ks_set"), fresh(prog, "ks_rest")
    s_hi, s_lo, s_turn, s_out, s_out2 = (Slots(prog, n, UNROLL) for n in ("ks_hi", "ks_lo", "ks_turn", "ks_dve", "ks_act"))
    with ExitStack() as cx:
        nat = cx.enter_context(nc.sbuf_tensor(f"knat{prog['n']}", [P, UNROLL, H, P], BF16))
        rest = [cx.enter_context(nc.sbuf_tensor(f"krest{prog['n']}_{p}", [P, H, HD], F32)) for p in range(2)]
        ps = cx.enter_context(nc.psum_tensor(f"kps{prog['n']}", [P, 4, 8, P], BF16))
        block = cx.enter_context(nc.Block())

        def slots(r, first, count):
            return nat[:, r, :, first * HD:(first + 2 * count) * HD].rearrange("p h (s d) -> p h s d", d=2 * HD)[:, :, :, 0:HD]

        @block.gpsimd
        def _(g):
            g.memset(nat[:, :, :, MAXROW:P], 0.0).then_inc(s_set, 1)
            g.wait_ge(s_set, 1)
            g.memset(nat[:, :, :, MAXROW:MAXROW + 3], 1.0).then_inc(s_set, 1)

        def has(n):
            return not (type(n) is int and n >= tiles)

        def every(eng, body, split):
            rounds = (tiles - 2) // UNROLL
            if split is not None:
                split(0, 0)
                split(1, 1)

            def step(n, r):
                if split is not None and has(n + 2):
                    split(n + 2, (r + 2) % UNROLL)
                body(n, r)
            with eng.Fori(0, rounds) as i:
                for r in range(UNROLL):
                    step(UNROLL * i + r, r)
            for n in range(UNROLL * rounds, tiles):
                step(n, n % UNROLL)

        @block.scalar
        def _(a):
            def split(n, r):
                s_turn.wait(a, n + 1 - UNROLL)
                src = kn[:, n, :].rearrange("p (h d) -> p h d", d=HD)
                a.copy(slots(r, 0, 3), src.unsqueeze(2).to_broadcast([P, H, 3, HD])).then_inc(s_hi.sem, 1)

            def out(n, r):
                s_turn.wait(a, n + 1)
                a.copy(kt[:, 8:16, at(n * P, P)], ps[:, 2 * (r % 2) + 1, :, :]).then_inc(s_out2.sem, 1)
            s_hi.open(a)
            s_out2.open(a)
            every(a, out, split)

        @block.vector
        def _(v):
            def split(n, r):
                s_turn.wait(v, n + 1 - UNROLL)
                s_hi.wait(v, n + 1)
                left = rest[r % 2][:, :, :]
                src = kn[:, n, :].rearrange("p (h d) -> p h d", d=HD)
                v.tensor_tensor(left, src, nat[:, r, :, 0:HD], ALU.subtract).then_inc(s_rest, 1)
                v.wait_ge(s_rest, 2 * n + 1)
                v.tensor_copy(slots(r, 1, 2), left.unsqueeze(2).to_broadcast([P, H, 2, HD])).then_inc(s_rest, 1)
                v.wait_ge(s_rest, 2 * n + 2)
                v.tensor_tensor(nat[:, r, :, 5 * HD:6 * HD], left, nat[:, r, :, HD:2 * HD], ALU.subtract)\
                 .then_inc(s_lo.sem, 1)

            def out(n, r):
                s_turn.wait(v, n + 1)
                v.tensor_copy(kt[:, 0:8, at(n * P, P)], ps[:, 2 * (r % 2), :, :]).then_inc(s_out.sem, 1)
            s_lo.open(v)
            s_out.open(v)
            every(v, out, split)

        @block.tensor
        def _(pe):
            def turn(n, r):
                s_lo.wait(pe, n + 1)
                s_out.wait(pe, n - 1)
                s_out2.wait(pe, n - 1)
                for h in range(H):
                    m = pe.transpose(ps[:, 2 * (r % 2) + h // 8, h % 8, :], nat[:, r, h, :], identb[:, :])
                m.then_inc(s_turn.sem, 1)
            s_turn.open(pe)
            pe.wait_ge(s_set, 2)
            every(pe, turn, None)


def ring(count, banks):
    use = [k % banks for k in range(count)]
    return [(use[k], next(b for b in range(1, count) if use[(k - b) % count] == use[k])) for k in range(count)]


def attention(prog, qn, v_nat, key_tiles, kt, valid, ident, identb):
    nc = prog["nc"]
    NU = QC * HG
    FULL, REST = divmod(key_tiles * P, 512)
    KB = FULL + (REST > 0)
    assert REST * HG <= 512
    UA = HG * FULL + (REST > 0)
    UN = QC * UA
    NCH = T // QC * H // HG
    s = {k: fresh(prog, k) for k in ("set", "qsplit", "ta", "taev", "mx", "msplit", "tb", "tbev",
                                     "sc", "rc", "vst", "qcopy")}
    s["tb0"], s["qset"] = fresh(prog, "tb0"), fresh(prog, "qset")
    s["tick"] = fresh(prog, "tick")
    for k in ("mred", "exp", "norm", "av", "avev", "te"):
        s[k] = Slots(prog, k, BANKS_M)
    QS, MS = 8, 5
    with ExitStack() as cx:
        def sb(name, shape, dt):
            return cx.enter_context(nc.sbuf_tensor(f"{name}_{prog['n']}", shape, dt))
        qnat = [sb(f"qnat{p}", [P, QC, HG, P], BF16) for p in range(2)]
        qtmp = sb("qtmp", [P, QC, HG, HD], F32)
        qm = [sb(f"qm{p}", [MAXROW, HG, QC, P], BF16) for p in range(2)]
        qt = [sb(f"qt{p}", [P, HG, QC, P], BF16) for p in range(2)]
        vst = [sb(f"vst{p}", [P, key_tiles, HG, 32], F32) for p in range(2)]
        pbuf = [sb(f"pb{p}", [P, HG, 512], F32) for p in range(2)]
        mxp = [sb(f"mxp{p}", [P, NU, KB], F32) for p in range(2)]
        negm = sb("negm", [P, NU], F32)
        mtmp = sb("mtmp", [P, NU], F32)
        avs = sb("avs", [P, QC, P], F32)
        rc = sb("rc", [P, QC, HG], F32)
        ps_s = cx.enter_context(nc.psum_tensor(f"ps_s{prog['n']}", [P, BANKS_S, 512], F32))
        ps_m = cx.enter_context(nc.psum_tensor(f"ps_m{prog['n']}", [P, BANKS_M, 512], F32))
        ps_av = cx.enter_context(nc.psum_tensor(f"ps_av{prog['n']}", [P, 512], F32))
        ps_t = cx.enter_context(nc.psum_tensor(f"ps_t{prog['n']}", [P, QC, P], F32))
        ps_tb = ps_t[:, :, :].rearrange("p a b -> p (a b)").bitcast(BF16).rearrange("p (a b) -> p a b", b=P)
        block = cx.enter_context(nc.Block())

        def group(n):
            return n // (T // QC)

        def chunk(n):
            return n % (T // QC)

        def pairs(eng, body):
            body(0, 0, True, True)
            body(1, 1, False, True)
            with eng.Fori(1, NCH // 2 - 1) as j:
                for p in range(2):
                    body(2 * j + p, p, False, True)
            body(NCH - 2, 0, False, True)
            body(NCH - 1, 1, False, False)

        share = [SHARE_LIGHT if t == LIGHT_STEP else 1.0 for t in range(key_tiles)]
        bounds = [round(UN * sum(share[:t]) / sum(share)) for t in range(key_tiles + 1)]
        lead = UN - bounds[key_tiles - TAIL]
        ring_m, ring_s = ring(UN, BANKS_M), ring(key_tiles * HG, BANKS_S)
        TURN = (key_tiles - TAIL - 3, key_tiles - TAIL - 1)

        def queries(eng, n, p):
            if not (type(n) is int and n < 2):
                eng.wait_ge(s["tb"], n - 1)
            on_pool = not (type(n) is int and n < 2)
            if on_pool:
                eng.sem_inc(s["tick"], 1)
            c = Counted(eng, s["qsplit"], n * QS, s["tick"] if on_pool else None)
            src = qn[:, at(chunk(n) * QC, QC), at(group(n) * GW, GW)].rearrange("p t (h d) -> p t h d", d=HD)
            c(eng.tensor_copy(qtmp[:, :, :, :], src))
            c.wait()
            hi, mid, lo = parts(qnat[p][:, :, :, :], "q")
            for d in hi:
                c(eng.tensor_copy(d, qtmp[:, :, :, :]))
            c.wait()
            c(eng.tensor_tensor(qtmp[:, :, :, :], qtmp[:, :, :, :], hi[0], ALU.subtract))
            c.wait()
            for d in mid:
                c(eng.tensor_copy(d, qtmp[:, :, :, :]))
            c.wait()
            c(eng.tensor_tensor(lo[0], qtmp[:, :, :, :], mid[0], ALU.subtract))
            assert c.n == QS, c.n
            c.wait()

        TURN_M = (key_tiles - 3, key_tiles - 2)

        @block.gpsimd
        def _(g):
            for p in range(2):
                g.memset(vst[p][:, :, :, HD + 1:32], 0.0).then_inc(s["set"], 1)
                for h in range(HG):
                    g.tensor_copy(vst[p][:, :, h, HD], valid[:, 0:key_tiles]).then_inc(s["set"], 1)
            g.wait_ge(s["set"], 2 + 2 * HG)

            def values(n, p):
                g.tensor_copy(vst[p][:, :, :, 0:HD],
                              v_nat[:, 0:key_tiles, at(group(n) * GW, GW)].rearrange("p t (h d) -> p t h d", d=HD))\
                 .then_inc(s["vst"], 1)

            def query_rows(n, p):
                g.wait_ge(s["taev"], 2 * n + 2)
                if not (type(n) is int and n < 2):
                    g.wait_ge(s["sc"], HG * key_tiles * (n - 1))
                g.sem_inc(s["tick"], 1)
                g.tensor_copy(qt[p][0:MAXROW, :, :, :], qm[p][:, :, :, :]).then_inc(s["qcopy"], 1)

            values(0, 0)
            query_rows(0, 0)

            def body(n, p, first, more):
                if more:
                    query_rows(n + 1, 1 - p)
                    if not first:
                        s["av"].wait(g, n * key_tiles)
                        g.sem_inc(s["tick"], 1)
                    values(n + 1, 1 - p)
                    if not (type(n) is int and n + 2 >= NCH):
                        queries(g, n + 2, p)
            pairs(g, body)

        @block.tensor
        def _(pe):
            def turn_q(n, p, half):
                if half == 0:
                    pe.wait_ge(s["qsplit"], n * QS + QS)
                    s["norm"].wait(pe, n - 2)
                    if type(n) is int and n == 1:
                        pe.wait_ge(s["tbev"], 2)
                else:
                    pe.wait_ge(s["taev"], 2 * n + 1)
                for u in range(8):
                    a, h = 2 * half + u // HG, u % HG
                    m = pe.transpose(ps_tb[0:MAXROW, u, :], qnat[p][:, a, h, 0:MAXROW], identb[:, :])
                m.then_inc(s["ta"], 1)

            def turn_m(n, p, half):
                if half == 0:
                    pe.wait_ge(s["msplit"], n * MS + MS)
                    if type(n) is int and n in (0, NCH - 1):
                        pe.wait_ge(s["taev"], 2 * n + 2)
                        s["norm"].wait(pe, n - 1)
                    else:
                        pe.wait_ge(s["taev"], 2 * n + 4)
                else:
                    pe.wait_ge(s["tbev"], 2 * n + 1)
                for u in range(8):
                    a, h = 2 * half + u // HG, u % HG
                    m = pe.transpose(ps_tb[MAXROW:P, u, :], qnat[p][:, a, h, MAXROW:P], identb[:, :])
                m.then_inc(s["tb"] if half else s["tb0"], 1)

            def max_unit(n, p, u):
                a, k = divmod(u, UA)
                bank, back = ring_m[(u - lead) % UN]
                s["mred"].wait(pe, n * UN + u - back + 1)
                if k < HG * FULL:
                    work = [(k // FULL, k % FULL * 512, 512, 0)]
                else:
                    work = [(h, FULL * 512, REST, h * REST) for h in range(HG)]
                for h, key, width, col in work:
                    m = pe.matmul(ps_m[:, bank, col:col + width], qm[p][:, h, a, :],
                                  kt[0:MAXROW, group(n) * HG + h, key:key + width], start=True, stop=True)
                m.then_inc(s["mx"], 1)

            def score(n, p, t, h):
                bank, back = ring_s[t * HG + h]
                s["exp"].wait(pe, (n * key_tiles + t) * HG + h - back + 1)
                m = pe.matmul(ps_s[:, bank, :], kt[:, group(n) * HG + h, t * P:(t + 1) * P], qt[p][:, h, :, :],
                              start=True, stop=True)
                m.then_inc(s["sc"], 1)

            def values(n, p, t):
                s["exp"].wait(pe, (n * key_tiles + t) * HG + HG)
                if t == 0:
                    pe.wait_ge(s["vst"], n + 1)
                    s["avev"].wait(pe, n)
                for h in range(HG):
                    m = pe.matmul(ps_av[32 * h:32 * h + 32, :], vst[p][:, t, h, :], pbuf[t % 2][:, h, :],
                                  start=(t == 0), stop=(t == key_tiles - 1))
                m.then_inc(s["av"].sem, 1)

            def results(n):
                s["avev"].wait(pe, n + 1)
                for a in range(QC):
                    m = pe.transpose(ps_t[:, a, :], avs[:, a, :], ident[:, :])
                m.then_inc(s["te"].sem, 1)

            def max_units(n, p, lo, hi):
                for k in range(lo, hi):
                    u = lead + k
                    if u < UN:
                        max_unit(n + 1, 1 - p, u)
                    elif not (type(n) is int and n + 2 >= NCH):
                        if u == UN:
                            pe.wait_ge(s["taev"], 2 * n + 6)
                        max_unit(n + 2, p, u - UN)

            s["av"].open(pe)
            s["te"].open(pe)
            turn_q(0, 0, 0)
            turn_q(0, 0, 1)
            pe.wait_ge(s["taev"], 2)
            for u in range(UN):
                max_unit(0, 0, u)
            turn_m(0, 0, 0)
            turn_m(0, 0, 1)
            turn_q(1, 1, 0)
            turn_q(1, 1, 1)
            pe.wait_ge(s["taev"], 4)
            for u in range(lead):
                max_unit(1, 1, u)

            def body(n, p, first, more):
                more2 = not (type(n) is int and n + 2 >= NCH)
                pe.wait_ge(s["tbev"], 2 * n + 2)
                pe.wait_ge(s["qcopy"], n + 1)
                for h in range(HG):
                    score(n, p, 0, h)
                for t in range(key_tiles):
                    if t == LIGHT_STEP and not first:
                        results(n - 1)
                    if t in TURN and more2:
                        turn_q(n + 2, p, TURN.index(t))
                    if t in TURN_M and more:
                        turn_m(n + 1, 1 - p, TURN_M.index(t))
                    units = bounds[t + 1] - bounds[t]
                    for h in range(HG):
                        if more:
                            max_units(n, p, bounds[t] + units * h // HG, bounds[t] + units * (h + 1) // HG)
                        if t + 1 < key_tiles:
                            score(n, p, t + 1, h)
                    values(n, p, t)
                if not more:
                    s["norm"].wait(pe, n)
                    results(n)
            pairs(pe, body)

        @block.scalar
        def _(a):
            def ev_q(n, p, half):
                a.wait_ge(s["ta"], 2 * n + half + 1)
                a.copy(qm[p][:, :, 2 * half:2 * half + 2, :],
                       ps_tb[0:MAXROW, :, :].rearrange("p (a h) b -> p h a b", h=HG)).then_inc(s["taev"], 1)

            def ev_m(n, p, half):
                a.wait_ge(s["tb0"] if half == 0 else s["tb"], n + 1)
                a.copy(qt[p][MAXROW:P, :, 2 * half:2 * half + 2, :],
                       ps_tb[MAXROW:P, :, :].rearrange("p (a h) b -> p h a b", h=HG)).then_inc(s["tbev"], 1)

            def body(n, p, first, more):
                more2 = not (type(n) is int and n + 2 >= NCH)
                for t in range(key_tiles):
                    for h in range(HG):
                        a.wait_ge(s["sc"], (n * key_tiles + t) * HG + h + 1)
                        if h == 0:
                            s["av"].wait(a, n * key_tiles + t - 1)
                        a.activation(pbuf[t % 2][:, h, :], ps_s[:, ring_s[t * HG + h][0], :], ACT.Exp)\
                         .then_inc(s["exp"].sem, 1)
                        if more2 and h == 1 and t - 1 in TURN:
                            ev_q(n + 2, p, TURN.index(t - 1))
                        if more and h == 1 and t - 1 in TURN_M:
                            ev_m(n + 1, 1 - p, TURN_M.index(t - 1))
                s["av"].wait(a, (n + 1) * key_tiles)
                s["te"].wait(a, n)
                a.copy(avs[:, :, :], ps_av[:, :].rearrange("p (a b) -> p a b", b=P)).then_inc(s["avev"].sem, 1)

            s["exp"].open(a)
            s["avev"].open(a)
            ev_q(0, 0, 0)
            ev_q(0, 0, 1)
            ev_m(0, 0, 0)
            ev_m(0, 0, 1)
            ev_q(1, 1, 0)
            ev_q(1, 1, 1)
            pairs(a, body)

        @block.vector
        def _(v):
            def reduce_unit(n, p, u):
                v.wait_ge(s["mx"], n * UN + u + 1)
                a, k = divmod(u, UA)
                bank = ring_m[(u - lead) % UN][0]
                if k < HG * FULL:
                    dst, src = mxp[p][:, a * HG + k // FULL, k % FULL:k % FULL + 1], ps_m[:, bank, :]
                else:
                    dst = mxp[p][:, a * HG:a * HG + HG, FULL]
                    src = ps_m[:, bank, 0:HG * REST].rearrange("p (h n) -> p h n", h=HG)
                v.tensor_reduce(dst, src, AX.X, ALU.max).then_inc(s["mred"].sem, 1)

            def stream(n, p, lo, hi):
                for k in range(lo, hi):
                    u = lead + k
                    if u < UN:
                        reduce_unit(n + 1, 1 - p, u)
                    elif not (type(n) is int and n + 2 >= NCH):
                        reduce_unit(n + 2, p, u - UN)

            def maxima(n, p, between):
                s["mred"].wait(v, n * UN + UN)
                c = Counted(v, s["msplit"], n * MS)
                place = [qnat[p][:, :, :, MAXROW + i] for i in range(3)]
                neg = negm[:, :].rearrange("p (a h) -> p a h", h=HG)
                tmp = mtmp[:, :].rearrange("p (a h) -> p a h", h=HG)
                c(v.tensor_reduce(negm[:, :], mxp[p][:, :, :], AX.X, ALU.max, negate=True))
                between()
                c.wait()
                v.wait_ge(s["qset"], 2)
                v.wait_ge(s["qsplit"], n * QS + QS)
                c(v.tensor_copy(place[0], neg))
                between()
                c.wait()
                c(v.tensor_tensor(tmp, neg, place[0], ALU.subtract))
                between()
                c.wait()
                c(v.tensor_copy(place[1], tmp))
                between()
                c.wait()
                c(v.tensor_tensor(place[2], tmp, place[1], ALU.subtract))
                assert c.n == MS, c.n
                c.wait()

            def normalise(n):
                s["te"].wait(v, n + 1)
                res = ps_t[:, :, :].rearrange("p a (h d) -> p a h d", d=32)
                v.reciprocal(rc[:, :, :], res[:, :, :, HD]).then_inc(s["rc"], 1)
                v.wait_ge(s["rc"], n + 1)
                v.tensor_tensor(qn[:, at(chunk(n) * QC, QC), at(group(n) * GW, GW)].rearrange("p t (h d) -> p t h d", d=HD),
                                res[:, :, :, 0:HD], rc[:, :, :].unsqueeze(3).to_broadcast([P, QC, HG, HD]),
                                ALU.mult).then_inc(s["norm"].sem, 1)

            def body(n, p, first, more):
                if not more:
                    normalise(n - 1)
                    normalise(n)
                    s["norm"].wait(v, n + 1)
                    return
                early, end = bounds[2], UN - lead
                stream(n, p, 0, early)
                if not first:
                    normalise(n - 1)
                stream(n, p, early, end)
                at_unit = [end]

                def between():
                    if at_unit[0] < UN:
                        stream(n, p, at_unit[0], at_unit[0] + 1)
                        at_unit[0] += 1
                maxima(n + 1, 1 - p, between)
                stream(n, p, at_unit[0], UN)
            s["mred"].open(v)
            s["norm"].open(v)
            for p in range(2):
                v.memset(qnat[p][:, :, :, MAXROW:P], 0.0).then_inc(s["qset"], 1)
                queries(v, p, p)
            for u in range(UN):
                reduce_unit(0, 0, u)
            maxima(0, 0, lambda: None)
            for u in range(lead):
                reduce_unit(1, 1, u)
            pairs(v, body)



def self_qkv(prog, x, mean, rstd, w, gain, shift, qn, kn, v_nat, ident):
    nc = prog["nc"]
    s_w = fresh(prog, "head_weights")
    s_affine, s_tick = fresh(prog, "head_affine"), fresh(prog, "head_tick")
    s_sq, s_var, s_sd = fresh(prog, "head_squares"), fresh(prog, "head_var"), fresh(prog, "head_sd")
    with ExitStack() as cx:
        wsum = cx.enter_context(nc.sbuf_tensor("hwsum", [P, 2, 2 * H], F32))
        squares = cx.enter_context(nc.sbuf_tensor("hsq", [P, 2 * H, HD], F32))
        sums, var, sd, rs = (cx.enter_context(nc.sbuf_tensor(k, [P, 2 * H], F32)) for k in ("hsum", "hvar", "hsd", "hrs"))
        with nc.Block() as block:
            @block.vector
            def _(v):
                c = Counted(v, s_w)
                wh = w[:, :, 0:2 * D].rearrange("p k (h d) -> p k h d", d=HD)
                c(v.tensor_scalar(gain[:, 0, :], gain[:, 0, :], 0.25, None, ALU.mult))
                c(v.tensor_scalar(shift[:, 0, :], shift[:, 0, :], 0.25, None, ALU.mult))
                c(v.tensor_reduce(wsum[:, :, :], wh, AX.X, ALU.add))
                c.wait()
                c(v.tensor_scalar(wsum[:, :, :], wsum[:, :, :], 1.0 / HD, None, ALU.mult))
                c.wait()
                for k in range(2):
                    c(v.tensor_tensor(wh[:, k, :, :], wh[:, k, :, :],
                                      wsum[:, k, :].unsqueeze(2).to_broadcast([P, 2 * H, HD]), ALU.subtract))
                c.wait()

        def side(a, prod, n, r, s_read):
            a.activation(squares[:, :, :], prod[:, 0, :].rearrange("p (h d) -> p h d", d=HD), ACT.Square).then_inc(s_sq, 1)
            a.copy(v_nat[:, n, :], prod[:, 1, 0:D]).then_inc(s_read, 1)
            a.wait_ge(s_var, n + 1)
            a.activation(sd[:, :], var[:, :], ACT.Sqrt).then_inc(s_sd, 1)

        def epilogue(v, prod, n, r, c):
            v.wait_ge(s_sq, n + 1)
            c(v.tensor_reduce(sums[:, :], squares[:, :, :], AX.X, ALU.add))
            c.wait()
            v.tensor_scalar(var[:, :], sums[:, :], 1.0 / HD, EPS_LN, ALU.mult, ALU.add).then_inc(s_var, 1)
            v.wait_ge(s_sd, n + 1)
            c(v.reciprocal(rs[:, :], sd[:, :]))
            c.wait()
            for i, dst in enumerate((qn, kn)):
                c(v.tensor_tensor(dst[:, n, :].rearrange("p (h d) -> p h d", d=HD),
                                  prod[:, 0, i * D:i * D + D].rearrange("p (h d) -> p h d", d=HD),
                                  rs[:, i * H:i * H + H].unsqueeze(2).to_broadcast([P, H, HD]), ALU.mult))

        def late(g, n, r):
            c = Counted(g, s_affine, n * 4, s_tick)
            for i, dst in enumerate((qn, kn)):
                c(g.tensor_tensor(dst[:, n, :], dst[:, n, :], gain[:, i, :], ALU.mult))
            c.wait()
            for i, dst in enumerate((qn, kn)):
                c(g.tensor_tensor(dst[:, n, :], dst[:, n, :], shift[:, i, :], ALU.add))
            c.wait()

        linear(prog, T, ln_rows(x, mean, rstd), w, 3 * D, epilogue, 4, ident, side=side, late=late)


def cross_q(prog, x, mean, rstd, w, bias, qn, ident):
    def epilogue(v, prod, n, r, c):
        c(v.scalar_tensor_tensor(qn[:, n, :], prod[:, 0, 0:D], 0.25, bias[:, :], ALU.mult, ALU.add))
    linear(prog, T, ln_rows(x, mean, rstd), w, D, epilogue, 1, ident)


def experts(prog, x, st, mean, rstd, gate, w, iota, ident):
    nc = prog["nc"]
    s_fetch, s_turned = fresh(prog, "mfetch"), fresh(prog, "mturned")
    s_copied, s_gate, s_w = Slots(prog, "mcopied"), Slots(prog, "mgate"), Slots(prog, "mprod", 5)
    s_d, s_e = fresh(prog, "mdiff"), fresh(prog, "mexp")
    s_gc, s_acc = fresh(prog, "mgchain"), fresh(prog, "msum")
    s_used, s_gused = Slots(prog, "mused", 4), Slots(prog, "mgused", 2)
    s_tick = fresh(prog, "mtick")
    per = 9
    with ExitStack() as cx:
        def sb(name, shape, dt=F32):
            return cx.enter_context(nc.sbuf_tensor(name, shape, dt))
        xn = [sb(f"mxn{p}", [P, D]) for p in range(2)]
        xt = [sb(f"mxt{p}", [P, 2, P]) for p in range(2)]
        lg, m8, i8, pair = sb("mlg", [P, NE]), sb("mm8", [P, 8]), sb("mi8", [P, 8], U32), sb("mpair", [P, 2])
        dif, ex, den, w1, w2 = (sb(k, [P, 1]) for k in ("mdif", "mex", "mden", "mw1", "mw2"))
        wa, wb, mix = sb("mwa", [P, NE]), sb("mwb", [P, NE]), [sb(f"mmix{p}", [P, NE]) for p in range(2)]
        turn = [cx.enter_context(nc.psum_tensor(f"mturn{p}", [P, 512], F32)) for p in range(2)]
        pg = [cx.enter_context(nc.psum_tensor(f"mpg{p}", [P, 512], F32)) for p in range(2)]
        prod = cx.enter_context(nc.psum_tensor("mprodp", [P, 4, 512], F32))
        block = cx.enter_context(nc.Block())

        def every(body, eng):
            with eng.Fori(0, T // 4 - 1) as i:
                for r in range(4):
                    body(4 * i + r, r % 2)
            for n in range(T - 4, T):
                body(n, n % 2)

        def has(n):
            return not (type(n) is int and n >= T)

        @block.tensor
        def _(pe):
            def turn_tile(n, p):
                pe.wait_ge(s_fetch, n + 1)
                s_copied.wait(pe, n - 1)
                for k in range(2):
                    m = pe.transpose(turn[p][:, k * P:(k + 1) * P], xn[p][:, k * P:(k + 1) * P], ident[:, :])
                m.then_inc(s_turned, 1)

            def logits(n, p):
                s_copied.wait(pe, n + 1)
                s_gused.wait(pe, n - 1)
                for k in range(2):
                    m = pe.matmul(pg[p][:, 0:NE], xt[p][:, k, :], gate[:, k, :], start=(k == 0), stop=(k == 1))
                m.then_inc(s_gate.sem, 1)

            def multiply(n, p):
                if has(n + 1):
                    turn_tile(n + 1, 1 - p)
                for b in range(4):
                    if b == 1 and has(n + 1):
                        logits(n + 1, 1 - p)
                    s_used.wait(pe, 4 * n + b - 3)
                    for k in range(2):
                        m = pe.matmul(prod[:, b, :], xt[p][:, k, :], w[:, k, b * 512:b * 512 + 512],
                                      start=(k == 0), stop=(k == 1))
                    m.then_inc(s_w.sem, 1)
            s_gate.open(pe)
            s_w.open(pe)
            turn_tile(0, 0)
            logits(0, 0)
            every(multiply, pe)

        @block.scalar
        def _(a):
            def copy(n, p):
                s_w.wait(a, 4 * (n - 1))
                a.wait_ge(s_turned, n + 1)
                a.copy(xt[p][:, :, :], turn[p][:, 0:D].rearrange("p (k n) -> p k n", k=2)).then_inc(s_copied.sem, 1)
                a.wait_ge(s_d, n + 1)
                a.activation(ex[:, :], dif[:, :], ACT.Exp).then_inc(s_e, 1)
            s_copied.open(a)
            every(copy, a)

        @block.vector
        def _(v):
            fetch = ln_rows(x, mean, rstd)
            s_used.open(v)
            s_gused.open(v)

            def mixture(n, p):
                we = mix[p]
                c = Counted(v, s_gc, n * per)
                s_gate.wait(v, n + 1)
                v.tensor_copy(lg[:, :], pg[p][:, 0:NE]).then_inc(s_gused.sem, 1)
                yield
                s_gused.wait(v, n + 1)
                v.sem_inc(s_tick, 1)
                c(v.max(m8[:, :], lg[:, :]))
                yield
                c.wait()
                v.sem_inc(s_tick, 1)
                c(v.max_index(i8[:, :], m8[:, :], lg[:, :]))
                v.tensor_tensor(dif[:, :], m8[:, 1:2], m8[:, 0:1], ALU.subtract).then_inc(s_d, 1)
                yield
                c.wait()
                c(v.tensor_copy(pair[:, :], i8[:, 0:2]))
                yield
                v.wait_ge(s_e, n + 1)
                c(v.tensor_scalar(den[:, :], ex[:, :], 1.0, None, ALU.add))
                yield
                c.wait()
                c(v.reciprocal(w1[:, :], den[:, :]))
                yield
                c.wait()
                c(v.tensor_tensor(w2[:, :], ex[:, :], w1[:, :], ALU.mult))
                c(v.tensor_scalar(wa[:, :], iota[:, :], pair[:, 0:1], w1[:, :], ALU.is_equal, ALU.mult))
                yield
                c.wait()
                c(v.tensor_scalar(wb[:, :], iota[:, :], pair[:, 1:2], w2[:, :], ALU.is_equal, ALU.mult))
                yield
                c.wait()
                c(v.tensor_tensor(we[:, :], wa[:, :], wb[:, :], ALU.add))
                assert c.n == per, c.n
                yield
                c.wait()

            def accumulate(n, p):
                we = mix[p]
                c = Counted(v, s_acc, n * 5)
                for e in range(NE):
                    if e % 2 == 0:
                        s_w.wait(v, 4 * n + e // 2 + 1)
                    o = v.scalar_tensor_tensor(x[:, n, :], prod[:, e // 2, (e % 2) * D:(e % 2) * D + D], we[:, e:e + 1],
                                               x[:, n, :], ALU.mult, ALU.add)
                    if e % 2:
                        o.then_inc(s_used.sem, 1)
                        yield
                        s_used.wait(v, 4 * n + e // 2 + 1)
                    else:
                        c(o)
                        yield
                        c.wait()
                c(v.bn_stats(st[:, n, :], x[:, n, :]))
                assert c.n == 5, c.n

            def body(n, p):
                if has(n + 2):
                    v.wait_ge(s_turned, n + 1)
                    fetch(v, xn[p], n + 2).then_inc(s_fetch, 1)
                turns = [accumulate(n, p)] + ([mixture(n + 1, 1 - p)] if has(n + 1) else [])
                while turns:
                    turns = [g for g in turns if next(g, "done") != "done"]
            for n in range(2):
                fetch(v, xn[n], n).then_inc(s_fetch, 1)
            list(mixture(0, 0))
            every(body, v)



def focused_qkv(prog, x, mean, rstd, w, qf, ps_kv, ident):
    nc = prog["nc"]
    with ExitStack() as cx:
        sums = cx.enter_context(nc.sbuf_tensor("fsum", [P, 2 * H], F32))
        rs = cx.enter_context(nc.sbuf_tensor("frs", [P, 2 * H], F32))
        a = [cx.enter_context(nc.sbuf_tensor(f"fa{r}", [P, 2 * H, HD], F32)) for r in range(UNROLL)]
        b = [cx.enter_context(nc.sbuf_tensor(f"fb{p}", [P, 2 * H, HD], F32)) for p in range(2)]
        square = [cx.enter_context(nc.sbuf_tensor(f"fsquare{p}", [P, 2 * H, HD], F32)) for p in range(2)]
        sums2 = cx.enter_context(nc.sbuf_tensor("fsum2", [P, 2 * H], F32))
        eps = cx.enter_context(nc.sbuf_tensor("feps", [P, 1], F32))
        s_cube, s_eps = Slots(prog, "focus_cube", 3 * UNROLL), fresh(prog, "focus_eps")
        cube = [cx.enter_context(nc.sbuf_tensor(f"fcube{p}", [P, 2 * H, HD], F32)) for p in range(2)]
        rs2 = [cx.enter_context(nc.sbuf_tensor(f"frs2{p}", [P, 2 * H], F32)) for p in range(2)]
        v_ring = [cx.enter_context(nc.sbuf_tensor(f"fv{r}", [P, 2, P + 1], F32)) for r in range(UNROLL)]
        k_ring = [cx.enter_context(nc.sbuf_tensor(f"fk{r}", [P, D], F32)) for r in range(UNROLL)]
        s_late, s_kv, s_tick = Slots(prog, "focus_late", 3), Slots(prog, "focus_kv", UNROLL), fresh(prog, "focus_tick")
        s_ones = fresh(prog, "focus_ones")
        s_relu, s_norm, s_sq = fresh(prog, "focus_relu"), fresh(prog, "focus_norm"), fresh(prog, "focus_squares")
        spread = lambda t, i, n: t[:, i:i + n].unsqueeze(2).to_broadcast([P, n, HD])

        def side(act, prod, n, r, s_read):
            qk = prod[:, 0, :].rearrange("p (h d) -> p h d", d=HD)
            act.activation(b[r % 2][:, :, :], qk, ACT.Relu).then_inc(s_relu, 1)
            s_kv.wait(act, n + 1 - UNROLL)
            act.copy(v_ring[r][:, :, 0:P], prod[:, 1, 0:D].rearrange("p (j c) -> p j c", j=2)).then_inc(s_read, 1)
            s_cube.wait(act, 3 * (n + 1 - UNROLL))
            act.wait_ge(s_relu, n + 1)
            act.activation(a[r][:, :, :], b[r % 2][:, :, :], ACT.Identity, bias=eps[:, :]).then_inc(s_eps, 1)
            if not (type(n) is int and n == 0):
                squares(act, n - 1, (r - 1) % UNROLL)

        def squares(act, n, r):
            act.wait_ge(s_norm, n + 1)
            act.activation(square[r % 2][:, :, :], a[r][:, :, :], ACT.Square).then_inc(s_sq, 1)

        def epilogue(v, prod, n, r, c):
            a_n = a[r]
            v.wait_ge(s_eps, n + 1)
            c(v.tensor_reduce(sums[:, :], a_n[:, :, :], AX.X, ALU.add))
            c.wait()
            c(v.reciprocal(rs[:, :], sums[:, :]))
            c.wait()
            v.tensor_tensor(a_n[:, :, :], a_n[:, :, :], spread(rs, 0, 2 * H), ALU.mult).then_inc(s_norm, 1)

        def second(v, n, r):
            p = r % 2
            c = Counted(v, s_cube.sem, 3 * n + s_cube.ahead)
            v.wait_ge(s_norm, n + 1)
            v.wait_ge(s_sq, n + 1)
            s_late.wait(v, 2 * (n - 1))
            c(v.tensor_tensor(cube[p][:, :, :], square[p][:, :, :], a[r][:, :, :], ALU.mult))
            c.wait()
            c(v.tensor_reduce(sums2[:, :], cube[p][:, :, :], AX.X, ALU.add))
            c.wait()
            c(v.reciprocal(rs2[p][:, :], sums2[:, :]))
            c.wait()

        def late(g, n, r):
            s_cube.wait(g, 3 * n + 3)
            s_kv.wait(g, n + 1 - UNROLL)
            g.sem_inc(s_tick, 1)
            c = Counted(g, s_late.sem, 2 * n + s_late.ahead, s_tick)
            for i, dst in enumerate((qf[:, n, :], k_ring[r][:, :])):
                c(g.tensor_tensor(dst.rearrange("p (h d) -> p h d", d=HD), cube[r % 2][:, i * H:i * H + H, :],
                                  spread(rs2[r % 2], i * H, H), ALU.mult))
            c.wait()

        def beside(pe, n, r):
            s_late.wait(pe, 2 * n + 2)
            start, stop = type(n) is int and n == 0, type(n) is int and n == T - 1
            for j in range(2):
                m = pe.matmul(ps_kv[:, j, 0:P + 1], k_ring[r][:, j * P:j * P + P], v_ring[r][:, j, :], start=start, stop=stop)
            m.then_inc(s_kv.sem, 1)
        with nc.Block() as block:
            @block.gpsimd
            def _(g):
                s_late.open(g)
                for r in range(UNROLL):
                    g.memset(v_ring[r][:, :, P], 1.0).then_inc(s_ones, 1)
                g.memset(eps[:, :], EPS_FOCUS).then_inc(s_ones, 1)
                g.wait_ge(s_ones, UNROLL + 1)

            @block.vector
            def _(v):
                s_cube.open(v)

            @block.tensor
            def _(pe):
                s_kv.open(pe)
        linear(prog, T, ln_rows(x, mean, rstd), w, 3 * D, epilogue, 2, ident, side=side, late=late, beside=(beside, 3),
               second=second, side_end=lambda act: squares(act, T - 1, (T - 1) % UNROLL))


def linear_attention(prog, qf, ps_kv, yt, tap, tap_bias, mask, ident):
    nc = prog["nc"]
    s = {k: fresh(prog, "la_" + k) for k in ("set", "copy", "num", "den", "o", "to", "conv", "tick")}
    s["tq"] = Slots(prog, "la_tq", UNROLL)
    s["qt"], s["ot"] = Slots(prog, "la_qt"), Slots(prog, "la_ot", 4)
    PH = P // HD
    N = P + PH
    with ExitStack() as cx:
        def sb(name, shape):
            return cx.enter_context(nc.sbuf_tensor(name, shape, F32))
        bd, ks, tap1 = sb("lbd", [P, 2, N]), sb("lks", [P, 2]), sb("ltap1", [P, 2])
        qs, qt = [sb(f"lqs{r}", [P, D]) for r in range(UNROLL)], [sb(f"lqt{p}", [P, 2, P]) for p in range(2)]
        z, rz, o = sb("lz", [P, 2, PH]), sb("lrz", [P, 2, PH]), [sb(f"lo{p}", [P, 2, P]) for p in range(2)]
        ot = sb("lot", [P, 2, S + 2])
        ps_q, ps_n, ps_o = ([cx.enter_context(nc.psum_tensor(f"lps{k}{p}", [P, 2, 256], F32)) for p in range(2)] for k in "qno")
        block = cx.enter_context(nc.Block())

        def every(body, eng):
            with eng.Fori(0, T // UNROLL - 1) as i:
                for r in range(UNROLL):
                    body(UNROLL * i + r, r)
            for n in range(T - UNROLL, T):
                body(n, n % UNROLL)

        def has(n):
            return not (type(n) is int and n >= T)

        @block.gpsimd
        def _(g):
            def rows(n, r):
                s["tq"].wait(g, n + 1 - UNROLL)
                g.sem_inc(s["tick"], 1)
                g.tensor_copy(qs[r][:, :], qf[:, n, :]).then_inc(s["copy"], 1)
            every(rows, g)

        @block.tensor
        def _(pe):
            def turn_q(n, r):
                pe.wait_ge(s["copy"], n + 1)
                s["qt"].wait(pe, n - 1)
                for j in range(2):
                    m = pe.transpose(ps_q[r % 2][:, j, 0:P], qs[r][:, j * P:j * P + P], ident[:, :])
                m.then_inc(s["tq"].sem, 1)

            def turn_o(n, r):
                pe.wait_ge(s["o"], n + 1)
                s["ot"].wait(pe, 3 * (n - 1))
                for j in range(2):
                    m = pe.transpose(ps_o[r % 2][:, j, 0:P], o[r % 2][:, j, :], ident[:, :])
                m.then_inc(s["to"], 1)

            def body(n, r):
                p = r % 2
                if has(n + 1):
                    turn_q(n + 1, (r + 1) % UNROLL)
                s["qt"].wait(pe, n + 1)
                for j in range(2):
                    m = pe.matmul(ps_n[p][:, j, 0:N], qt[p][:, j, :], bd[:, j, :], start=True, stop=True)
                m.then_inc(s["num"], 1)
                if not (type(n) is int and n == 0):
                    turn_o(n - 1, (r - 1) % UNROLL)
            s["tq"].open(pe)
            turn_q(0, 0)
            pe.wait_ge(s["set"], 6)
            for n in range(UNROLL):
                body(n, n)
            with pe.Fori(1, T // UNROLL - 1) as i:
                for r in range(UNROLL):
                    body(UNROLL * i + r, r)
            for n in range(T - UNROLL, T):
                body(n, n % UNROLL)
            turn_o(T - 1, UNROLL - 1)

        @block.scalar
        def _(a):
            def out(n, p):
                a.wait_ge(s["to"], n + 1)
                a.copy(ot[:, :, at(n * P + 1, P)], ps_o[p][:, :, 0:P]).then_inc(s["ot"].sem, 1)
                for j in range(2):
                    a.activation(yt[:, j, at(n * P, P)], ps_o[p][:, j, 0:P], ACT.Identity, bias=tap_bias[:, j:j + 1],
                                 scale=tap1[:, j:j + 1]).then_inc(s["ot"].sem, 1)

            def turned(n, p):
                s["tq"].wait(a, n + 1)
                a.copy(qt[p][:, :, :], ps_q[p][:, :, 0:P]).then_inc(s["qt"].sem, 1)
            s["qt"].open(a)
            s["ot"].open(a)
            a.wait_ge(s["set"], 6)

            def body(n, r):
                if has(n + 1):
                    turned(n + 1, 1 - r % 2)
                if not (type(n) is int and n == 0):
                    out(n - 1, 1 - r % 2)
            turned(0, 0)
            for n in range(UNROLL):
                body(n, n)
            with a.Fori(1, T // UNROLL - 1) as i:
                for r in range(UNROLL):
                    body(UNROLL * i + r, r)
            for n in range(T - UNROLL, T):
                body(n, n % UNROLL)
            out(T - 1, 1)

        @block.vector
        def _(v):
            c = Counted(v, s["set"])
            v.memset(ot[:, :, 0:S + 2:S + 1], 0.0).then_inc(s["conv"], 1)
            c(v.tensor_scalar(tap1[:, :], tap[:, :, 1], 1.0, None, ALU.add))
            c(v.tensor_copy(ks[:, :], ps_kv[:, :, P]))
            for j in range(2):
                c(v.tensor_tensor(bd[:, j, 0:P], ps_kv[:, j, 0:P], mask[:, :], ALU.mult))
            v.wait_ge(s["set"], 2)
            for j in range(2):
                c(v.tensor_scalar(bd[:, j, P:N], mask[:, 0:P:HD], ks[:, j:j + 1], None, ALU.mult))
            c.wait()

            def body(n, r):
                p = r % 2
                c = Counted(v, s["den"], 2 * n)
                v.wait_ge(s["num"], n + 1)
                c(v.tensor_scalar(z[:, :, :], ps_n[p][:, :, P:N], EPS_FOCUS, None, ALU.add))
                c.wait()
                c(v.reciprocal(rz[:, :, :], z[:, :, :]))
                c.wait()
                s["ot"].wait(v, 3 * (n - 1))
                v.tensor_tensor(o[p][:, :, :].rearrange("p j (h d) -> p j h d", d=HD),
                                ps_n[p][:, :, 0:P].rearrange("p j (h d) -> p j h d", d=HD),
                                rz[:, :, :].unsqueeze(3).to_broadcast([P, 2, PH, HD]), ALU.mult).then_inc(s["o"], 1)
            every(body, v)
            s["ot"].wait(v, 3 * T)
            c = Counted(v, s["conv"])
            c.n = 1
            for sh, i in ((0, 0), (2, 2)):
                c.wait()
                for j in range(2):
                    c(v.scalar_tensor_tensor(yt[:, j, :], ot[:, j, sh:sh + S], tap[:, j, i:i + 1], yt[:, j, :],
                                             ALU.mult, ALU.add))
            c.wait()


def cross_keys(prog, ctx_t, wk, bk, keyt):
    nc = prog["nc"]
    s_m, s_c = fresh(prog, "ckm"), fresh(prog, "ckc")
    with ExitStack() as cx:
        ps = cx.enter_context(nc.psum_tensor("ckps", [P, 2, 4, 512], F32))
        block = cx.enter_context(nc.Block())

        @block.tensor
        def _(pe):
            for j in range(2):
                for b in range(4):
                    w = min(512, M - 512 * b)
                    for k in range(2):
                        m = pe.matmul(ps[:, j, b, 0:w], wk[0:CH, k, j * P:j * P + P], ctx_t[:, k, 512 * b:512 * b + w],
                                      start=(k == 0), stop=(k == 1))
                m.then_inc(s_m, 1)

        @block.vector
        def _(v):
            for j in range(2):
                v.wait_ge(s_m, j + 1)
                v.tensor_scalar(keyt[:, j, 0:M], ps[:, j, :, :].rearrange("p b n -> p (b n)")[:, 0:M], bk[:, j:j + 1], None,
                                ALU.add).then_inc(s_c, 1)
            v.wait_ge(s_c, 2)


def cross_one_head(prog, x, st, mean, rstd, wq, bq, keyt, vals, ident):
    nc = prog["nc"]
    s = {k: fresh(prog, k) for k in ("xf", "xtr", "xcp", "qm", "qc", "sc", "mx", "r", "ev")}
    for k in ("ex", "pt", "av", "o"):
        s[k] = Slots(prog, "x" + k)
    LAST = M - (TM - 1) * P
    UT = -(-TM // 4)
    with ExitStack() as cx:
        def sb(name, shape, dt=F32):
            return cx.enter_context(nc.sbuf_tensor(name, shape, dt))
        xn, xt, qt = sb("oxn", [P, D]), sb("oxt", [P, 2, P]), [sb(f"oqt{p}", [P, 2, P]) for p in range(2)]
        pn, pt = [sb(f"opn{p}", [P, MP]) for p in range(2)], sb("opt", [P, TM, P])
        nm, sm, rr = [sb(f"onm{p}", [P, 1]) for p in range(2)], [sb(f"osm{p}", [P, 1]) for p in range(2)], sb("orr", [P, 1])
        ps_s = cx.enter_context(nc.psum_tensor("ops_s", [P, 2048], F32))
        ps_x = cx.enter_context(nc.psum_tensor("ops_x", [P, 2, P], F32))
        ps_p = cx.enter_context(nc.psum_tensor("ops_p", [P, 2, 4, P], F32))
        ps_o = cx.enter_context(nc.psum_tensor("ops_o", [P, 512], F32))
        block = cx.enter_context(nc.Block())

        def every(body, eng):
            with eng.Fori(0, T // 4 - 1) as i:
                for r in range(4):
                    body(4 * i + r, r % 2)
            for n in range(T - 4, T):
                body(n, n % 2)

        def has(n):
            return not (type(n) is int and n >= T)

        @block.tensor
        def _(pe):
            def turn_x(n):
                pe.wait_ge(s["xf"], n + 1)
                if not (type(n) is int and n == 0):
                    pe.wait_ge(s["qc"], n)
                for k in range(2):
                    m = pe.transpose(ps_x[:, k, :], xn[:, k * P:k * P + P], ident[:, :])
                m.then_inc(s["xtr"], 1)

            def query(n):
                pe.wait_ge(s["xcp"], n + 1)
                for j in range(2):
                    for k in range(2):
                        m = pe.matmul(ps_x[:, j, :], wq[:, k, j * P:j * P + P], xt[:, k, :], start=(k == 0), stop=(k == 1))
                m.then_inc(s["qm"], 1)

            def score(n, p):
                pe.wait_ge(s["qc"], n + 1)
                s["ex"].wait(pe, n)
                for b in range(4):
                    w = min(512, M - 512 * b)
                    for j in range(2):
                        m = pe.matmul(ps_s[:, 512 * b:512 * b + w], qt[p][:, j, :], keyt[:, j, 512 * b:512 * b + w],
                                      start=(j == 0), stop=(j == 1))
                m.then_inc(s["sc"], 1)
            s["av"].open(pe)
            turn_x(0)
            query(0)
            turn_x(1)
            score(0, 0)
            query(1)

            def body(n, p):
                s["ex"].wait(pe, n + 1)
                for u in range(UT):
                    s["pt"].wait(pe, n * UT + u - 1)
                    for t in range(4 * u, min(TM, 4 * u + 4)):
                        r = P if t < TM - 1 else LAST
                        m = pe.transpose(ps_p[0:r, u % 2, t % 4, :], pn[p][:, t * P:t * P + r], ident[:, :])
                    m.then_inc(s["ev"], 1)
                if has(n + 2):
                    turn_x(n + 2)
                if has(n + 1):
                    score(n + 1, 1 - p)
                s["pt"].wait(pe, n * UT + UT)
                s["o"].wait(pe, n)
                for t in range(TM):
                    r = P if t < TM - 1 else LAST
                    m = pe.matmul(ps_o[:, 0:D], pt[0:r, t, :], vals[0:r, t, :], start=(t == 0), stop=(t == TM - 1))
                m.then_inc(s["av"].sem, 1)
                if has(n + 2):
                    query(n + 2)
            every(body, pe)

        @block.scalar
        def _(a):
            def copy_x(n):
                a.wait_ge(s["xtr"], n + 1)
                a.copy(xt[:, :, :], ps_x[:, :, :]).then_inc(s["xcp"], 1)

            def weights(n, p):
                a.wait_ge(s["mx"], n + 1)
                a.activation(pn[p][:, 0:M], ps_s[:, 0:M], ACT.Exp, bias=nm[p][:, :], accum_out=sm[p][:, :])\
                 .then_inc(s["ex"].sem, 1)
            s["ex"].open(a)
            s["pt"].open(a)
            copy_x(0)
            copy_x(1)
            weights(0, 0)

            def body(n, p):
                for u in range(UT):
                    a.wait_ge(s["ev"], n * UT + u + 1)
                    s["av"].wait(a, n)
                    lo, hi = 4 * u, min(TM, 4 * u + 4)
                    r = P if hi < TM else LAST
                    a.copy(pt[0:r, lo:hi, :], ps_p[0:r, u % 2, 0:hi - lo, :]).then_inc(s["pt"].sem, 1)
                if has(n + 2):
                    copy_x(n + 2)
                if has(n + 1):
                    weights(n + 1, 1 - p)
            every(body, a)

        @block.vector
        def _(v):
            rows = ln_rows(x, mean, rstd)

            def fetch(n):
                if not (type(n) is int and n == 0):
                    v.wait_ge(s["xtr"], n)
                rows(v, xn, n).then_inc(s["xf"], 1)

            def query(n, p):
                v.wait_ge(s["qm"], n + 1)
                for j in range(2):
                    o = v.tensor_scalar(qt[p][:, j, :], ps_x[:, j, :], bq[:, j:j + 1], 1.0 / 16.0, ALU.add, ALU.mult)
                o.then_inc(s["qc"], 1)

            def maximum(n, p):
                v.wait_ge(s["sc"], n + 1)
                v.tensor_reduce(nm[p][:, :], ps_s[:, 0:M], AX.X, ALU.max, negate=True).then_inc(s["mx"], 1)
            s["o"].open(v)
            fetch(0)
            fetch(1)
            query(0, 0)
            fetch(2)
            maximum(0, 0)
            query(1, 1)

            def body(n, p):
                if has(n + 1):
                    maximum(n + 1, 1 - p)
                if has(n + 3):
                    fetch(n + 3)
                if has(n + 2):
                    query(n + 2, p)
                s["ex"].wait(v, n + 1)
                v.reciprocal(rr[:, :], sm[p][:, :]).then_inc(s["r"], 1)
                v.wait_ge(s["r"], 2 * n + 1)
                s["av"].wait(v, n + 1)
                v.scalar_tensor_tensor(x[:, n, :], ps_o[:, 0:D], rr[:, :], x[:, n, :], ALU.mult, ALU.add).then_inc(s["o"].sem, 1)
                s["o"].wait(v, n + 1)
                v.bn_stats(st[:, n, :], x[:, n, :]).then_inc(s["r"], 1)
                v.wait_ge(s["r"], 2 * n + 2)
            every(body, v)


def quantised_ffn(prog, x, mean, rstd, w, bias, out_rows, identb):
    nc = prog["nc"]
    s = {k: fresh(prog, "f" + k) for k in ("am", "norm", "all", "v", "w", "y", "chain", "sum", "tick", "turned", "out")}
    for k in ("sub", "xt", "prod", "half", "x"):
        s[k] = Slots(prog, "f" + k, 3)
    G = 2
    STEPS = T // G
    with ExitStack() as cx:
        def sb(name, shape, dt=F32):
            return cx.enter_context(nc.sbuf_tensor(name, shape, dt))
        xn, nmr = sb("fxn", [P, T, D]), sb("fnmr", [P, T])
        am, al = sb("fam", [P, 5]), sb("fal", [P, 2])
        scale, inv, back = sb("fscale", [P, 2]), sb("finv", [P, 2]), sb("fback", [P, 1])
        wm, wq = sb("fwm", [P, 2, D]), sb("fwq", [P, 2, D], BF16)
        y, magic = ([sb(f"f{k}{r}", [P, G, D]) for r in range(2)] for k in ("y", "magic"))
        yq, half = ([sb(f"f{k}{r}", [P, G, D], BF16) for r in range(2)] for k in ("yq", "half"))
        xt = [sb(f"fxt{r}", [P, G, 2, P], BF16) for r in range(2)]
        turn = [cx.enter_context(nc.psum_tensor(f"fturn{r}", [P, G * 2, 256], BF16)) for r in range(2)]
        prod = [cx.enter_context(nc.psum_tensor(f"fprod{r}", [P, G, D], F32)) for r in range(2)]

        with nc.Block() as block:
            @block.scalar
            def _(a):
                a.wait_ge(s["v"], 1)
                for t in range(T):
                    a.activation(xn[:, t, :], x[:, t, :], ACT.Identity, bias=nmr[:, t:t + 1], scale=rstd[:, t:t + 1])\
                     .then_inc(s["norm"], 1)

            @block.vector
            def _(v):
                c = Counted(v, s["v"])
                c(v.scalar_tensor_tensor(nmr[:, :], mean[:, :], -1.0, rstd[:, :], ALU.mult, ALU.mult))
                v.tensor_reduce(am[:, 4:5], w[:, :, :], AX.XY, ALU.max, apply_absolute_value=True).then_inc(s["am"], 1)
                for g in range(4):
                    v.wait_ge(s["norm"], (g + 1) * T // 4)
                    v.tensor_reduce(am[:, g:g + 1], xn[:, g * T // 4:(g + 1) * T // 4, :], AX.XY, ALU.max,
                                    apply_absolute_value=True).then_inc(s["am"], 1)
                v.wait_ge(s["am"], 5)
                c(v.tensor_reduce(am[:, 0:1], am[:, 0:4], AX.X, ALU.max))
                c.wait()
                c(v.tensor_copy(am[:, 1:2], am[:, 4:5]))
                v.wait_ge(s["all"], 1)
                c(v.tensor_scalar(scale[:, :], al[:, :], 1e-12, None, ALU.max))
                c.wait()
                c(v.reciprocal(inv[:, :], scale[:, :]))
                c.wait()
                c(v.tensor_scalar(scale[:, :], inv[:, :], FP8_MAX, FP8_MAX, ALU.mult, ALU.min))
                c.wait()
                c(v.reciprocal(inv[:, :], scale[:, :]))
                c.wait()
                c(v.tensor_tensor(back[:, :], inv[:, 0:1], inv[:, 1:2], ALU.mult))
                c.wait()

            @block.gpsimd
            def _(g):
                g.wait_ge(s["v"], 3)
                g.partition_all_reduce(al[:, :], am[:, 0:2], P, bass.bass_isa.ReduceOp.max).then_inc(s["all"], 1)

        block = cx.enter_context(nc.Block())

        def every(body, eng):
            with eng.Fori(0, STEPS // 2 - 1) as i:
                for r in range(2):
                    body(2 * i + r, r)
            for k in range(STEPS - 2, STEPS):
                body(k, k % 2)

        def has(k):
            return not (type(k) is int and k >= STEPS)

        def to_sum(v, c, src, mg):
            c(v.tensor_scalar(src, src, FP8_MAX, -FP8_MAX, ALU.min, ALU.max))
            c.wait()
            c(v.tensor_scalar(mg.bitcast(I32), src.bitcast(I32), 0x7F800000, None, ALU.bitwise_and))
            c.wait()
            c(v.tensor_scalar(mg, mg, 2.0 ** -6, 1.5 * 2.0 ** 20, ALU.max, ALU.mult))
            c.wait()

        @block.scalar
        def _(a):
            def scaled(k, r):
                s["sub"].wait(a, k - 1)
                a.activation(y[r][:, :, :], xn[:, at(k * G, G), :], ACT.Copy, scale=scale[:, 0:1]).then_inc(s["y"], 1)
            s["xt"].open(a)
            scaled(0, 0)
            scaled(1, 1)

            def body(k, r):
                a.wait_ge(s["turned"], k + 1)
                s["prod"].wait(a, k - 1)
                a.copy(xt[r][:, :, :, :], turn[r][:, :, 0:P].rearrange("p (g k) n -> p g k n", k=2)).then_inc(s["xt"].sem, 1)
                if has(k + 2):
                    scaled(k + 2, r)
            every(body, a)

        @block.vector
        def _(v):
            c = Counted(v, s["w"])
            c(v.tensor_scalar(w[:, :, :], w[:, :, :], scale[:, 1:2], None, ALU.mult))
            c.wait()
            to_sum(v, c, w[:, :, :], wm[:, :, :])
            c(v.tensor_tensor(w[:, :, :], w[:, :, :], wm[:, :, :], ALU.add))
            c.wait()
            c(v.tensor_tensor(wq[:, :, :], w[:, :, :], wm[:, :, :], ALU.subtract))

            def rounded(k, r):
                v.wait_ge(s["y"], k + 1)
                s["sub"].wait(v, k - 1)
                c = Counted(v, s["chain"], k * 3)
                to_sum(v, c, y[r][:, :, :], magic[r][:, :, :])
                v.tensor_tensor(y[r][:, :, :], y[r][:, :, :], magic[r][:, :, :], ALU.add).then_inc(s["sum"], 1)
            s["half"].open(v)
            rounded(0, 0)
            rounded(1, 1)

            def body(k, r):
                if has(k + 2):
                    rounded(k + 2, r)
                s["prod"].wait(v, k + 1)
                s["x"].wait(v, k - 1)
                v.scalar_tensor_tensor(half[r][:, :, :], prod[r][:, :, :], back[:, :],
                                       bias[:, :].unsqueeze(1).to_broadcast([P, G, D]), ALU.mult, ALU.add).then_inc(s["half"].sem, 1)
            every(body, v)

        @block.gpsimd
        def _(g):
            s["sub"].open(g)
            s["x"].open(g)

            def quantised(k, r):
                g.wait_ge(s["sum"], k + 1)
                s["prod"].wait(g, k - 1)
                g.sem_inc(s["tick"], 1)
                g.tensor_tensor(yq[r][:, :, :], y[r][:, :, :], magic[r][:, :, :], ALU.subtract).then_inc(s["sub"].sem, 1)
            quantised(0, 0)
            quantised(1, 1)

            def body(k, r):
                if has(k + 2):
                    quantised(k + 2, r)
                s["half"].wait(g, k + 1)
                g.sem_inc(s["tick"], 1)
                g.tensor_tensor(x[:, at(k * G, G), :], x[:, at(k * G, G), :], half[r][:, :, :], ALU.add).then_inc(s["x"].sem, 1)
            every(body, g)

        @block.tensor
        def _(pe):
            s["prod"].open(pe)

            def turn_step(k, r):
                s["sub"].wait(pe, k + 1)
                s["xt"].wait(pe, k - 1)
                for g in range(G):
                    for i in range(2):
                        m = pe.transpose(turn[r][:, 2 * g + i, 0:P], yq[r][:, g, i * P:i * P + P], identb[:, :])
                m.then_inc(s["turned"], 1)
            turn_step(0, 0)
            pe.wait_ge(s["w"], 6)

            def body(k, r):
                if has(k + 1):
                    turn_step(k + 1, 1 - r)
                s["xt"].wait(pe, k + 1)
                s["half"].wait(pe, k - 1)
                for g in range(G):
                    for i in range(2):
                        m = pe.matmul(prod[r][:, g, :], xt[r][:, g, i, :], wq[:, i, :], start=(i == 0), stop=(i == 1))
                m.then_inc(s["prod"].sem, 1)
            every(body, pe)

        @block.sync
        def _(e):
            def body(k, r):
                s["x"].wait(e, k + 1)
                e.dma_start(out_rows[:, at(k * G, G), :], x[:, at(k * G, G), :]).then_inc(s["out"], 16)
            every(body, e)
            e.wait_ge(s["out"], 16 * STEPS)



def decoder(nc, a, out):
    with ExitStack() as ctx:
        prog = {"nc": nc, "used": []}

        def sb(cx, name, shape, dt=F32):
            return cx.enter_context(nc.sbuf_tensor(name, shape, dt))

        def layer_norm(extra=None):
            ln_finish(prog, st, mean, rstd, tmp, extra)
        x = sb(ctx, "x_res", [P, T, D])
        st, tmp = sb(ctx, "stats", [P, T, 6]), sb(ctx, "ln_tmp", [P, 2, T])
        mean, rstd = sb(ctx, "ln_mean", [P, T]), sb(ctx, "ln_rstd", [P, T])
        ident, identb = sb(ctx, "ident", [P, P]), sb(ctx, "identb", [P, P], BF16)
        ones = sb(ctx, "ones", [P, P])
        qn, v_nat = sb(ctx, "q_rows", [P, T, D]), sb(ctx, "v_rows", [P, T, D])
        ctx_t, valid = sb(ctx, "ctx_t", [CH, 2, MP]), sb(ctx, "valid", [P, TM])
        w_proj = sb(ctx, "w_proj", [P, 2, D])
        wq, bq = sb(ctx, "w_xq", [P, 2, D]), sb(ctx, "b_xq", [P, D])
        wkv, bkv = sb(ctx, "w_xkv", [CH, 2, 2 * D]), sb(ctx, "b_xkv", [P, 2 * D])
        x_rows, out_rows = (t.rearrange("(t p) d -> p t d", p=P) for t in (a["x"], out))

        with ExitStack() as cs:
            kt = sb(cs, "k_stack", [P, H, S], BF16)
            with ExitStack() as cx:
                kn = sb(cx, "k_rows", [P, T, D])
                w = sb(cx, "w_qkv", [P, 2, 3 * D])
                gain, shift = sb(cx, "gain", [P, 2, D]), sb(cx, "shift", [P, 2, D])
                s_x = [fresh(prog, f"x_in{q}") for q in range(4)]
                s_w, s0 = fresh(prog, "w_in"), fresh(prog, "start")
                cross_in = [
                    (ones[:, :], a["ones"]), (w_proj[:, :, :], rows2(a["w0_proj"])), (wq[:, :, :], rows2(a["w0_xq"])),
                    (bq[:, :], a["b0_xq"]), (wkv[:, :, :], rows2(a["w0_xkv"])), (bkv[:, :], a["b0_xkv"]),
                    (ctx_t[:, :, :], rows2(a["ctx_t"])), (valid[:, :], a["valid"])]
                s_cross = nc.alloc_semaphore("cross_in")
                with nc.Block() as block:
                    @block.sync
                    def _(e):
                        for q in range(4):
                            e.dma_start(x[:, 4 * q:4 * q + 4, :], x_rows[:, 4 * q:4 * q + 4, :]).then_inc(s_x[q], 16)
                        for dst, src in cross_in:
                            e.dma_start(dst, src).then_inc(s_cross, 16)

                    @block.scalar
                    def _(e):
                        for dst, src in ((ident[:, :], a["ident"]), (w[:, :, :], rows2(a["w0_qkv"])), (gain[:, :, :], a["gain"]),
                                         (shift[:, :, :], a["shift"])):
                            e.dma_start(dst, src).then_inc(s_w, 16)
                        e.wait_ge(s_w, 64)

                    @block.vector
                    def _(v):
                        for t in range(T):
                            if t % 4 == 0:
                                v.wait_ge(s_x[t // 4], 16)
                            v.bn_stats(st[:, t, :], x[:, t, :]).then_inc(s0, 1)
                        v.wait_ge(s_w, 64)
                        v.tensor_copy(identb[:, :], ident[:, :]).then_inc(s0, 1)
                        v.wait_ge(s0, T + 1)
                layer_norm()
                self_qkv(prog, x, mean, rstd, w, gain, shift, qn, kn, v_nat, ident)
                build_kt(prog, kn, T, kt, identb)
            end_load(prog, (s_cross, 16 * len(cross_in)))
            attention(prog, qn, v_nat, T, kt, ones, ident, identb)
        linear(prog, T, plain_rows(qn), w_proj, D, residual(x, st), 2, ident)
        recycle(prog)
        layer_norm(lambda v: v.tensor_scalar(bq[:, :], bq[:, :], 0.25, None, ALU.mult))
        wo, bo = sb(ctx, "w_xo", [P, 2, D]), sb(ctx, "b_xo", [P, D])
        gate, we, iota = sb(ctx, "w_gate", [P, 2, NE]), sb(ctx, "w_experts", [P, 2, NE * D]), sb(ctx, "iota8", [P, NE])
        experts_in = begin_load(prog, [
            (wo[:, :, :], rows2(a["w0_xo"])), (bo[:, :], a["b0_xo"]), (gate[:, :, :], rows2(a["w0_gate"])),
            (we[:, :, :], rows2(a["w0_experts"])), (iota[:, :], a["iota"])])
        with ExitStack() as cs:
            kt = sb(cs, "k_stack2", [P, H, MP], BF16)
            with ExitStack() as cx:
                kn = sb(cx, "k_rows2", [P, TM, D])
                cross_q(prog, x, mean, rstd, wq, bq, qn, ident)

                def keys_values(v, prod, n, r, c):
                    c(v.tensor_tensor(kn[:, n, :], prod[:, 0, 0:D], bkv[:, 0:D], ALU.add))
                    c(v.tensor_tensor(v_nat[:, n, :], prod[:, 0, D:2 * D], bkv[:, D:2 * D], ALU.add))
                    c.wait()
                    c(v.tensor_scalar(v_nat[:, n, :], v_nat[:, n, :], valid[:, at(n)], None, ALU.mult))
                linear(prog, TM, None, wkv, 2 * D, keys_values, 3, rows=CH, direct=lambda n: ctx_t[:, :, at(n * P, P)])
                build_kt(prog, kn, TM, kt, identb)
            end_load(prog, experts_in)
            attention(prog, qn, v_nat, TM, kt, valid, ident, identb)
        w1, mask = sb(ctx, "w1_qkv", [P, 2, 3 * D]), sb(ctx, "head_mask", [P, P])
        tap, tap_bias = sb(ctx, "taps", [P, 2, 3]), sb(ctx, "tap_bias", [P, 2])
        w1p, b1p = sb(ctx, "w1_proj", [P, 2, D]), sb(ctx, "b1_proj", [P, D])
        wk, wv = sb(ctx, "w1_xk", [CH, 2, D]), sb(ctx, "w1_xv", [CH, 2, D])
        bk, bv = sb(ctx, "b1_xk", [P, 2]), sb(ctx, "b1_xv", [P, D])
        w1q, b1q = sb(ctx, "w1_xq", [P, 2, D]), sb(ctx, "b1_xq", [P, 2])
        w1f, b1f = sb(ctx, "w1_ffn", [P, 2, D]), sb(ctx, "b1_ffn", [P, D])
        layer1_in = begin_load(prog, [
            (w1[:, :, :], rows2(a["w1_qkv"])), (mask[:, :], a["mask"]), (tap[:, :, :], rows2(a["taps"])),
            (tap_bias[:, :], a["tap_bias"]), (w1p[:, :, :], rows2(a["w1_proj"])), (b1p[:, :], a["b1_proj"]),
            (wk[:, :, :], rows2(a["w1_xk"])), (wv[:, :, :], rows2(a["w1_xv"])), (bk[:, :], a["b1_xk"]),
            (bv[:, :], a["b1_xv"]), (w1q[:, :, :], rows2(a["w1_xq"])), (b1q[:, :], a["b1_xq"]),
            (w1f[:, :, :], rows2(a["w1_ffn"])), (b1f[:, :], a["b1_ffn"])])
        add, early = biased_residual(prog, x, st, bo)
        linear(prog, T, plain_rows(qn), wo, D, add, 2, ident, early=early)
        layer_norm()
        experts(prog, x, st, mean, rstd, gate, we, iota, ident)
        recycle(prog)
        end_load(prog, layer1_in)
        layer_norm()
        with ExitStack() as cx:
            yt = sb(cx, "conv_out", [P, 2, S])
            with ExitStack() as cy:
                ps_kv = cy.enter_context(nc.psum_tensor("ps_kv", [P, 2, 512], F32))
                focused_qkv(prog, x, mean, rstd, w1, qn, ps_kv, ident)
                linear_attention(prog, qn, ps_kv, yt, tap, tap_bias, mask, ident)
            add, early = biased_residual(prog, x, st, b1p)
            linear(prog, T, None, w1p, D, add, 2, direct=lambda n: yt[:, :, at(n * P, P)], early=early)
        layer_norm()
        with ExitStack() as cx:
            keyt, vals = sb(cx, "key_t", [P, 2, MP]), sb(cx, "values1", [P, TM, D])
            cross_keys(prog, ctx_t, wk, bk, keyt)

            def value_rows(v, prod, n, r, c):
                c(v.tensor_tensor(vals[:, n, :], prod[:, 0, 0:D], bv[:, :], ALU.add))
            linear(prog, TM, None, wv, D, value_rows, 1, rows=CH, direct=lambda n: ctx_t[:, :, at(n * P, P)])
            cross_one_head(prog, x, st, mean, rstd, w1q, b1q, keyt, vals, ident)
        layer_norm()
        quantised_ffn(prog, x, mean, rstd, w1f, b1f, out_rows, identb)


def kernel(**inputs):
    import numpy as _np
    import concourse.bacc as _bacc
    from concourse.bass_utils import run_bass_kernel_spmd as _run

    i = {k: _np.asarray(v) for k, v in inputs.items()}
    wide = lambda v: _np.broadcast_to(v, (P, v.size))
    cols = lambda v: v.reshape(2, P).T
    kv = i["L0_xattn_Wkv"].reshape(H, 2, HD, C).transpose(1, 0, 2, 3).reshape(2 * D, C)
    bkv = i["L0_xattn_bkv"].reshape(H, 2, HD).transpose(1, 0, 2).reshape(2 * D)
    ctx = i["ctx_768"][0]
    ctx = _np.concatenate([ctx, _np.broadcast_to(ctx[-1:], (MP - M, C))])
    arrays = {
        "x": i["x"][0],
        "ctx_t": ctx.T,
        "ident": _np.eye(P, dtype=_np.float32),
        "ones": _np.ones((P, P), _np.float32),
        "valid": (_np.arange(MP).reshape(TM, P).T < M).astype(_np.float32),
        "mask": _np.kron(_np.eye(P // HD), _np.ones((HD, HD))).astype(_np.float32),
        "iota": wide(_np.arange(NE, dtype=_np.float32)),
        "w0_qkv": i["L0_attn_w_qkv"],
        "gain": _np.stack([wide(_np.tile(i[f"L0_attn_{k}_gamma"], H)) for k in "qk"], 1),
        "shift": _np.stack([wide(_np.tile(i[f"L0_attn_{k}_beta"], H)) for k in "qk"], 1),
        "w0_proj": i["L0_attn_w_proj"],
        "w0_xq": i["L0_xattn_Wq"].T, "b0_xq": wide(i["L0_xattn_bq"]),
        "w0_xkv": kv.T, "b0_xkv": wide(bkv),
        "w0_xo": i["L0_xattn_Wo"].T, "b0_xo": wide(i["L0_xattn_bo"]),
        "w0_gate": i["L0_ffn_gate_w"].T,
        "w0_experts": i["L0_ffn_weight"].transpose(1, 0, 2).reshape(D, NE * D),
        "w1_qkv": i["L1_attn_w_qkv"].T,
        "w1_proj": i["L1_attn_w_proj"].T, "b1_proj": wide(i["L1_attn_b_proj"]),
        "taps": i["L1_attn_w_dwc"], "tap_bias": cols(i["L1_attn_b_dwc"]),
        "w1_xq": i["L1_xattn_Wq"], "b1_xq": cols(i["L1_xattn_bq"]),
        "w1_xk": i["L1_xattn_Wk"], "b1_xk": cols(i["L1_xattn_bk"]),
        "w1_xv": i["L1_xattn_Wv"], "b1_xv": wide(i["L1_xattn_bv"]),
        "w1_ffn": i["L1_ffn_weight"].T, "b1_ffn": wide(i["L1_ffn_bias"]),
    }
    arrays = {"in_" + k: _np.ascontiguousarray(v) for k, v in arrays.items()}
    nc = _bacc.Bacc("TRN2", target_bir_lowering=False, num_devices=1)
    args = {k[3:]: nc.dram_tensor(k, v.shape, F32, kind="ExternalInput").ap() for k, v in arrays.items()}
    out = nc.dram_tensor("out", (S, D), F32, kind="ExternalOutput").ap()
    decoder(nc, args, out)
    r = _run(nc, [arrays], core_ids=[0])
    return r.results[0]["out"].reshape(1, S, D)
```
